# Optimizing a Trainium2 kernel written in Bass

```python
import numpy as np
import jax
import jax.numpy as jnp

def _softmax(x, axis=-1):
    return jax.nn.softmax(x, axis=axis)

def _gelu(x):
    return jax.nn.gelu(x, approximate=True)

def _silu(x):
    return jax.nn.silu(x)

def _sigmoid(x):
    return jax.nn.sigmoid(x)

def _layernorm(x, axis=-1, eps=1e-05):
    m = jnp.mean(x, axis=axis, keepdims=True)
    v = jnp.var(x, axis=axis, keepdims=True)
    return (x - m) / jnp.sqrt(v + eps)

def _scatter_add(tgt, idx, src, axis=0):
    return tgt.at[idx].add(src)

def _segment_sum(src, seg, n):
    return jax.ops.segment_sum(src, seg, n)
kernel_name = 'mk_adj_seq_d4_adj_r2_c84df9'

def setup_inputs(seed: int=0):
    np.random.seed(seed)
    _w = jnp.asarray

    def _rec_inputs():
        import jax
        import jax.numpy as jnp
        _gk = jax.random.key(seed)
        x = 7.22e-05 + 1 * jax.random.normal(jax.random.fold_in(_gk, 1), (8, 1024, 256), jnp.float32)
        _a = jax.random.bernoulli(jax.random.fold_in(_gk, 2), 0.0078125, (8, 1024, 1024))
        _a = jnp.logical_or(_a, jnp.eye(1024, dtype=bool))
        _af = _a.astype(jnp.float32)
        adj = _af
        return (x, adj)
    x, adj = _rec_inputs()

    def _L0_gnn_setup():
        import jax, jax.numpy as jnp
        import numpy as np
        BS, N, H = (8, 1024, 256)
        NEG_INF = -1000000000.0
        LEAKY_SLOPE = 0.01
        key = jax.random.key(seed)
        ks = jax.random.split(key, 8)
        feats = jax.random.normal(ks[0], (BS, N, H), dtype=jnp.float32)
        adj = jax.random.randint(ks[1], (BS, N, N), 0, 2).astype(jnp.float32)
        adj = jnp.maximum(adj, jnp.eye(N, dtype=jnp.float32)[None])
        s = 1.0 / np.sqrt(H)
        return {'feats': feats, 'adj_mat': adj, 'fc_w': jax.random.normal(ks[2], (H, H), dtype=jnp.float32) * s, 'fc_b': jax.random.normal(ks[3], (H,), dtype=jnp.float32) * s, 'q_w': jax.random.normal(ks[4], (1, H), dtype=jnp.float32) * s, 'q_b': jax.random.normal(ks[5], (1,), dtype=jnp.float32) * s, 'k_w': jax.random.normal(ks[6], (1, H), dtype=jnp.float32) * s, 'k_b': jax.random.normal(ks[7], (1,), dtype=jnp.float32) * s}
    _L0_gnn_all = _L0_gnn_setup()
    _L0_gnn_in = {k: v for k, v in _L0_gnn_all.items() if k in ('fc_w', 'fc_b', 'q_w', 'q_b', 'k_w', 'k_b')}
    del _L0_gnn_all

    def _L1_gnn_setup():
        import jax, jax.numpy as jnp
        import numpy as np
        import math
        EMBED = 256
        DFF = 256
        B, N = (8, 1024)
        key = jax.random.key(seed)
        ks = jax.random.split(key, 8)
        node_fts = jax.random.normal(ks[0], (B, N, EMBED), dtype=jnp.float32)
        rel_edges = jax.random.randint(ks[1], (B, N, N), 0, 2).astype(jnp.float32)
        s = 1.0 / math.sqrt(EMBED)
        Wq = jax.random.normal(ks[2], (EMBED, DFF), dtype=jnp.float32) * s
        bq = jnp.zeros((DFF,), dtype=jnp.float32)
        Wk = jax.random.normal(ks[3], (EMBED, DFF), dtype=jnp.float32) * s
        bk = jnp.zeros((DFF,), dtype=jnp.float32)
        Wc = jax.random.normal(ks[4], (EMBED, EMBED), dtype=jnp.float32) * s
        gamma = jnp.ones((EMBED,), dtype=jnp.float32)
        beta = jnp.zeros((EMBED,), dtype=jnp.float32)
        return {'node_fts': node_fts, 'rel_edges': rel_edges, 'Wq': Wq, 'bq': bq, 'Wk': Wk, 'bk': bk, 'Wc': Wc, 'gamma': gamma, 'beta': beta}
    _L1_gnn_all = _L1_gnn_setup()
    _L1_gnn_in = {k: v for k, v in _L1_gnn_all.items() if k in ('Wq', 'bq', 'Wk', 'bk', 'Wc', 'gamma', 'beta')}
    del _L1_gnn_all

    def _L2_gnn_setup():
        import jax, jax.numpy as jnp
        import numpy as np
        B, N, D, H = (8, 512, 256, 8)
        DK = D // H
        LN_EPS = 1e-05
        ADJ_MIN = 1e-08

        def _layer_norm(x, gamma, beta):
            mu = jnp.mean(x, axis=-1, keepdims=True)
            var = jnp.mean(jnp.square(x - mu), axis=-1, keepdims=True)
            return (x - mu) * jax.lax.rsqrt(var + LN_EPS) * gamma + beta
        key = jax.random.key(seed)
        ks = jax.random.split(key, 12)
        x = jax.random.normal(ks[0], (B, N, D), dtype=jnp.float32)
        adj = jax.random.uniform(ks[1], (B, N, N), dtype=jnp.float32)
        adj = adj / jnp.sum(adj, axis=-1, keepdims=True)
        s = 1.0 / np.sqrt(D)
        Wq = jax.random.normal(ks[2], (D, D), dtype=jnp.float32) * s
        bq = jnp.zeros((D,), dtype=jnp.float32)
        Wk = jax.random.normal(ks[3], (D, D), dtype=jnp.float32) * s
        bk = jnp.zeros((D,), dtype=jnp.float32)
        Wv = jax.random.normal(ks[4], (D, D), dtype=jnp.float32) * s
        bv = jnp.zeros((D,), dtype=jnp.float32)
        Wo = jax.random.normal(ks[5], (D, D), dtype=jnp.float32) * s
        bo = jnp.zeros((D,), dtype=jnp.float32)
        gamma = jnp.ones((D,), dtype=jnp.float32)
        beta = jnp.zeros((D,), dtype=jnp.float32)
        return {'x': x, 'adj': adj, 'Wq': Wq, 'bq': bq, 'Wk': Wk, 'bk': bk, 'Wv': Wv, 'bv': bv, 'Wo': Wo, 'bo': bo, 'gamma': gamma, 'beta': beta}
    _L2_gnn_all = _L2_gnn_setup()
    _L2_gnn_in = {k: v for k, v in _L2_gnn_all.items() if k in ('Wq', 'bq', 'Wk', 'bk', 'Wv', 'bv', 'Wo', 'bo', 'gamma', 'beta')}
    del _L2_gnn_all

    def _L3_gnn_setup():
        import jax, jax.numpy as jnp
        import numpy as np
        import math
        D_MODEL = 256
        NHEAD = 8
        HEAD_DIM = D_MODEL // NHEAD
        LN_EPS = 1e-05

        def _layernorm(x, g, b):
            mu = jnp.mean(x, axis=-1, keepdims=True)
            var = jnp.mean(jnp.square(x - mu), axis=-1, keepdims=True)
            return (x - mu) * jax.lax.rsqrt(var + LN_EPS) * g + b
        key = jax.random.key(seed)
        ks = jax.random.split(key, 12)
        B, N, D = (4, 1024, D_MODEL)
        s = 1.0 / math.sqrt(D)
        inp = {'hidden': jax.random.normal(ks[0], (B, N, D), jnp.float32), 'adjacency': (jax.random.uniform(ks[1], (B, N, N)) > 0.98).astype(jnp.float32), 'Wq': jax.random.normal(ks[2], (D, D), jnp.float32) * s, 'bq': jnp.zeros((D,), jnp.float32), 'Wk': jax.random.normal(ks[3], (D, D), jnp.float32) * s, 'bk': jnp.zeros((D,), jnp.float32), 'Wv': jax.random.normal(ks[4], (D, D), jnp.float32) * s, 'bv': jnp.zeros((D,), jnp.float32), 'Wo': jax.random.normal(ks[5], (D, D), jnp.float32) * s, 'bo': jnp.zeros((D,), jnp.float32), 'g1': jnp.ones((D,), jnp.float32), 'b1': jnp.zeros((D,), jnp.float32), 'g2': jnp.ones((D,), jnp.float32), 'b2': jnp.zeros((D,), jnp.float32), 'Wf1': jax.random.normal(ks[6], (D, 4 * D), jnp.float32) * s, 'bf1': jnp.zeros((4 * D,), jnp.float32), 'Wf2': jax.random.normal(ks[7], (4 * D, D), jnp.float32) * (1.0 / math.sqrt(4 * D)), 'bf2': jnp.zeros((D,), jnp.float32)}
        return inp
    _L3_gnn_all = _L3_gnn_setup()
    _L3_gnn_in = {k: v for k, v in _L3_gnn_all.items() if k in ('Wq', 'bq', 'Wk', 'bk', 'Wv', 'bv', 'Wo', 'bo', 'g1', 'b1', 'g2', 'b2', 'Wf1', 'bf1', 'Wf2', 'bf2')}
    del _L3_gnn_all
    return {'x': x, 'adj': adj, 'L0_gnn_fc_w': _L0_gnn_in['fc_w'], 'L0_gnn_fc_b': _L0_gnn_in['fc_b'], 'L0_gnn_q_w': _L0_gnn_in['q_w'], 'L0_gnn_q_b': _L0_gnn_in['q_b'], 'L0_gnn_k_w': _L0_gnn_in['k_w'], 'L0_gnn_k_b': _L0_gnn_in['k_b'], 'L1_gnn_Wq': _L1_gnn_in['Wq'], 'L1_gnn_bq': _L1_gnn_in['bq'], 'L1_gnn_Wk': _L1_gnn_in['Wk'], 'L1_gnn_bk': _L1_gnn_in['bk'], 'L1_gnn_Wc': _L1_gnn_in['Wc'], 'L1_gnn_gamma': _L1_gnn_in['gamma'], 'L1_gnn_beta': _L1_gnn_in['beta'], 'L2_gnn_Wq': _L2_gnn_in['Wq'], 'L2_gnn_bq': _L2_gnn_in['bq'], 'L2_gnn_Wk': _L2_gnn_in['Wk'], 'L2_gnn_bk': _L2_gnn_in['bk'], 'L2_gnn_Wv': _L2_gnn_in['Wv'], 'L2_gnn_bv': _L2_gnn_in['bv'], 'L2_gnn_Wo': _L2_gnn_in['Wo'], 'L2_gnn_bo': _L2_gnn_in['bo'], 'L2_gnn_gamma': _L2_gnn_in['gamma'], 'L2_gnn_beta': _L2_gnn_in['beta'], 'L3_gnn_Wq': _L3_gnn_in['Wq'], 'L3_gnn_bq': _L3_gnn_in['bq'], 'L3_gnn_Wk': _L3_gnn_in['Wk'], 'L3_gnn_bk': _L3_gnn_in['bk'], 'L3_gnn_Wv': _L3_gnn_in['Wv'], 'L3_gnn_bv': _L3_gnn_in['bv'], 'L3_gnn_Wo': _L3_gnn_in['Wo'], 'L3_gnn_bo': _L3_gnn_in['bo'], 'L3_gnn_g1': _L3_gnn_in['g1'], 'L3_gnn_b1': _L3_gnn_in['b1'], 'L3_gnn_g2': _L3_gnn_in['g2'], 'L3_gnn_b2': _L3_gnn_in['b2'], 'L3_gnn_Wf1': _L3_gnn_in['Wf1'], 'L3_gnn_bf1': _L3_gnn_in['bf1'], 'L3_gnn_Wf2': _L3_gnn_in['Wf2'], 'L3_gnn_bf2': _L3_gnn_in['bf2']}

def reference(x, adj, L0_gnn_fc_w, L0_gnn_fc_b, L0_gnn_q_w, L0_gnn_q_b, L0_gnn_k_w, L0_gnn_k_b, L1_gnn_Wq, L1_gnn_bq, L1_gnn_Wk, L1_gnn_bk, L1_gnn_Wc, L1_gnn_gamma, L1_gnn_beta, L2_gnn_Wq, L2_gnn_bq, L2_gnn_Wk, L2_gnn_bk, L2_gnn_Wv, L2_gnn_bv, L2_gnn_Wo, L2_gnn_bo, L2_gnn_gamma, L2_gnn_beta, L3_gnn_Wq, L3_gnn_bq, L3_gnn_Wk, L3_gnn_bk, L3_gnn_Wv, L3_gnn_bv, L3_gnn_Wo, L3_gnn_bo, L3_gnn_g1, L3_gnn_b1, L3_gnn_g2, L3_gnn_b2, L3_gnn_Wf1, L3_gnn_bf1, L3_gnn_Wf2, L3_gnn_bf2):
    import jax
    import jax.numpy as jnp

    def _L0_gnn_ref(feats, adj_mat, fc_w, fc_b, q_w, q_b, k_w, k_b):
        import jax, jax.numpy as jnp
        import numpy as np
        BS, N, H = (8, 1024, 256)
        NEG_INF = -1000000000.0
        LEAKY_SLOPE = 0.01
        feat_proj = jnp.einsum('bnh,oh->bno', feats, fc_w) + fc_b
        q = jnp.einsum('bnh,oh->bno', feat_proj, q_w) + q_b
        k = jnp.einsum('bnh,oh->bno', feat_proj, k_w) + k_b
        logits = q + jnp.swapaxes(k, 2, 1)
        masked = logits + (1.0 - adj_mat) * NEG_INF
        masked = jnp.where(masked >= 0, masked, LEAKY_SLOPE * masked)
        atten = jax.nn.softmax(masked, axis=-1)
        out = jnp.einsum('bnm,bmh->bnh', atten, feat_proj)
        return out + feats

    def _L1_gnn_ref(node_fts, rel_edges, Wq, bq, Wk, bk, Wc, gamma, beta):
        import jax, jax.numpy as jnp
        import numpy as np
        import math
        EMBED = 256
        DFF = 256
        B, N = (8, 1024)
        denom = math.sqrt(DFF)
        q = node_fts @ Wq + bq
        k = node_fts @ Wk + bk
        scores = jnp.einsum('bod,bid->boi', q, k) / denom
        mask = rel_edges == 0
        scores = jnp.where(mask, -1e+18, scores)
        attn = jax.nn.softmax(scores, axis=2)
        attn = jnp.where(mask, 0.0, attn)
        ctx = jnp.einsum('boi,bie->boe', attn, node_fts) @ Wc
        x = node_fts + ctx
        mu = jnp.mean(x, axis=-1, keepdims=True)
        var = jnp.mean(jnp.square(x - mu), axis=-1, keepdims=True)
        out = (x - mu) * jax.lax.rsqrt(var + 1e-05) * gamma + beta
        return out

    def _L2_gnn_ref(x, adj, Wq, bq, Wk, bk, Wv, bv, Wo, bo, gamma, beta):
        import jax, jax.numpy as jnp
        import numpy as np
        B, N, D, H = (8, 512, 256, 8)
        DK = D // H
        LN_EPS = 1e-05
        ADJ_MIN = 1e-08

        def _layer_norm(x, gamma, beta):
            mu = jnp.mean(x, axis=-1, keepdims=True)
            var = jnp.mean(jnp.square(x - mu), axis=-1, keepdims=True)
            return (x - mu) * jax.lax.rsqrt(var + LN_EPS) * gamma + beta
        b, n, d = x.shape
        q = (x @ Wq.T + bq).reshape(b, n, H, DK).transpose(0, 2, 1, 3)
        k = (x @ Wk.T + bk).reshape(b, n, H, DK).transpose(0, 2, 1, 3)
        v = (x @ Wv.T + bv).reshape(b, n, H, DK).transpose(0, 2, 1, 3)
        logits = jnp.einsum('bhqd,bhkd->bhqk', q, k) / np.sqrt(DK)
        logits = logits + jnp.log(jnp.clip(adj, ADJ_MIN, None))[:, None, :, :]
        attn = jax.nn.softmax(logits, axis=-1)
        out = jnp.einsum('bhqk,bhkd->bhqd', attn, v)
        out = out.transpose(0, 2, 1, 3).reshape(b, n, d)
        out = out @ Wo.T + bo
        return _layer_norm(x + out, gamma, beta)

    def _L3_gnn_ref(hidden, adjacency, Wq, bq, Wk, bk, Wv, bv, Wo, bo, g1, b1, g2, b2, Wf1, bf1, Wf2, bf2):
        import jax, jax.numpy as jnp
        import numpy as np
        import math
        D_MODEL = 256
        NHEAD = 8
        HEAD_DIM = D_MODEL // NHEAD
        LN_EPS = 1e-05

        def _layernorm(x, g, b):
            mu = jnp.mean(x, axis=-1, keepdims=True)
            var = jnp.mean(jnp.square(x - mu), axis=-1, keepdims=True)
            return (x - mu) * jax.lax.rsqrt(var + LN_EPS) * g + b
        B, N, D = hidden.shape
        H, Hd = (NHEAD, HEAD_DIM)
        normed = _layernorm(hidden, g1, b1)
        q = (normed @ Wq + bq).reshape(B, N, H, Hd).transpose(0, 2, 1, 3)
        k = (normed @ Wk + bk).reshape(B, N, H, Hd).transpose(0, 2, 1, 3)
        v = (normed @ Wv + bv).reshape(B, N, H, Hd).transpose(0, 2, 1, 3)
        logits = jnp.einsum('bhnd,bhmd->bhnm', q, k) / math.sqrt(Hd)
        adj = adjacency[:, None, :, :]
        logits = logits + (2.0 * adj - 1.0)
        weights = jax.nn.softmax(logits, axis=-1)
        weights = weights * (0.25 + 0.75 * adj)
        weights = weights / jnp.maximum(weights.sum(axis=-1, keepdims=True), 1e-06)
        attended = jnp.einsum('bhnm,bhmd->bhnd', weights, v)
        attended = attended.transpose(0, 2, 1, 3).reshape(B, N, D)
        hidden = hidden + attended @ Wo + bo
        h2 = _layernorm(hidden, g2, b2)
        ff = jax.nn.gelu(h2 @ Wf1 + bf1, approximate=False) @ Wf2 + bf2
        return hidden + ff
    x = _L0_gnn_ref(x, adj, L0_gnn_fc_w, L0_gnn_fc_b, L0_gnn_q_w, L0_gnn_q_b, L0_gnn_k_w, L0_gnn_k_b)
    x = _L1_gnn_ref(x, adj, L1_gnn_Wq, L1_gnn_bq, L1_gnn_Wk, L1_gnn_bk, L1_gnn_Wc, L1_gnn_gamma, L1_gnn_beta)
    x = _L2_gnn_ref(x, adj, L2_gnn_Wq, L2_gnn_bq, L2_gnn_Wk, L2_gnn_bk, L2_gnn_Wv, L2_gnn_bv, L2_gnn_Wo, L2_gnn_bo, L2_gnn_gamma, L2_gnn_beta)
    x = _L3_gnn_ref(x, adj, L3_gnn_Wq, L3_gnn_bq, L3_gnn_Wk, L3_gnn_bk, L3_gnn_Wv, L3_gnn_bv, L3_gnn_Wo, L3_gnn_bo, L3_gnn_g1, L3_gnn_b1, L3_gnn_g2, L3_gnn_b2, L3_gnn_Wf1, L3_gnn_bf1, L3_gnn_Wf2, L3_gnn_bf2)
    return x

_drawn_inputs = setup_inputs


def setup_inputs(seed=0):
    import zlib

    import numpy as np

    out = dict(_drawn_inputs(seed))
    spreads = {'L1_gnn_bq': (0.0, 0.1),
     'L1_gnn_bk': (0.0, 0.8),
     'L1_gnn_gamma': (1.0, 0.2),
     'L1_gnn_beta': (0.0, 0.1),
     'L2_gnn_bq': (0.0, 0.1),
     'L2_gnn_bk': (0.0, 0.8),
     'L2_gnn_bv': (0.0, 0.1),
     'L2_gnn_bo': (0.0, 0.1),
     'L2_gnn_gamma': (1.0, 0.2),
     'L2_gnn_beta': (0.0, 0.1),
     'L3_gnn_bq': (0.0, 0.676),
     'L3_gnn_bk': (0.0, 0.8),
     'L3_gnn_bv': (0.0, 0.1),
     'L3_gnn_bo': (0.0, 0.1),
     'L3_gnn_g1': (1.0, 0.2),
     'L3_gnn_b1': (0.0, 0.1),
     'L3_gnn_g2': (1.0, 0.2),
     'L3_gnn_b2': (0.0, 0.1),
     'L3_gnn_bf1': (0.0, 0.1),
     'L3_gnn_bf2': (0.0, 0.1)}
    factors = {}
    for name, (base, spread) in spreads.items():
        noise = np.random.default_rng([zlib.crc32(name.encode()), seed]).standard_normal(out[name].shape)
        drawn = base * np.exp(spread * noise) if base else spread * noise
        out[name] = jnp.asarray(drawn.astype(out[name].dtype))
    for name, factor in factors.items():
        out[name] = (out[name] * factor).astype(out[name].dtype)
    return out
```

```python
from contextlib import ExitStack

import concourse.bass as bass
from concourse import mybir

F32 = mybir.dt.float32
BF16 = mybir.dt.bfloat16
ACT = mybir.ActivationFunctionType
ALU = mybir.AluOpType
AX = mybir.AxisListType

P = 128
N = 1024
D = 256
T = N // P
C = D // P
HALF = 512
H = 8
DK = D // H
FF = 4 * D
F = FF // P
AUG = 3 * DK + 1
LAG = 3
RING = 4
POOL_TILES = (1, 3, 5, 7)
DVE_TILES = tuple(t for t in range(T) if t not in POOL_TILES)
EPS = 1e-5
LOWEST = -3.0e38

LINEAR = [
    ("x_t", 4, "AD"), ("proj0", 4, "D"), ("key0", 2, "A"), ("query0", 1, "D"),
    ("y1_t", 4, "AD"), ("q1", 4, "AD"), ("k1", 4, "AD"), ("v1", 4, "AD"),
    ("y2_t", 4, "AD"), ("q2", 4, "D"), ("k2", 4, "D"), ("v2", 4, "D"), ("o2", 4, "D"),
    ("y3_t", 4, "AD"), ("q3", 4, "D"), ("k3", 4, "D"), ("v3", 4, "D"), ("o3", 4, "D"),
    ("h_t", 4, "AD"), ("ff1", 16, "A"), ("ff2", 4, "D"),
]
UNITS = [(name, i, owners[i % len(owners)]) for name, n, owners in LINEAR for i in range(n)]
PLACE = {(name, i): at for at, (name, i, _) in enumerate(UNITS)}
N_LIN = len(UNITS)
N_ACT = sum(o == "A" for _, _, o in UNITS)
N_DVE = N_LIN - N_ACT
LIN_BANKS = 4
CONSTS = 6
DVE_STEPS = 141


def emptied_before(name, i):
    at = PLACE[(name, i)]
    a = sum(o == "A" for _, _, o in UNITS[:at])
    return a, at - a


def build(nc, a, out):
    B = out.shape[0]
    with ExitStack() as ctx:
        def sb(name, shape, dt=F32):
            return ctx.enter_context(nc.sbuf_tensor(name, shape, dt))

        def sem(name):
            return ctx.enter_context(nc.semaphore(name))

        ps = ctx.enter_context(nc.psum_tensor("ps", [P, 8, HALF], F32))
        flat = ps[:, :, :].rearrange("p b n -> p (b n)")

        x_in = sb("x_in", [P, T, D])
        y = sb("y", [P, T, D])
        y_t = sb("y_t", [P, C, N])
        o_t = y_t
        values = sb("values", [P, T, D])
        x_hat = values
        mask = sb("mask", [P, T, N])
        sums_t = sb("sums_t", [P, C, N])
        region_q = sb("region_q", [P, 4096])
        region_k = sb("region_k", [P, 4096])
        region_p = sb("region_p", [P, 4096])
        q_aug = region_q[:, :].bitcast(BF16).rearrange("p (h n) -> p h n", h=H)
        k_aug = region_k[:, :].bitcast(BF16).rearrange("p (h n) -> p h n", h=H)
        probs = region_p[:, :].rearrange("p (r n) -> p r n", r=RING)
        parts = region_p[:, :].bitcast(BF16).rearrange("p (s g n) -> p s g n", s=4, g=C)
        mask_exp = region_q[:, :].rearrange("p (r n) -> p r n", r=4)
        q_t = region_q[:, 0:C * N].rearrange("p (c n) -> p c n", c=C)
        k_t = region_q[:, C * N:2 * C * N].rearrange("p (c n) -> p c n", c=C)
        scores = region_k[:, 0:3 * N].rearrange("p (r n) -> p r n", r=3)
        slack = region_q[:, :].rearrange("p (r n) -> p r n", r=4)
        key_row = region_k[:, 3 * N:4 * N]
        probs_t = region_p[:, 0:2 * N].rearrange("p (r t q) -> p r t q", r=2, t=T)
        hidden = [region_q[:, :].rearrange("p (f n) -> p f n", f=4),
                  region_k[:, :].rearrange("p (f n) -> p f n", f=4)]
        fcw = region_q[:, 0:C * D].rearrange("p (c n) -> p c n", c=C)
        bias_rep = region_q[:, 1024:1024 + C * P].rearrange("p (c n) -> p c n", c=C)

        v_head = [sb(f"v_head{i}", [P, T, 2 * DK]) for i in range(2)]
        o_raw = [sb(f"o_raw{i}", [P, HALF]) for i in range(2)]
        row_max = [sb(f"row_max{i}", [P, T]) for i in range(2)]
        row_max_bf = [sb(f"row_max_bf{i}", [P, T], BF16) for i in range(2)]
        max_rows = [sb(f"max_rows{i}", [T, P], BF16) for i in range(2)]

        w = {n: sb(f"w_{n}", [P, C, D]) for n in
             ("fc", "q1", "k1", "c1", "q2", "k2", "v2", "o2", "q3", "k3", "v3", "o3")}
        wf1 = sb("wf1", [P, C, FF])
        wf2 = sb("wf2", [P, F, D])
        rows = {n: sb(f"r_{n}", [P, D]) for n in
                ("fc_b", "gamma1", "beta1", "bv2", "bo2", "gamma2", "beta2", "bv3", "bo3", "bf2")}
        cols = {n: sb(f"c_{n}", [P, C]) for n in
                ("q_w", "k_w", "fc_b", "bq1", "bk1", "bq2", "bk2", "bq3", "bk3", "g1", "b1", "g2", "b2")}
        bf1 = sb("bf1", [P, F])
        key_w = sb("key_w", [P, C, P])
        query_w = sb("query_w", [P, C])
        qk_b = sb("qk_b", [P, 2])
        qk_const = sb("qk_const", [P, 2])
        ident = sb("ident", [P, P])
        ident_bf = sb("ident_bf", [P, P], BF16)
        ones = sb("ones", [P, P])
        minus_one = sb("minus_one", [H, N], BF16)
        minus_ones = sb("minus_ones", [P, 1])

        q_n = sb("q_n", [P, T])
        slack_q = sb("slack_q", [P, T])
        top = sb("top", [P, T])
        top2 = sb("top2", [P, T])
        neg_top = sb("neg_top", [P, T])
        denom = sb("denom", [P, T])
        rden = sb("rden", [P, T])
        rden2 = sb("rden2", [P, T])
        some = sb("some", [P, T])
        stats = sb("stats", [P, T, 6])
        mean_var = sb("mean_var", [P, T, 2])
        var_eps = sb("var_eps", [P, T])
        minus_half = sb("minus_half", [P, 1])
        rstd = sb("rstd", [P, T])

        weights_in = sem("weights_in")
        const_made = sem("const_made")
        ident_made = sem("ident_made")
        quarter_done = sem("quarter_done")
        setup_mm = sem("setup_mm")
        setup_dve = sem("setup_dve")
        x_loaded = sem("x_loaded")
        mask_loaded = [sem(f"mask_loaded{t}") for t in range(T)]
        lin_done = sem("lin_done")
        act_emptied = sem("act_emptied")
        dve_emptied = sem("dve_emptied")
        dve_step = sem("dve_step")
        pen_ready = sem("pen_ready")
        mask_used = sem("mask_used")
        s_done = sem("s_done")
        s_ready = sem("s_ready")
        slack_done = sem("slack_done")
        leaky_done = sem("leaky_done")
        p_ready = sem("p_ready")
        t_done = sem("t_done")
        t_act = sem("t_act")
        t_dve = sem("t_dve")
        av_done = sem("av_done")
        y_ready = sem("y_ready")
        hi_ready = sem("hi_ready")
        aug_loaded = sem("aug_loaded")
        g_ready = sem("g_ready")
        e_ready = sem("e_ready")
        g3_ready = sem("g3_ready")
        nat_done = sem("nat_done")
        max_done = sem("max_done")
        max_cast = sem("max_cast")
        max_row_in = [sem(f"max_row_in{i}") for i in range(2)]
        st_done = sem("st_done")
        exp_done = sem("exp_done")
        masked_dve = sem("masked_dve")
        masked_pool = sem("masked_pool")
        v_ready = sem("v_ready")
        pv_done = sem("pv_done")
        o_out = sem("o_out")
        o_moved = [sem(f"o_moved{i}") for i in range(2)]
        o_normal = sem("o_normal")
        residual = sem("residual")
        passed = sem("passed")
        stats_ready = sem("stats_ready")
        var_ready = sem("var_ready")
        rstd_ready = sem("rstd_ready")
        normal = sem("normal")
        stored = sem("stored")

        def att(b, layer, h, per, c):
            return b * (2 * H * per) + layer * H * per + c + h * per

        def max_count(b, layer, order):
            return b * (2 * H * (T + 1)) + layer * H * (T + 1) + order

        def max_order(s, k):
            return s * (T + 1) + k - 1

        def wait_lin(eng, b, name, i):
            eng.wait_ge(lin_done, b * N_LIN + PLACE[(name, i)] + 1)

        def wait_emptied(eng, b, name, i):
            na, nd = emptied_before(name, i)
            if UNITS[PLACE[(name, i)]][2] == "A":
                eng.wait_ge(act_emptied, b * N_ACT + na + 1)
            else:
                eng.wait_ge(dve_emptied, b * N_DVE + nd + 1)

        def wait_all_emptied(eng, b, name, n):
            na, nd = emptied_before(name, n - 1)
            last_a = UNITS[PLACE[(name, n - 1)]][2] == "A"
            eng.wait_ge(act_emptied, b * N_ACT + na + last_a)
            eng.wait_ge(dve_emptied, b * N_DVE + nd + (not last_a))

        weight_dmas = []

        block = ctx.enter_context(nc.Block())

        @block.sync
        def _(sp):
            def load(dst, src):
                sp.dma_start(dst, src).then_inc(weights_in, 16)
                weight_dmas.append(1)

            def tiled(name):
                return a[name].rearrange("(c p) n -> p c n", p=P)

            load(fcw, tiled("L0_gnn_fc_w"))
            for key, name in (("fc", "L0_fc_wT"), ("q1", "L1_gnn_Wq"), ("k1", "L1_gnn_Wk"), ("c1", "L1_gnn_Wc"),
                              ("q2", "L2_WqT"), ("k2", "L2_WkT"), ("v2", "L2_WvT"), ("o2", "L2_WoT"),
                              ("q3", "L3_gnn_Wq"), ("k3", "L3_gnn_Wk"), ("v3", "L3_gnn_Wv"), ("o3", "L3_gnn_Wo")):
                load(w[key][:, :, :], tiled(name))
            load(wf1[:, :, :], tiled("L3_gnn_Wf1"))
            load(wf2[:, :, :], tiled("L3_gnn_Wf2"))
            for key, name in (("fc_b", "L0_gnn_fc_b"), ("gamma1", "L1_gnn_gamma"), ("beta1", "L1_gnn_beta"),
                              ("bv2", "L2_gnn_bv"), ("bo2", "L2_gnn_bo"), ("gamma2", "L2_gnn_gamma"),
                              ("beta2", "L2_gnn_beta"), ("bv3", "L3_gnn_bv"), ("bo3", "L3_gnn_bo"),
                              ("bf2", "L3_gnn_bf2")):
                load(rows[key][:, :], a[name].rearrange("(a n) -> a n", a=1).broadcast_to([P, D]))
            for key, name in (("q_w", "L0_gnn_q_w"), ("k_w", "L0_gnn_k_w"), ("fc_b", "L0_gnn_fc_b"), ("bq1", "L1_gnn_bq"), ("bk1", "L1_gnn_bk"),
                              ("bq2", "L2_gnn_bq"), ("bk2", "L2_gnn_bk"), ("bq3", "L3_gnn_bq"),
                              ("bk3", "L3_gnn_bk"), ("g1", "L3_gnn_g1"), ("b1", "L3_gnn_b1"),
                              ("g2", "L3_gnn_g2"), ("b2", "L3_gnn_b2")):
                load(cols[key][:, :], a[name + "_columns"])
            load(bf1[:, :], a["L3_gnn_bf1_columns"])
            load(qk_b[:, 0:1], a["L0_gnn_q_b"].rearrange("(a n) -> a n", a=1).broadcast_to([P, 1]))
            load(qk_b[:, 1:2], a["L0_gnn_k_b"].rearrange("(a n) -> a n", a=1).broadcast_to([P, 1]))

            sp.wait_ge(const_made, CONSTS)
            with sp.Fori(0, B) as b:
                sp.wait_ge(y_ready, b * 2 * T)
                sp.dma_start(x_in[:, :, :], a["x"][b].rearrange("(t p) d -> p t d", p=P)).then_inc(x_loaded, 16)
                for t in range(T):
                    last = att(b, 0, 0, len(DVE_TILES), 0) if t in DVE_TILES else att(b, 0, 0, len(POOL_TILES), 0)
                    sp.wait_ge(masked_dve if t in DVE_TILES else masked_pool, last)
                    sp.dma_start(mask[:, t, :], a["adj"][b, t * P:(t + 1) * P, :]).then_inc(mask_loaded[t], 16)
                for t in range(T):
                    sp.wait_ge(mask_used, b * T + t + 1)
                    sp.dma_start(mask[:, t, :], a["adj_t"][b, t * P:(t + 1) * P, :]).then_inc(mask_loaded[t], 16)

                for layer, names in enumerate((("q2", "k2"), ("q3", "k3"))):
                    if layer == 0:
                        wait_emptied(sp, b, "y2_t", 3)
                        wait_emptied(sp, b, "y2_t", 2)
                        sp.dma_start(k_aug[AUG - 1:AUG, :, :], minus_one[:, :]).then_inc(aug_loaded, 16)
                    for s, (name, aug) in enumerate(zip(names, (q_aug, k_aug))):
                        wait_emptied(sp, b, name, 3)
                        if layer == 1 and s == 0:
                            sp.wait_ge(g3_ready, b * T + T)
                        for g in range(C):
                            high, low = parts[:, 2 * s, g, :], parts[:, 2 * s + 1, g, :]
                            stack = (high, low, high) if s == 0 else (high, high, low)
                            for r, part in enumerate(stack):
                                for j in range(4):
                                    sp.dma_start(aug[r * DK:(r + 1) * DK, 4 * g + j, :],
                                                 part[j * DK:(j + 1) * DK, :]).then_inc(aug_loaded, 16)

                    def max_row(h):
                        if h >= 2:
                            sp.wait_ge(max_row_in[h % 2], (b * 2 + layer) * 16 * (H // 2) + 16 * (h // 2))
                            sp.sem_inc(passed, 1)
                        sp.wait_ge(max_done, max_count(b, layer, max_order(h + 1, 2) + 1 if h < H - 1 else H * (T + 1)))
                        sp.dma_start(q_aug[AUG - 1:AUG, h, :], max_rows[h % 2][:, :]).then_inc(max_row_in[h % 2], 16)

                    max_row(0)
                    max_row(1)
                    for h in range(H):
                        if h + 2 < H:
                            max_row(h + 2)
                        sp.wait_ge(o_out, att(b, layer, h, 1, 1))
                        r, g = DK * (h % 4), h // 4
                        for c in range(2):
                            cut = slice(c * HALF, (c + 1) * HALF)
                            for dst, at in ((o_t, 2 * DK * c), (sums_t, 2 * DK * c + DK)):
                                sp.dma_start(dst[r:r + DK, g, cut], o_raw[h % 2][at:at + DK, :])\
                                  .then_inc(o_moved[h % 2], 16)

                for g in range(4):
                    wait_emptied(sp, b, "ff2", g)
                    sp.dma_start(out[b].rearrange("(t p) d -> p t d", p=P)[:, 2 * g:2 * g + 2, :],
                                 y[:, 2 * g:2 * g + 2, :]).then_inc(stored, 16)
            sp.wait_ge(stored, B * 64)

        @block.tensor
        def _(pe):
            pe.wait_ge(weights_in, 16 * len(weight_dmas))
            for c in range(C):
                for o in range(C):
                    nc.tensor.matmul(ps[:, 0, c:c + 1], fcw[:, o, c * P:(c + 1) * P], cols["k_w"][:, o:o + 1],
                                     start=(o == 0), stop=(o == C - 1))
                for o in range(C):
                    nc.tensor.matmul(ps[:, 1, c:c + 1], fcw[:, o, c * P:(c + 1) * P], cols["q_w"][:, o:o + 1],
                                     start=(o == 0), stop=(o == C - 1))
            pe.wait_ge(setup_dve, 3)
            for i, key in enumerate(("q_w", "k_w")):
                for o in range(C):
                    last = nc.tensor.matmul(ps[:, 2 + i, 0:1], bias_rep[:, o, :], cols[key][:, o:o + 1],
                                            start=(o == 0), stop=(o == C - 1))
            last.then_inc(setup_mm, 1)
            pe.wait_ge(setup_dve, 7)
            pe.wait_ge(const_made, CONSTS)

            def turn(name, i, group):
                bank = free_bank(name, i)
                for j in range(4):
                    t = 4 * (i % 2) + j
                    last = nc.tensor.transpose(ps[:, bank, j * P:(j + 1) * P],
                                               group[:, t, (i // 2) * P:(i // 2 + 1) * P], ident[:, :])
                last.then_inc(lin_done, 1)

            def free_bank(name, i):
                at = PLACE[(name, i)]
                if at < LIN_BANKS:
                    pe.wait_ge(act_emptied, graph[0] * N_ACT)
                    pe.wait_ge(dve_emptied, graph[0] * N_DVE)
                else:
                    wait_emptied(pe, graph[0], *UNITS[at - LIN_BANKS][:2])
                return at % LIN_BANKS

            def nodes_by(name, i, lhs, rhs, tiles):
                bank = free_bank(name, i)
                for j in range(2):
                    t = 2 * i + j
                    for c in range(tiles):
                        last = nc.tensor.matmul(ps[:, bank, j * D:(j + 1) * D], lhs(c, t), rhs[:, c, :],
                                                start=(c == 0), stop=(c == tiles - 1))
                last.then_inc(lin_done, 1)

            def features_by(name, i, weight, half, m):
                bank = free_bank(name, i)
                for c in range(C):
                    last = nc.tensor.matmul(ps[:, bank, :], weight[:, c, m * P:(m + 1) * P],
                                            y_t[:, c, half * HALF:(half + 1) * HALF],
                                            start=(c == 0), stop=(c == C - 1))
                last.then_inc(lin_done, 1)

            def y_tile(c, t):
                return y_t[:, c, t * P:(t + 1) * P]

            def attend(b, layer, t):
                base = b * 2 * T + layer * T
                if t < T:
                    pe.wait_ge(p_ready, base + t + 1)
                    pe.wait_ge(t_act, base + t)
                    pe.wait_ge(t_dve, base + t)
                    for k in range(T):
                        last = nc.tensor.transpose(flat[:, 4 * HALF + k * P:4 * HALF + (k + 1) * P],
                                                   scores[:, t % 3, k * P:(k + 1) * P], ident[:, :])
                    last.then_inc(t_done, 1)
                if t > 0:
                    pe.wait_ge(t_act, base + t)
                    pe.wait_ge(t_dve, base + t)
                    if layer or t > 2:
                        pe.wait_ge(y_ready, base + t - 2)
                    for k in range(T):
                        last = nc.tensor.matmul(ps[:, 6 + (t - 1) % 2, 0:D], probs_t[:, (t - 1) % 2, k, :],
                                                values[:, k, :], start=(k == 0), stop=(k == T - 1))
                    last.then_inc(av_done, 1)

            def head(b, layer, h, i, scores_two_ahead, first=False):
                for t in range(T):
                    if t == 2 and scores_two_ahead:
                        rows_of_maxima(b, layer, h + 1, 1 - i, max_order(h + 2, 2), (i + 1) % 2)
                    if t == 2 and not scores_two_ahead and i == 0:
                        rows_of_maxima(b, layer, h + 1, 1 - i, max_order(H, 0), 1)
                    if scores_two_ahead:
                        k = t if t < 2 else t + 1
                        scores_for_maximum(b, layer, h + 2, t, max_order(h + 2, k), (i + k + 1) % 2)
                    if t == 0:
                        pe.wait_ge(max_row_in[i], (b * 2 + layer) * 8 * H + h * 8 + (16 - 8 * i))
                    for c in range(2):
                        if not first or t > 0:
                            pe.wait_ge(exp_done, att(b, layer, h, 2 * T, 2 * t + c - 1))
                        nc.tensor.matmul(ps[:, 4 + c, :], k_aug[0:AUG, h, t * P:(t + 1) * P],
                                         q_aug[0:AUG, h, c * HALF:(c + 1) * HALF],
                                         start=True, stop=True).then_inc(st_done, 1)
                    if t >= LAG:
                        with_values(b, layer, h, i, t - LAG, first)
                    elif not first:
                        with_values(b, layer, h - 1, 1 - i, T - LAG + t)

            def scores_for_maximum(b, layer, h, t, order, slot):
                pe.wait_ge(max_done, max_count(b, layer, order - 1))
                for c in range(2):
                    last = nc.tensor.matmul(ps[:, 2 * slot + c, :], q_aug[0:AUG - 1, h, t * P:(t + 1) * P],
                                            k_aug[0:AUG - 1, h, c * HALF:(c + 1) * HALF], start=True, stop=True)
                last.then_inc(nat_done, 1)

            def rows_of_maxima(b, layer, h, i, order, slot):
                pe.wait_ge(max_done, max_count(b, layer, order - 1))
                pe.wait_ge(max_cast, att(b, layer, h, 1, 1))
                nc.tensor.transpose(ps[0:T, 2 * slot, 0:P // 2].bitcast(BF16), row_max_bf[i][:, :],
                                    ident_bf[:, :]).then_inc(nat_done, 1)

            def with_values(b, layer, h, i, t, first=False):
                if t in DVE_TILES:
                    pe.wait_ge(masked_dve, att(b, layer, h, len(DVE_TILES), DVE_TILES.index(t) + 1))
                else:
                    pe.wait_ge(masked_pool, att(b, layer, h, len(POOL_TILES), POOL_TILES.index(t) + 1))
                if t == 0:
                    pe.wait_ge(v_ready, att(b, layer, h, 1, 1))
                    if not first:
                        pe.wait_ge(o_out, att(b, layer, h, 1, -1))
                for c in range(2):
                    last = nc.tensor.matmul(ps[64 * c:64 * c + 64, 6 + i, :], v_head[i][:, t, :],
                                            probs[:, t % RING, c * HALF:(c + 1) * HALF],
                                            start=(t == 0), stop=(t == T - 1))
                last.then_inc(pv_done, 1)

            def heads(b, layer):
                wait_all_emptied(pe, b, ("v2", "v3")[layer], 4)
                pe.wait_ge(aug_loaded, b * 16 * 97 + (16 * 49 if layer == 0 else 16 * 97))
                for t in range(T):
                    order = t
                    if order < 2:
                        for c in range(2):
                            last = nc.tensor.matmul(ps[:, 2 * order + c, :], q_aug[0:AUG - 1, 0, t * P:(t + 1) * P],
                                                    k_aug[0:AUG - 1, 0, c * HALF:(c + 1) * HALF], start=True, stop=True)
                        last.then_inc(nat_done, 1)
                    else:
                        scores_for_maximum(b, layer, 0, t, order, order % 2)
                for t in range(T):
                    if t == 2:
                        rows_of_maxima(b, layer, 0, 0, max_order(1, 2), max_order(1, 2) % 2)
                    order = max_order(1, t if t < 2 else t + 1)
                    scores_for_maximum(b, layer, 1, t, order, order % 2)
                for h in range(2):
                    head(b, layer, h, h, True, h == 0)
                with pe.Fori(1, H // 2 - 1) as pair:
                    for i in range(2):
                        head(b, layer, 2 * pair + i, i, True)
                for h in range(H - 2, H):
                    head(b, layer, h, h % 2, False)
                for t in range(T - LAG, T):
                    with_values(b, layer, H - 1, 1, t)

            graph = [0]
            with pe.Fori(0, B) as b:
                graph[0] = b
                pe.wait_ge(x_loaded, b * 16 + 16)
                for i in range(4):
                    turn("x_t", i, x_in)
                wait_all_emptied(pe, b, "x_t", 4)
                for i in range(4):
                    nodes_by("proj0", i, y_tile, w["fc"], C)
                for i in range(2):
                    bank = free_bank("key0", i)
                    for c in range(C):
                        last = nc.tensor.matmul(ps[:, bank, :], key_w[:, c, :], y_t[:, c, i * HALF:(i + 1) * HALF],
                                                start=(c == 0), stop=(c == C - 1))
                    last.then_inc(lin_done, 1)
                bank = free_bank("query0", 0)
                for t in range(T):
                    for c in range(C):
                        last = nc.tensor.matmul(ps[:, bank, t:t + 1], y_tile(c, t), query_w[:, c:c + 1],
                                                start=(c == 0), stop=(c == C - 1))
                last.then_inc(lin_done, 1)
                wait_all_emptied(pe, b, "query0", 1)
                for t in range(T + 1):
                    attend(b, 0, t)
                pe.wait_ge(y_ready, b * 2 * T + T)
                for i in range(4):
                    turn("y1_t", i, y)
                wait_all_emptied(pe, b, "y1_t", 4)
                for name in ("q1", "k1"):
                    for i in range(4):
                        features_by(name, i, w[name], i % 2, i // 2)
                for i in range(4):
                    nodes_by("v1", i, y_tile, w["c1"], C)
                wait_all_emptied(pe, b, "v1", 4)
                for t in range(T + 2):
                    if t < T:
                        if t >= 2:
                            pe.wait_ge(s_ready, b * 2 * T + T + t - 1)
                        for n in range(2):
                            for c in range(C):
                                last = nc.tensor.matmul(ps[:, 2 * (t % 2) + n, :], q_t[:, c, t * P:(t + 1) * P],
                                                        k_t[:, c, n * HALF:(n + 1) * HALF],
                                                        start=(c == 0), stop=(c == C - 1))
                        last.then_inc(s_done, 1)
                    if t > 0:
                        attend(b, 1, t - 1)
                for layer, (turned, group, ready, q, k, v, o) in enumerate((
                        ("y2_t", y, (y_ready, b * 2 * T + 2 * T), "q2", "k2", "v2", "o2"),
                        ("y3_t", x_hat, (normal, b * 2 * T + T), "q3", "k3", "v3", "o3"))):
                    pe.wait_ge(*ready)
                    for i in range(4):
                        turn(turned, i, group)
                    wait_all_emptied(pe, b, turned, 4)
                    for name in (q, k):
                        for i in range(4):
                            features_by(name, i, w[name], i % 2, i // 2)
                    for i in range(4):
                        nodes_by(v, i, y_tile, w[v], C)
                    heads(b, layer)
                    for i in range(4):
                        pe.wait_ge(o_normal, b * 4 + layer * 2 + 2)
                        nodes_by(o, i, y_tile, w[o], C)
                pe.wait_ge(normal, b * 2 * T + 2 * T)
                for i in range(4):
                    turn("h_t", i, x_hat)
                wait_all_emptied(pe, b, "h_t", 4)
                for i in range(2 * F):
                    features_by("ff1", i, wf1, i % 2, i // 2)
                for i in range(4):
                    if i == 0:
                        wait_all_emptied(pe, b, "ff1", 2 * F)
                    nodes_by("ff2", i, lambda f, t: hidden[f // 4][:, f % 4, t * P:(t + 1) * P], wf2, F)

        @block.scalar
        def _(act):
            def empty_copy(b, name, i, dst):
                wait_lin(act, b, name, i)
                nc.scalar.copy(dst, ps[:, PLACE[(name, i)] % LIN_BANKS, :]).then_inc(act_emptied, 1)

            def empty(b, name, i, dst, func=ACT.Identity, bias=0.0, scale=1.0):
                wait_lin(act, b, name, i)
                nc.scalar.activation(dst, ps[:, PLACE[(name, i)] % LIN_BANKS, :], func, bias=bias,
                                     scale=scale).then_inc(act_emptied, 1)

            def copy_probs(b, layer, t):
                base = b * 2 * T + layer * T
                act.wait_ge(t_done, base + t + 1)
                act.wait_ge(av_done, base + (t - 1 if t >= 2 else 0))
                nc.scalar.copy(probs_t[:, t % 2, 0:4, :].rearrange("p t q -> p (t q)"), ps[:, 4, :]).then_inc(t_act, 1)

            def head(b, layer, h, i, first=False):
                for t in range(T):
                    for c in range(2):
                        act.wait_ge(st_done, att(b, layer, h, 2 * T, 2 * t + c + 1))
                        if c == 0 and (not first or t >= RING):
                            act.wait_ge(pv_done, att(b, layer, h, T, t - RING + 1))
                        nc.scalar.activation(probs[:, t % RING, c * HALF:(c + 1) * HALF], ps[:, 4 + c, :], ACT.Exp,
                                             scale=DK ** -0.5).then_inc(exp_done, 1)
                    if t == LAG and not first:
                        take_sums(b, layer, h - 1, 1 - i)

            def take_sums(b, layer, h, i):
                act.wait_ge(pv_done, att(b, layer, h, T, T))
                act.wait_ge(o_moved[i], (b * 2 + layer) * 4 * 64 + h * 32 + (-32 * i))
                nc.scalar.copy(o_raw[i][:, :], ps[:, 6 + i, :]).then_inc(o_out, 1)

            act.wait_ge(const_made, CONSTS)
            with act.Fori(0, B) as b:
                for i in range(0, 4, 2):
                    empty_copy(b, "x_t", i, y_t[:, i // 2, 0:HALF])
                for i in range(2):
                    empty(b, "key0", i, key_row[:, i * HALF:(i + 1) * HALF], bias=qk_const[:, 1:2])
                for t in range(T + 2):
                    if t < T:
                        act.wait_ge(s_ready, b * 2 * T + t + 1)
                        nc.scalar.activation(slack[:, t % 4, :], scores[:, t % 3, :], ACT.Identity,
                                             bias=slack_q[:, t:t + 1], scale=0.01).then_inc(slack_done, 1)
                    if 0 < t <= T:
                        u = t - 1
                        act.wait_ge(leaky_done, b * T + u + 1)
                        nc.scalar.activation(scores[:, u % 3, :], scores[:, u % 3, :], ACT.Exp,
                                             bias=neg_top[:, u:u + 1], accum_out=denom[:, u:u + 1]).then_inc(p_ready, 1)
                    if t > 1:
                        copy_probs(b, 0, t - 2)
                for i in range(0, 4, 2):
                    empty_copy(b, "y1_t", i, y_t[:, i // 2, 0:HALF])
                for name, dst, bias in (("q1", q_t, "bq1"), ("k1", k_t, "bk1")):
                    for i in range(0, 4, 2):
                        empty(b, name, i, dst[:, i // 2, 0:HALF], bias=cols[bias][:, i // 2:i // 2 + 1])
                for i in range(0, 4, 2):
                    empty_copy(b, "v1", i, values[:, 2 * i:2 * i + 2, :].rearrange("p t d -> p (t d)"))
                for t in range(T + 1):
                    if t < T:
                        act.wait_ge(s_ready, b * 2 * T + T + t + 1)
                        s = scores[:, t % 3, :]
                        nc.scalar.activation(s, s, ACT.Exp, bias=neg_top[:, t:t + 1], scale=D ** -0.5,
                                             accum_out=denom[:, t:t + 1]).then_inc(p_ready, 1)
                    if t > 0:
                        copy_probs(b, 1, t - 1)
                for layer in range(2):
                    turned, q, k = ("y2_t", "q2", "k2") if layer == 0 else ("y3_t", "q3", "k3")
                    if layer == 1:
                        for t in range(T):
                            if t >= 4:
                                act.wait_ge(g3_ready, b * T + t - 3)
                            else:
                                act.wait_ge(g_ready, b * T + T)
                            nc.scalar.activation(mask_exp[:, t % 4, :], mask[:, t, :], ACT.Exp, bias=minus_ones[:, 0:1],
                                                 scale=2.0).then_inc(e_ready, 1)
                    for i in range(0, 4, 2):
                        if layer == 0:
                            empty_copy(b, turned, i, y_t[:, i // 2, 0:HALF])
                        else:
                            empty(b, turned, i, y_t[:, i // 2, 0:HALF], bias=cols["b1"][:, i // 2:i // 2 + 1],
                                  scale=cols["g1"][:, i // 2:i // 2 + 1])
                    for s, name in enumerate((q, k)):
                        for i in range(4):
                            wait_lin(act, b, name, i)
                            nc.scalar.activation(parts[:, 2 * s, i // 2, (i % 2) * HALF:(i % 2 + 1) * HALF],
                                                 ps[:, PLACE[(name, i)] % LIN_BANKS, :], ACT.Identity,
                                                 bias=cols["b" + name][:, i // 2:i // 2 + 1]).then_inc(hi_ready, 1)
                    for h in range(2):
                        head(b, layer, h, h, h == 0)
                    with act.Fori(1, H // 2 - 1) as pair:
                        for i in range(2):
                            head(b, layer, 2 * pair + i, i)
                    for h in range(H - 2, H):
                        head(b, layer, h, h % 2)
                    take_sums(b, layer, H - 1, 1)
                for i in range(0, 4, 2):
                    empty(b, "h_t", i, y_t[:, i // 2, 0:HALF], bias=cols["b2"][:, i // 2:i // 2 + 1],
                          scale=cols["g2"][:, i // 2:i // 2 + 1])
                for i in range(2 * F):
                    f, half = i // 2, i % 2
                    empty(b, "ff1", i, hidden[f // 4][:, f % 4, half * HALF:(half + 1) * HALF], ACT.Gelu,
                          bias=bf1[:, f:f + 1])

        @block.vector
        def _(dve):
            graph = [0]
            steps = [0]
            norms = [0]

            def then(ins):
                steps[0] += 1
                ins.then_inc(dve_step, 1)
                dve.wait_ge(dve_step, graph[0] * DVE_STEPS + steps[0])

            def row(name, n):
                return rows[name][:, :].rearrange("p (a d) -> p a d", a=1).broadcast_to([P, n, D])

            def unit(name, i):
                wait_lin(dve, graph[0], name, i)
                return ps[:, PLACE[(name, i)] % LIN_BANKS, :]

            def copy_probs(b, layer, t):
                base = b * 2 * T + layer * T
                dve.wait_ge(t_done, base + t + 1)
                dve.wait_ge(av_done, base + (t - 1 if t >= 2 else 0))
                nc.vector.tensor_copy(probs_t[:, t % 2, 4:8, :].rearrange("p t q -> p (t q)"), ps[:, 5, :])\
                  .then_inc(t_dve, 1)

            def normalize(t, dst):
                nc.vector.bn_stats(stats[:, t, :], y[:, t, :]).then_inc(stats_ready, 1)
                dve.wait_ge(stats_ready, graph[0] * 4 * T + norms[0] + 1)
                dve.sem_inc(passed, 1)
                then(nc.vector.bn_aggr(mean_var[:, t, :], stats[:, t, :]))
                nc.vector.tensor_scalar(var_eps[:, t:t + 1], mean_var[:, t, 1:2], EPS, None, ALU.add)\
                  .then_inc(var_ready, 1)
                norms[0] += 1
                dve.wait_ge(rstd_ready, graph[0] * 4 * T + norms[0])
                return nc.vector.tensor_scalar(dst[:, t, :], y[:, t, :], mean_var[:, t, 0:1], rstd[:, t:t + 1],
                                               ALU.subtract, ALU.mult)

            def head(b, layer, h, i, maxima_two_ahead):
                for t in range(T):
                    if t == 2 and (maxima_two_ahead or i == 0):
                        take_rows(b, layer, h + 1, 1 - i, max_order(h + 2, 2) if maxima_two_ahead else max_order(H, 0),
                                  (i + 1) % 2, False)
                    if maxima_two_ahead:
                        k = t if t < 2 else t + 1
                        maximum(b, layer, i, t, max_order(h + 2, k), (i + k + 1) % 2)
                    if t in DVE_TILES:
                        dve.wait_ge(exp_done, att(b, layer, h, 2 * T, 2 * t + 2))
                        p = probs[:, t % RING, :]
                        nc.vector.tensor_tensor(p, p, mask[:, t, :], ALU.mult).then_inc(masked_dve, 1)
                if maxima_two_ahead:
                    cast_maxima(b, layer, h + 2, i, max_order(h + 2, T))

            def maximum(b, layer, i, t, order, slot):
                dve.wait_ge(nat_done, max_count(b, layer, order + 1))
                nc.vector.tensor_reduce(row_max[i][:, t:t + 1], flat[:, slot * N:(slot + 1) * N], AX.X, ALU.max)\
                  .then_inc(max_done, 1)

            def cast_maxima(b, layer, h, i, last_order):
                dve.wait_ge(max_done, max_count(b, layer, last_order + 1))
                nc.vector.tensor_copy(row_max_bf[i][:, :], row_max[i][:, :]).then_inc(max_cast, 1)

            def take_rows(b, layer, h, i, order, slot, first):
                dve.wait_ge(nat_done, max_count(b, layer, order + 1))
                dve.wait_ge(max_row_in[i], (b * 2 + layer) * 8 * H + h * 8 - 8 * i)
                nc.vector.tensor_copy(max_rows[i][:, :], ps[0:T, 2 * slot, 0:P // 2].bitcast(BF16))\
                  .then_inc(max_done, 1)

            nc.vector.memset(ones[:, :], 1.0).then_inc(setup_dve, 1)
            nc.vector.memset(minus_one[:, :], -1.0).then_inc(const_made, 1)
            for i in range(2):
                last = nc.vector.memset(v_head[i][:, :, :], 1.0)
            last.then_inc(const_made, 1)
            nc.vector.memset(minus_ones[:, :], -1.0).then_inc(const_made, 1)
            nc.vector.memset(minus_half[:, :], -0.5).then_inc(const_made, 1)
            dve.wait_ge(setup_dve, 1)
            dve.wait_ge(weights_in, 16 * len(weight_dmas))
            for c in range(C):
                nc.vector.tensor_scalar(bias_rep[:, c, :], ones[:, :], cols["fc_b"][:, c:c + 1], None, ALU.mult)\
                  .then_inc(setup_dve, 1)
            dve.wait_ge(setup_mm, 1)
            for c in range(C):
                nc.vector.tensor_scalar(key_w[:, c, :], ones[:, :], ps[:, 0, c:c + 1], None, ALU.mult)\
                  .then_inc(setup_dve, 1)
            nc.vector.tensor_copy(query_w[:, :], ps[:, 1, 0:C]).then_inc(setup_dve, 1)
            for i in range(2):
                last = nc.vector.tensor_tensor(qk_const[:, i:i + 1], ps[:, 2 + i, 0:1], qk_b[:, i:i + 1], ALU.add)
            last.then_inc(setup_dve, 1)
            dve.wait_ge(const_made, CONSTS)

            with dve.Fori(0, B) as b:
                graph[0] = b
                for i in (1, 3):
                    nc.vector.tensor_copy(y_t[:, i // 2, HALF:N], unit("x_t", i)).then_inc(dve_emptied, 1)
                for i in range(4):
                    nc.vector.tensor_tensor(values[:, 2 * i:2 * i + 2, :],
                                            unit("proj0", i).rearrange("p (t d) -> p t d", t=2),
                                            row("fc_b", 2), ALU.add).then_inc(dve_emptied, 1)
                nc.vector.tensor_scalar(q_n[:, :], unit("query0", 0)[:, 0:T], qk_const[:, 0:1], None, ALU.add)\
                  .then_inc(dve_emptied, 1)
                wait_all_emptied(dve, b, "query0", 1)
                then(nc.vector.tensor_scalar(slack_q[:, :], q_n[:, :], 0.01, None, ALU.mult))
                for t in range(T + 3):
                    if t < T:
                        s = scores[:, t % 3, :]
                        dve.wait_ge(pen_ready, b * T + t + 1)
                        dve.sem_inc(passed, 1)
                        then(nc.vector.tensor_tensor_reduce(s, s, key_row, 1.0, LOWEST, ALU.add, ALU.max,
                                                            top[:, t:t + 1]))
                        then(nc.vector.tensor_scalar(top2[:, t:t + 1], top[:, t:t + 1], q_n[:, t:t + 1], None, ALU.add))
                        then(nc.vector.scalar_tensor_tensor(top[:, t:t + 1], top2[:, t:t + 1], 0.01, top2[:, t:t + 1],
                                                            ALU.mult, ALU.max))
                        nc.vector.tensor_scalar(neg_top[:, t:t + 1], top[:, t:t + 1], -1.0, None, ALU.mult)\
                          .then_inc(s_ready, 1)
                    if 0 < t <= T:
                        u = t - 1
                        s = scores[:, u % 3, :]
                        dve.wait_ge(slack_done, b * T + u + 1)
                        nc.vector.scalar_tensor_tensor(s, s, q_n[:, u:u + 1], slack[:, u % 4, :], ALU.add, ALU.max)\
                          .then_inc(leaky_done, 1)
                    if 1 < t <= T + 1:
                        copy_probs(b, 0, t - 2)
                    if t > 2:
                        u = t - 3
                        then(nc.vector.reciprocal(rden[:, u:u + 1], denom[:, u:u + 1]))
                        dve.wait_ge(av_done, b * 2 * T + u + 1)
                        if u == 0:
                            dve.wait_ge(stored, b * 64)
                        nc.vector.scalar_tensor_tensor(y[:, u, :], ps[:, 6 + u % 2, 0:D], rden[:, u:u + 1],
                                                       x_in[:, u, :], ALU.mult, ALU.add).then_inc(y_ready, 1)
                for i in (1, 3):
                    nc.vector.tensor_copy(y_t[:, i // 2, HALF:N], unit("y1_t", i)).then_inc(dve_emptied, 1)
                for name, dst, bias in (("q1", q_t, "bq1"), ("k1", k_t, "bk1")):
                    for i in (1, 3):
                        nc.vector.tensor_scalar(dst[:, i // 2, HALF:N], unit(name, i), cols[bias][:, i // 2:i // 2 + 1],
                                                None, ALU.add).then_inc(dve_emptied, 1)
                for i in (1, 3):
                    nc.vector.tensor_copy(values[:, 2 * i:2 * i + 2, :].rearrange("p t d -> p (t d)"), unit("v1", i))\
                      .then_inc(dve_emptied, 1)
                for t in range(T + 2):
                    if t < T:
                        s = scores[:, t % 3, :]
                        if t >= 3:
                            dve.wait_ge(t_done, b * 2 * T + T + t - 2)
                        nc.vector.tensor_scalar(s, mask[:, t, :], 0.0, -1e18 * D ** 0.5, ALU.is_equal, ALU.mult)\
                          .then_inc(mask_used, 1)
                        dve.wait_ge(mask_used, b * T + t + 1)
                        dve.wait_ge(s_done, b * T + t + 1)
                        dve.sem_inc(passed, 1)
                        then(nc.vector.tensor_tensor_reduce(s, flat[:, (t % 2) * N:(t % 2 + 1) * N], s, 1.0, LOWEST,
                                                            ALU.add, ALU.max, top[:, t:t + 1]))
                        nc.vector.tensor_scalar(some[:, t:t + 1], top[:, t:t + 1], -0.5e18 * D ** 0.5, None, ALU.is_gt)
                        nc.vector.tensor_scalar(neg_top[:, t:t + 1], top[:, t:t + 1], -(D ** -0.5), None, ALU.mult)\
                          .then_inc(s_ready, 1)
                    if 0 < t <= T:
                        copy_probs(b, 1, t - 1)
                    if t > 1:
                        u = t - 2
                        dve.wait_ge(av_done, b * 2 * T + T + u + 1)
                        then(nc.vector.reciprocal(rden[:, u:u + 1], denom[:, u:u + 1]))
                        then(nc.vector.tensor_tensor(rden2[:, u:u + 1], rden[:, u:u + 1], some[:, u:u + 1], ALU.mult))
                        then(nc.vector.scalar_tensor_tensor(y[:, u, :], ps[:, 6 + u % 2, 0:D], rden2[:, u:u + 1],
                                                            y[:, u, :], ALU.mult, ALU.add))
                        then(normalize(u, y))
                        then(nc.vector.tensor_tensor(y[:, u, :], y[:, u, :], rows["gamma1"][:, :], ALU.mult))
                        nc.vector.tensor_tensor(y[:, u, :], y[:, u, :], rows["beta1"][:, :], ALU.add).then_inc(y_ready, 1)
                for layer in range(2):
                    turned, q, k, v, o = [x + "23"[layer] for x in ("y", "q", "k", "v", "o")]
                    turned += "_t"
                    for i in (1, 3):
                        if layer == 0:
                            nc.vector.tensor_copy(y_t[:, i // 2, HALF:N], unit(turned, i)).then_inc(dve_emptied, 1)
                        else:
                            nc.vector.tensor_scalar(y_t[:, i // 2, HALF:N], unit(turned, i),
                                                    cols["g1"][:, i // 2:i // 2 + 1], cols["b1"][:, i // 2:i // 2 + 1],
                                                    ALU.mult, ALU.add).then_inc(dve_emptied, 1)
                    for s, name in enumerate((q, k)):
                        for i in range(4):
                            cut = slice((i % 2) * HALF, (i % 2 + 1) * HALF)
                            dve.wait_ge(hi_ready, b * 16 + layer * 8 + s * 4 + i + 1)
                            nc.vector.scalar_tensor_tensor(parts[:, 2 * s + 1, i // 2, cut], unit(name, i),
                                                           cols["b" + name][:, i // 2:i // 2 + 1],
                                                           parts[:, 2 * s, i // 2, cut], ALU.add, ALU.subtract)\
                              .then_inc(dve_emptied, 1)
                    for i in range(4):
                        nc.vector.tensor_tensor(values[:, 2 * i:2 * i + 2, :],
                                                unit(v, i).rearrange("p (t d) -> p t d", t=2),
                                                row("b" + v, 2), ALU.add).then_inc(dve_emptied, 1)
                    if layer == 0:
                        for t in range(T):
                            dve.wait_ge(mask_loaded[t], b * 32 + 32)
                            nc.vector.tensor_scalar(mask[:, t, :], mask[:, t, :], 1e-8, None, ALU.max)\
                              .then_inc(g_ready, 1)
                        dve.wait_ge(g_ready, b * T + T)
                    else:
                        dve.wait_ge(g3_ready, b * T + T)
                    for t in range(T):
                        maximum(b, layer, 0, t, t, t % 2)
                    cast_maxima(b, layer, 0, 0, T - 1)
                    for t in range(T):
                        if t == 2:
                            take_rows(b, layer, 0, 0, max_order(1, 2), max_order(1, 2) % 2, True)
                        order = max_order(1, t if t < 2 else t + 1)
                        maximum(b, layer, 1, t, order, order % 2)
                    cast_maxima(b, layer, 1, 1, max_order(1, T))
                    for h in range(2):
                        head(b, layer, h, h, True)
                    with dve.Fori(1, H // 2 - 1) as pair:
                        for i in range(2):
                            head(b, layer, 2 * pair + i, i, True)
                    for h in range(H - 2, H):
                        head(b, layer, h, h % 2, False)
                    for i in range(2):
                        dve.wait_ge(o_moved[i], (b * 2 + layer + 1) * 4 * 64)
                    for g in range(C):
                        then(nc.vector.reciprocal(sums_t[:, g, :], sums_t[:, g, :]))
                        nc.vector.tensor_tensor(o_t[:, g, :], o_t[:, g, :], sums_t[:, g, :], ALU.mult)\
                          .then_inc(o_normal, 1)
                    dve.wait_ge(residual, b * 3 + layer + 1)
                    for i in range(4):
                        nc.vector.tensor_tensor(y[:, 2 * i:2 * i + 2, :],
                                                unit(o, i).rearrange("p (t d) -> p t d", t=2),
                                                y[:, 2 * i:2 * i + 2, :], ALU.add).then_inc(dve_emptied, 1)
                        wait_emptied(dve, b, o, i)
                        for t in (2 * i, 2 * i + 1):
                            if layer == 0:
                                then(normalize(t, y))
                                then(nc.vector.tensor_tensor(y[:, t, :], y[:, t, :], rows["gamma2"][:, :], ALU.mult))
                                then(nc.vector.tensor_tensor(y[:, t, :], y[:, t, :], rows["beta2"][:, :], ALU.add))
                            normalize(t, x_hat).then_inc(normal, 1)
                for i in (1, 3):
                    nc.vector.tensor_scalar(y_t[:, i // 2, HALF:N], unit("h_t", i), cols["g2"][:, i // 2:i // 2 + 1],
                                            cols["b2"][:, i // 2:i // 2 + 1], ALU.mult, ALU.add)\
                      .then_inc(dve_emptied, 1)
                dve.wait_ge(residual, b * 3 + 3)
                for i in range(4):
                    nc.vector.tensor_tensor(y[:, 2 * i:2 * i + 2, :], unit("ff2", i).rearrange("p (t d) -> p t d", t=2),
                                            y[:, 2 * i:2 * i + 2, :], ALU.add).then_inc(dve_emptied, 1)
            assert steps[0] == DVE_STEPS, steps[0]

        @block.gpsimd
        def _(pool):
            nc.gpsimd.memset(ident[:, :], 0.0).then_inc(ident_made, 1)
            nc.gpsimd.memset(ident_bf[:, :], 0.0).then_inc(ident_made, 1)
            pool.wait_ge(ident_made, 2)
            for m in (ident, ident_bf):
                nc.gpsimd.affine_select(out=m[:, :], in_=m[:, :], compare_op=ALU.not_equal, fill=1.0, base=0,
                                        pattern=[[-1, P]], channel_multiplier=1).then_inc(const_made, 1)

            def copy_values(b, layer, h, i, first=False):
                pool.wait_ge(pv_done, att(b, layer, h, T, -T if not first else 0))
                pool.sem_inc(passed, 1)
                nc.gpsimd.tensor_copy(v_head[i][:, :, 0:DK], values[:, :, bass.ds(h * DK, DK)]).then_inc(v_ready, 1)

            def head(b, layer, h, i, last=False):
                for t in POOL_TILES:
                    pool.wait_ge(exp_done, att(b, layer, h, 2 * T, 2 * t + 2))
                    p = probs[:, t % RING, :]
                    nc.gpsimd.tensor_tensor(p, p, mask[:, t, :], ALU.mult).then_inc(masked_pool, 1)
                    if t == POOL_TILES[1] and not last:
                        copy_values(b, layer, h + 1, 1 - i)

            pool.wait_ge(const_made, CONSTS)
            norms = [0]

            def inverse_deviations(b, tiles):
                for t in tiles:
                    norms[0] += 1
                    pool.wait_ge(var_ready, b * 4 * T + norms[0])
                    nc.gpsimd.tensor_tensor(rstd[:, t:t + 1], var_eps[:, t:t + 1], minus_half[:, 0:1], ALU.pow)\
                      .then_inc(rstd_ready, 1)

            with pool.Fori(0, B) as b:
                for t in range(T):
                    pool.wait_ge(mask_loaded[t], b * 32 + 16)
                    if t >= 3:
                        pool.wait_ge(t_done, b * 2 * T + t - 2)
                    elif t == 0:
                        pool.wait_ge(dve_emptied, b * N_DVE)
                    pool.sem_inc(passed, 1)
                    nc.gpsimd.tensor_scalar(scores[:, t % 3, :], mask[:, t, :], -1.0, 1e9, ALU.add, ALU.mult)\
                      .then_inc(pen_ready, 1)
                inverse_deviations(b, range(T))
                for layer in range(2):
                    if layer == 1:
                        for t in range(T):
                            pool.wait_ge(e_ready, b * T + t + 1)
                            pool.sem_inc(passed, 1)
                            nc.gpsimd.tensor_scalar(mask[:, t, :], mask[:, t, :], 0.75, 0.25, ALU.mult, ALU.add)\
                              .then_inc(quarter_done, 1)
                            pool.wait_ge(quarter_done, b * T + t + 1)
                            nc.gpsimd.tensor_tensor(mask[:, t, :], mask[:, t, :], mask_exp[:, t % 4, :], ALU.mult)\
                              .then_inc(g3_ready, 1)
                    wait_all_emptied(pool, b, ("v2", "v3")[layer], 4)
                    copy_values(b, layer, 0, 0, True)
                    nc.gpsimd.tensor_tensor(y[:, :, :], y[:, :, :],
                                            rows[("bo2", "bo3")[layer]][:, :].rearrange("p (a d) -> p a d", a=1)
                                            .broadcast_to([P, T, D]), ALU.add).then_inc(residual, 1)
                    if layer == 0:
                        pool.wait_ge(g_ready, b * T + T)
                    for h in range(2):
                        head(b, layer, h, h)
                    with pool.Fori(1, H // 2 - 1) as pair:
                        for i in range(2):
                            head(b, layer, 2 * pair + i, i)
                    for h in range(H - 2, H):
                        head(b, layer, h, h % 2, h == H - 1)
                    inverse_deviations(b, [t for t in range(T) for _ in range(2 - layer)])
                pool.wait_ge(normal, b * 2 * T + 2 * T)
                nc.gpsimd.tensor_tensor(y[:, :, :], y[:, :, :],
                                        rows["bf2"][:, :].rearrange("p (a d) -> p a d", a=1)
                                        .broadcast_to([P, T, D]), ALU.add).then_inc(residual, 1)


LAYOUTS = {"L0_fc_wT": "L0_gnn_fc_w", "L2_WqT": "L2_gnn_Wq", "L2_WkT": "L2_gnn_Wk", "L2_WvT": "L2_gnn_Wv",
           "L2_WoT": "L2_gnn_Wo"}

COLUMNS = ("L0_gnn_q_w", "L0_gnn_k_w", "L0_gnn_fc_b", "L1_gnn_bq", "L1_gnn_bk", "L2_gnn_bq", "L2_gnn_bk",
           "L3_gnn_bq", "L3_gnn_bk", "L3_gnn_g1", "L3_gnn_b1", "L3_gnn_g2", "L3_gnn_b2", "L3_gnn_bf1")
UNUSED = ("L2_gnn_Wq", "L2_gnn_Wk", "L2_gnn_Wv", "L2_gnn_Wo", *(n for n in COLUMNS if n != "L0_gnn_fc_b"))


def kernel(**inputs):
    import numpy as np
    import concourse.bacc as bacc
    from concourse.bass_utils import run_bass_kernel_spmd

    arrays = {name: np.ascontiguousarray(x) for name, x in inputs.items()}
    for name, source in LAYOUTS.items():
        arrays[name] = np.ascontiguousarray(np.asarray(inputs[source]).T)
    arrays["adj_t"] = np.ascontiguousarray(np.asarray(inputs["adj"]).transpose(0, 2, 1))
    for name in COLUMNS:
        arrays[name + "_columns"] = np.ascontiguousarray(np.asarray(inputs[name]).reshape(-1, P).T)
    for unused in UNUSED:
        del arrays[unused]
    nc = bacc.Bacc("TRN2", target_bir_lowering=False, num_devices=1)
    aps = {name: nc.dram_tensor(f"in_{name}", x.shape, mybir.dt.from_np(x.dtype), kind="ExternalInput").ap()
           for name, x in arrays.items()}
    shape = arrays["x"].shape
    result = nc.dram_tensor("result", shape, F32, kind="ExternalOutput").ap()
    build(nc, aps, result)
    r = run_bass_kernel_spmd(nc, [{f"in_{name}": x for name, x in arrays.items()}], core_ids=[0])
    return r.results[0]["result"]
```

```python
from contextlib import ExitStack

import concourse.bass as bass
from concourse import mybir

F32 = mybir.dt.float32
BF16 = mybir.dt.bfloat16
ACT = mybir.ActivationFunctionType
ALU = mybir.AluOpType
AX = mybir.AxisListType

P = 128
N = 1024
D = 256
T = N // P
C = D // P
HALF = 512
H = 8
DK = D // H
FF = 4 * D
F = FF // P
AUG = 3 * DK + 1
LAG = 3
RING = 4
POOL_TILES = (1, 3, 5, 7)
DVE_TILES = tuple(t for t in range(T) if t not in POOL_TILES)
EARLY_EXPS = (1, 2, 5, 6)
EARLY_MASKS = (3, 4, 6, 7)
EPS = 1e-5
AUG_DMAS = 6
AUG_COUNT = 16 * (2 * AUG_DMAS + 1)
LOWEST = -3.0e38

LINEAR = [
    ("x_t", 4, "AD"), ("proj0", 4, "D"), ("key0", 2, "A"), ("query0", 1, "D"),
    ("y1_t", 4, "AD"), ("q1", 4, "AD"), ("k1", 4, "AD"), ("v1", 4, "AD"),
    ("y2_t", 4, "AD"), ("q2.0", 2, "D"), ("k2.0", 2, "D"), ("q2.1", 2, "D"), ("k2.1", 2, "D"), ("v2", 4, "D"),
    ("o2", 4, "D"),
    ("y3_t", 4, "AD"), ("q3.0", 2, "D"), ("k3.0", 2, "D"), ("q3.1", 2, "D"), ("k3.1", 2, "D"), ("v3", 4, "D"),
    ("o3", 4, "D"),
    ("h_t", 4, "AD"), ("ff1", 16, "A"), ("ff2", 4, "D"),
]
UPPER = ("q2.1", "k2.1", "v2", "q3.1", "k3.1", "v3")
UNITS = [(name, i, owners[i % len(owners)]) for name, n, owners in LINEAR for i in range(n)]
PLACE = {(name, i): at for at, (name, i, _) in enumerate(UNITS)}
N_LIN = len(UNITS)
N_ACT = sum(o == "A" for _, _, o in UNITS)
N_DVE = N_LIN - N_ACT
LIN_BANKS = 4


def bank_of(name, i):
    return PLACE[(name, i)] % LIN_BANKS + (LIN_BANKS if name in UPPER else 0)


CONSTS = 6
NORMS = T + 6
DVE_STEPS = 99


def emptied_before(name, i):
    at = PLACE[(name, i)]
    a = sum(o == "A" for _, _, o in UNITS[:at])
    return a, at - a


def build(nc, a, out):
    B = out.shape[0]
    with ExitStack() as ctx:
        def sb(name, shape, dt=F32):
            return ctx.enter_context(nc.sbuf_tensor(name, shape, dt))

        def sem(name):
            return ctx.enter_context(nc.semaphore(name))

        ps = ctx.enter_context(nc.psum_tensor("ps", [P, 8, HALF], F32))
        flat = ps[:, :, :].rearrange("p b n -> p (b n)")

        x_in = sb("x_in", [P, T, D])
        y = sb("y", [P, T, D])
        y_t = sb("y_t", [P, C, N])
        o_t = y_t
        values = sb("values", [P, T, D])
        x_hat = values
        mask = sb("mask", [P, T, N])
        sums_t = sb("sums_t", [P, C, N])
        region_q = sb("region_q", [P, 4096])
        region_k = sb("region_k", [P, 4096])
        region_p = sb("region_p", [P, 4096])
        q_aug = region_q[:, :].bitcast(BF16).rearrange("p (h n) -> p h n", h=H)
        k_aug = region_k[:, :].bitcast(BF16).rearrange("p (h n) -> p h n", h=H)
        probs = region_p[:, :].rearrange("p (r n) -> p r n", r=RING)
        parts = region_p[:, :].bitcast(BF16).rearrange("p (s g n) -> p s g n", s=4, g=C)
        mask_exp = x_in[:, :, :].rearrange("p (s t) d -> p s (t d)", s=2)
        q_t = region_q[:, 0:C * N].rearrange("p (c n) -> p c n", c=C)
        k_t = region_q[:, C * N:2 * C * N].rearrange("p (c n) -> p c n", c=C)
        scores = region_k[:, 0:3 * N].rearrange("p (r n) -> p r n", r=3)
        slack = region_q[:, :].rearrange("p (r n) -> p r n", r=4)
        key_row = region_k[:, 3 * N:4 * N]
        probs_t = region_p[:, 0:2 * N].rearrange("p (r t q) -> p r t q", r=2, t=T)
        hidden = [region_q[:, :].rearrange("p (f n) -> p f n", f=4),
                  region_k[:, :].rearrange("p (f n) -> p f n", f=4)]
        fcw = region_q[:, 0:C * D].rearrange("p (c n) -> p c n", c=C)
        bias_rep = region_q[:, 1024:1024 + C * P].rearrange("p (c n) -> p c n", c=C)

        v_head = [sb(f"v_head{i}", [P, T, 2 * DK]) for i in range(2)]
        o_raw = [sb(f"o_raw{i}", [P, HALF]) for i in range(2)]
        row_max = [sb(f"row_max{i}", [P, T]) for i in range(2)]
        row_max_bf = [sb(f"row_max_bf{i}", [P, T], BF16) for i in range(2)]
        max_rows = [sb(f"max_rows{i}", [T, P], BF16) for i in range(2)]

        w = {n: sb(f"w_{n}", [P, C, D]) for n in
             ("fc", "q1", "k1", "c1", "q2", "k2", "v2", "o2", "q3", "k3", "v3", "o3")}
        wf1 = sb("wf1", [P, C, FF])
        wf2 = sb("wf2", [P, F, D])
        rows = {n: sb(f"r_{n}", [P, D]) for n in
                ("fc_b", "gamma1", "beta1", "bv2", "bo2", "gamma2", "beta2", "bv3", "bo3", "bf2")}
        cols = {n: sb(f"c_{n}", [P, C]) for n in
                ("q_w", "k_w", "fc_b", "bq1", "bk1", "bq2", "bk2", "bq3", "bk3", "g1", "b1", "g2", "b2")}
        bf1 = sb("bf1", [P, F])
        key_w = sb("key_w", [P, C, P])
        query_w = sb("query_w", [P, C])
        qk_b = sb("qk_b", [P, 2])
        qk_const = sb("qk_const", [P, 2])
        ident = sb("ident", [P, P])
        ident_bf = sb("ident_bf", [P, P], BF16)
        ones = sb("ones", [P, P])
        minus_one = sb("minus_one", [1, N], BF16)
        minus_ones = sb("minus_ones", [P, 1])

        q_n = sb("q_n", [P, T])
        slack_q = sb("slack_q", [P, T])
        top = sb("top", [P, T])
        top2 = sb("top2", [P, T])
        neg_top = sb("neg_top", [P, T])
        denom = sb("denom", [P, T])
        rden = sb("rden", [P, T])
        rden2 = sb("rden2", [P, T])
        some = sb("some", [P, T])
        stats = sb("stats", [P, T, 6])
        mean_var = sb("mean_var", [P, T, 2])
        var_eps = sb("var_eps", [P, T])
        minus_half = sb("minus_half", [P, T])
        rstd = sb("rstd", [P, T])

        weights_in = sem("weights_in")
        const_made = sem("const_made")
        ident_made = sem("ident_made")
        setup_mm = sem("setup_mm")
        setup_dve = sem("setup_dve")
        x_loaded = sem("x_loaded")
        mask_loaded = [sem(f"mask_loaded{t}") for t in range(T)]
        lin_done = sem("lin_done")
        act_emptied = sem("act_emptied")
        dve_emptied = sem("dve_emptied")
        dve_step = sem("dve_step")
        pen_ready = sem("pen_ready")
        mask_used = sem("mask_used")
        s_done = sem("s_done")
        s_ready = sem("s_ready")
        slack_done = sem("slack_done")
        leaky_done = sem("leaky_done")
        p_ready = sem("p_ready")
        t_done = sem("t_done")
        t_act = sem("t_act")
        t_dve = sem("t_dve")
        av_done = sem("av_done")
        av_taken = sem("av_taken")
        y_ready = sem("y_ready")
        hi_ready = sem("hi_ready")
        aug_loaded = [sem(f"aug_loaded{h}") for h in range(H)]
        g_ready = sem("g_ready")
        e_ready = sem("e_ready")
        g3_ready = sem("g3_ready")
        nat_done = sem("nat_done")
        max_done = sem("max_done")
        max_cast = sem("max_cast")
        max_row_in = [sem(f"max_row_in{i}") for i in range(2)]
        st_done = sem("st_done")
        exp_done = sem("exp_done")
        masked_dve = sem("masked_dve")
        masked_pool = sem("masked_pool")
        v_ready = sem("v_ready")
        pv_done = sem("pv_done")
        o_out = sem("o_out")
        o_moved = [sem(f"o_moved{i}") for i in range(2)]
        o_normal = sem("o_normal")
        residual = sem("residual")
        passed = sem("passed")
        stats_ready = sem("stats_ready")
        var_ready = sem("var_ready")
        rstd_ready = sem("rstd_ready")
        normal = sem("normal")
        stored = sem("stored")

        per_graph = [(x_loaded, 16), (lin_done, N_LIN), (act_emptied, N_ACT), (dve_emptied, N_DVE),
                     (dve_step, DVE_STEPS), (hi_ready, 8 * C), (nat_done, 2 * H * (T + 1)),
                     (max_done, 2 * H * (T + 1)), (st_done, 2 * H * 2 * T), (exp_done, 2 * H * 2 * T),
                     (masked_dve, 2 * H * len(DVE_TILES)), (masked_pool, 2 * H * len(POOL_TILES)),
                     (pv_done, 2 * H * T), (o_normal, 6), (residual, 3), (stored, 64)]
        per_graph += [(s, 32) for s in mask_loaded] + [(s, AUG_COUNT) for s in aug_loaded]
        per_graph += [(s, 16 * H) for s in max_row_in] + [(s, 64 * H) for s in o_moved]
        per_graph += [(s, T) for s in (pen_ready, mask_used, s_done, slack_done, leaky_done, y_ready, g_ready,
                                       e_ready, g3_ready)]
        per_graph += [(s, 2 * T) for s in (s_ready, p_ready, t_done, t_act, t_dve, av_done, av_taken, normal)]
        per_graph += [(s, 2 * H) for s in (max_cast, v_ready, o_out)]
        per_graph += [(s, NORMS) for s in (stats_ready, var_ready, rstd_ready)]

        def att(b, layer, h, per, c):
            pair, k = h
            return (b * (2 * H) + pair * 2) * per + (layer * H + k) * per + c

        def max_count(b, layer, order):
            head, unit = order
            return att(b, layer, head, T + 1, unit)

        def max_order(head, k):
            return head, k - 1

        def later(order, n=1):
            head, unit = order
            return head, unit + n

        FIRST = (0, 0)

        def ahead(head, n=1):
            pair, k = head
            return pair, k + n

        def rows_moved(b, layer, h, i):
            return att(b, layer, h, 32, -32 * i)

        def max_rows_in(b, layer, h, i):
            return att(b, layer, h, 8, -8 * i)

        def number(head):
            pair, k = head
            return pair * 2 + k

        def wait_lin(eng, b, name, i):
            eng.wait_ge(lin_done, b * N_LIN + PLACE[(name, i)] + 1)

        def wait_emptied(eng, b, name, i):
            na, nd = emptied_before(name, i)
            if UNITS[PLACE[(name, i)]][2] == "A":
                eng.wait_ge(act_emptied, b * N_ACT + na + 1)
            else:
                eng.wait_ge(dve_emptied, b * N_DVE + nd + 1)

        def wait_all_emptied(eng, b, name, n):
            na, nd = emptied_before(name, n - 1)
            last_a = UNITS[PLACE[(name, n - 1)]][2] == "A"
            eng.wait_ge(act_emptied, b * N_ACT + na + last_a)
            eng.wait_ge(dve_emptied, b * N_DVE + nd + (not last_a))

        weight_dmas = []

        block = ctx.enter_context(nc.Block())

        @block.sync
        def _(sp):
            def load(dst, src):
                sp.dma_start(dst, src).then_inc(weights_in, 16)
                weight_dmas.append(1)

            def tiled(name):
                return a[name].rearrange("(c p) n -> p c n", p=P)

            load(fcw, tiled("L0_gnn_fc_w"))
            for key, name in (("fc", "L0_fc_wT"), ("q1", "L1_gnn_Wq"), ("k1", "L1_gnn_Wk"), ("c1", "L1_gnn_Wc"),
                              ("q2", "L2_WqT"), ("k2", "L2_WkT"), ("v2", "L2_WvT"), ("o2", "L2_WoT"),
                              ("q3", "L3_gnn_Wq"), ("k3", "L3_gnn_Wk"), ("v3", "L3_gnn_Wv"), ("o3", "L3_gnn_Wo")):
                load(w[key][:, :, :], tiled(name))
            load(wf1[:, :, :], tiled("L3_gnn_Wf1"))
            load(wf2[:, :, :], tiled("L3_gnn_Wf2"))
            for key, name in (("fc_b", "L0_gnn_fc_b"), ("gamma1", "L1_gnn_gamma"), ("beta1", "L1_gnn_beta"),
                              ("bv2", "L2_gnn_bv"), ("bo2", "L2_gnn_bo"), ("gamma2", "L2_gnn_gamma"),
                              ("beta2", "L2_gnn_beta"), ("bv3", "L3_gnn_bv"), ("bo3", "L3_gnn_bo"),
                              ("bf2", "L3_gnn_bf2")):
                load(rows[key][:, :], a[name].rearrange("(a n) -> a n", a=1).broadcast_to([P, D]))
            for key, name in (("q_w", "L0_gnn_q_w"), ("k_w", "L0_gnn_k_w"), ("fc_b", "L0_gnn_fc_b"), ("bq1", "L1_gnn_bq"), ("bk1", "L1_gnn_bk"),
                              ("bq2", "L2_gnn_bq"), ("bk2", "L2_gnn_bk"), ("bq3", "L3_gnn_bq"),
                              ("bk3", "L3_gnn_bk"), ("g1", "L3_gnn_g1"), ("b1", "L3_gnn_b1"),
                              ("g2", "L3_gnn_g2"), ("b2", "L3_gnn_b2")):
                load(cols[key][:, :], a[name + "_columns"])
            load(bf1[:, :], a["L3_gnn_bf1_columns"])
            load(qk_b[:, 0:1], a["L0_gnn_q_b"].rearrange("(a n) -> a n", a=1).broadcast_to([P, 1]))
            load(qk_b[:, 1:2], a["L0_gnn_k_b"].rearrange("(a n) -> a n", a=1).broadcast_to([P, 1]))

            sp.wait_ge(const_made, CONSTS)

            def load_x(at):
                sp.dma_start(x_in[:, :, :], a["x"][at].rearrange("(t p) d -> p t d", p=P)).then_inc(x_loaded, 16)

            def load_adjacency(at, t):
                sp.dma_start(mask[:, t, :], a["adj"][at, t * P:(t + 1) * P, :]).then_inc(mask_loaded[t], 16)

            def graph(b, last):
                for t in range(T):
                    sp.wait_ge(mask_used, b * T + t + 1)
                    sp.dma_start(mask[:, t, :], a["adj_t"][b - 1, t * P:(t + 1) * P, :]).then_inc(mask_loaded[t], 16)

                for layer in range(2):
                    for g in range(C):
                        for s, aug in enumerate((q_aug, k_aug)):
                            wait_emptied(sp, b, "qk"[s] + "23"[layer] + "." + str(g), 1)
                            high, low = parts[:, 2 * s, g, :], parts[:, 2 * s + 1, g, :]
                            stack = (high, low, high) if s == 0 else (high, high, low)
                            for j in range(4):
                                h = 4 * g + j
                                if layer == 0 and s == 0:
                                    sp.dma_start(k_aug[AUG - 1:AUG, h, :], minus_one[:, :]).then_inc(aug_loaded[h], 16)
                                for r, part in enumerate(stack):
                                    sp.dma_start(aug[r * DK:(r + 1) * DK, h, :],
                                                 part[j * DK:(j + 1) * DK, :]).then_inc(aug_loaded[h], 16)

                    def max_row(h):
                        if h >= 2:
                            sp.wait_ge(max_row_in[h % 2], max_rows_in(b, layer, (0, h), h % 2))
                            sp.sem_inc(passed, 1)
                        sp.wait_ge(max_done, max_count(b, layer, ((0, h + 1), 2 if h < H - 1 else 0)))
                        sp.dma_start(q_aug[AUG - 1:AUG, h, :], max_rows[h % 2][:, :]).then_inc(max_row_in[h % 2], 16)

                    max_row(0)
                    max_row(1)
                    for h in range(H):
                        if h + 2 < H:
                            max_row(h + 2)
                        sp.wait_ge(o_out, att(b, layer, (0, h), 1, 1))
                        r, g = DK * (h % 4), h // 4
                        for c in range(2):
                            cut = slice(c * HALF, (c + 1) * HALF)
                            for dst, at in ((o_t, 2 * DK * c), (sums_t, 2 * DK * c + DK)):
                                sp.dma_start(dst[r:r + DK, g, cut], o_raw[h % 2][at:at + DK, :])\
                                  .then_inc(o_moved[h % 2], 16)
                    if layer == 0 and not last:
                        sp.wait_ge(g3_ready, b * T + T)
                        load_x(b)
                if not last:
                    for t in range(T):
                        load_adjacency(b, t)
                for g in range(4):
                    wait_emptied(sp, b, "ff2", g)
                    sp.dma_start(out[b - 1].rearrange("(t p) d -> p t d", p=P)[:, 2 * g:2 * g + 2, :],
                                 y[:, 2 * g:2 * g + 2, :]).then_inc(stored, 16)

            load_x(0)
            for t in range(T):
                load_adjacency(0, t)
            with sp.Fori(1, B) as b:
                graph(b, False)
            graph(B, True)
            sp.wait_ge(stored, B * 64 + 64)

        @block.tensor
        def _(pe):
            pe.wait_ge(weights_in, 16 * len(weight_dmas))
            for c in range(C):
                for o in range(C):
                    nc.tensor.matmul(ps[:, 0, c:c + 1], fcw[:, o, c * P:(c + 1) * P], cols["k_w"][:, o:o + 1],
                                     start=(o == 0), stop=(o == C - 1))
                for o in range(C):
                    nc.tensor.matmul(ps[:, 1, c:c + 1], fcw[:, o, c * P:(c + 1) * P], cols["q_w"][:, o:o + 1],
                                     start=(o == 0), stop=(o == C - 1))
            pe.wait_ge(setup_dve, 3)
            for i, key in enumerate(("q_w", "k_w")):
                for o in range(C):
                    last = nc.tensor.matmul(ps[:, 2 + i, 0:1], bias_rep[:, o, :], cols[key][:, o:o + 1],
                                            start=(o == 0), stop=(o == C - 1))
            last.then_inc(setup_mm, 1)
            pe.wait_ge(setup_dve, 7)
            pe.wait_ge(const_made, CONSTS)

            def turn(name, i, group):
                bank = free_bank(name, i)
                for j in range(4):
                    t = 4 * (i // 2) + j
                    last = nc.tensor.transpose(ps[:, bank, j * P:(j + 1) * P],
                                               group[:, t, (i % 2) * P:(i % 2 + 1) * P], ident[:, :])
                last.then_inc(lin_done, 1)

            def free_bank(name, i):
                at = PLACE[(name, i)]
                if at < LIN_BANKS:
                    pe.wait_ge(act_emptied, graph[0] * N_ACT)
                    pe.wait_ge(dve_emptied, graph[0] * N_DVE)
                else:
                    wait_emptied(pe, graph[0], *UNITS[at - LIN_BANKS][:2])
                return bank_of(name, i)

            def nodes_by(name, i, lhs, rhs, tiles):
                bank = free_bank(name, i)
                for j in range(2):
                    t = 2 * i + j
                    for c in range(tiles):
                        last = nc.tensor.matmul(ps[:, bank, j * D:(j + 1) * D], lhs(c, t), rhs[:, c, :],
                                                start=(c == 0), stop=(c == tiles - 1))
                last.then_inc(lin_done, 1)

            def features_by(name, i, weight, half, m):
                bank = free_bank(name, i)
                for c in range(C):
                    last = nc.tensor.matmul(ps[:, bank, :], weight[:, c, m * P:(m + 1) * P],
                                            y_t[:, c, half * HALF:(half + 1) * HALF],
                                            start=(c == 0), stop=(c == C - 1))
                last.then_inc(lin_done, 1)

            def output_products(b, layer, name):
                def product(i, j, c):
                    return nc.tensor.matmul(ps[:, bank_of(name, i), j * D:(j + 1) * D], y_tile(c, 2 * i + j),
                                            w[name][:, c, :], start=(c == 0), stop=(c == C - 1))

                pe.wait_ge(o_normal, b * 6 + layer * 3 + 1)
                for i in range(4):
                    free_bank(name, i)
                    product(i, 0, 0)
                for i in range(4):
                    if i % 2 == 0:
                        pe.wait_ge(o_normal, b * 6 + layer * 3 + 2 + i // 2)
                    product(i, 0, 1)
                    product(i, 1, 0)
                    product(i, 1, 1).then_inc(lin_done, 1)

            def y_tile(c, t):
                return y_t[:, c, t * P:(t + 1) * P]

            def attend(b, layer, t):
                base = b * 2 * T + layer * T
                if t < T:
                    pe.wait_ge(p_ready, base + t + 1)
                    pe.wait_ge(t_act, base + t)
                    pe.wait_ge(t_dve, base + t)
                    for k in range(T):
                        last = nc.tensor.transpose(flat[:, 4 * HALF + k * P:4 * HALF + (k + 1) * P],
                                                   scores[:, t % 3, k * P:(k + 1) * P], ident[:, :])
                    last.then_inc(t_done, 1)
                if t > 0:
                    pe.wait_ge(t_act, base + t)
                    pe.wait_ge(t_dve, base + t)
                    if layer or t > 2:
                        pe.wait_ge(av_taken, base + t - 2)
                    for k in range(T):
                        last = nc.tensor.matmul(ps[:, 6 + (t - 1) % 2, 0:D], probs_t[:, (t - 1) % 2, k, :],
                                                values[:, k, :], start=(k == 0), stop=(k == T - 1))
                    last.then_inc(av_done, 1)

            def head(b, layer, h, i, scores_two_ahead, first=False):
                for t in range(T):
                    if t == 2 and scores_two_ahead:
                        rows_of_maxima(b, layer, ahead(h), 1 - i, max_order(ahead(h, 2), 2), (i + 1) % 2)
                    if t == 2 and not scores_two_ahead and i == 0:
                        rows_of_maxima(b, layer, ahead(h), 1 - i, max_order(ahead(h, 2), 0), 1)
                    if scores_two_ahead:
                        k = t if t < 2 else t + 1
                        scores_for_maximum(b, layer, ahead(h, 2), t, max_order(ahead(h, 2), k), (i + k + 1) % 2)
                    if t == 0:
                        pe.wait_ge(max_row_in[i], max_rows_in(b, layer, ahead(h, 2), i))
                    for c in range(2):
                        pe.wait_ge(exp_done, att(b, layer, h, 2 * T, 2 * t + c - 1))
                        nc.tensor.matmul(ps[:, 4 + c, :], k_aug[0:AUG, number(h), t * P:(t + 1) * P],
                                         q_aug[0:AUG, number(h), c * HALF:(c + 1) * HALF],
                                         start=True, stop=True).then_inc(st_done, 1)
                    if t >= LAG:
                        with_values(b, layer, h, i, t - LAG)
                    elif not first:
                        with_values(b, layer, ahead(h, -1), 1 - i, T - LAG + t)

            def scores_for_maximum(b, layer, h, t, order, slot):
                pe.wait_ge(max_done, max_count(b, layer, later(order, -1)))
                for c in range(2):
                    last = nc.tensor.matmul(ps[:, 2 * slot + c, :], q_aug[0:AUG - 1, number(h), t * P:(t + 1) * P],
                                            k_aug[0:AUG - 1, number(h), c * HALF:(c + 1) * HALF], start=True, stop=True)
                last.then_inc(nat_done, 1)

            def rows_of_maxima(b, layer, h, i, order, slot):
                pe.wait_ge(max_done, max_count(b, layer, later(order, -1)))
                pe.wait_ge(max_cast, att(b, layer, h, 1, 1))
                nc.tensor.transpose(ps[0:T, 2 * slot, 0:P // 2].bitcast(BF16), row_max_bf[i][:, :],
                                    ident_bf[:, :]).then_inc(nat_done, 1)

            def with_values(b, layer, h, i, t):
                if t in DVE_TILES:
                    pe.wait_ge(masked_dve, att(b, layer, h, len(DVE_TILES), DVE_TILES.index(t) + 1))
                else:
                    pe.wait_ge(masked_pool, att(b, layer, h, len(POOL_TILES), POOL_TILES.index(t) + 1))
                if t == 0:
                    pe.wait_ge(v_ready, att(b, layer, h, 1, 1))
                    pe.wait_ge(o_out, att(b, layer, h, 1, -1))
                for c in range(2):
                    last = nc.tensor.matmul(ps[64 * c:64 * c + 64, 6 + i, :], v_head[i][:, t, :],
                                            probs[:, t % RING, c * HALF:(c + 1) * HALF],
                                            start=(t == 0), stop=(t == T - 1))
                last.then_inc(pv_done, 1)

            def head_loaded(b, layer, h):
                pe.wait_ge(aug_loaded[h], b * AUG_COUNT + AUG_COUNT - 16 * AUG_DMAS * (1 - layer))

            def heads(b, layer, v):
                head_loaded(b, layer, 0)
                for t in range(T):
                    if t < 2:
                        for c in range(2):
                            last = nc.tensor.matmul(ps[:, 2 * t + c, :], q_aug[0:AUG - 1, 0, t * P:(t + 1) * P],
                                                    k_aug[0:AUG - 1, 0, c * HALF:(c + 1) * HALF], start=True, stop=True)
                        last.then_inc(nat_done, 1)
                    else:
                        scores_for_maximum(b, layer, FIRST, t, (FIRST, t), t % 2)
                    if t % 2:
                        nodes_by(v, t // 2, y_tile, w[v], C)
                head_loaded(b, layer, 1)
                for t in range(T):
                    if t == 2:
                        rows_of_maxima(b, layer, FIRST, 0, max_order(ahead(FIRST), 2), 0)
                    k = t if t < 2 else t + 1
                    scores_for_maximum(b, layer, ahead(FIRST), t, max_order(ahead(FIRST), k), k % 2)
                wait_all_emptied(pe, b, v, 4)
                for h in range(2, H):
                    head_loaded(b, layer, h)
                for h in range(2):
                    head(b, layer, (0, h), h, True, h == 0)
                with pe.Fori(1, H // 2 - 1) as pair:
                    for i in range(2):
                        head(b, layer, (pair, i), i, True)
                for h in range(H - 2, H):
                    head(b, layer, (0, h), h % 2, False)
                for t in range(T - LAG, T):
                    with_values(b, layer, (0, H - 1), 1, t)

            graph = [0]
            with pe.Fori(1, B + 1) as b:
                graph[0] = b
                pe.wait_ge(x_loaded, b * 16 + 16)
                for i in range(4):
                    turn("x_t", i, x_in)
                wait_all_emptied(pe, b, "x_t", 4)
                for i in range(4):
                    nodes_by("proj0", i, y_tile, w["fc"], C)
                for i in range(2):
                    bank = free_bank("key0", i)
                    for c in range(C):
                        last = nc.tensor.matmul(ps[:, bank, :], key_w[:, c, :], y_t[:, c, i * HALF:(i + 1) * HALF],
                                                start=(c == 0), stop=(c == C - 1))
                    last.then_inc(lin_done, 1)
                bank = free_bank("query0", 0)
                for t in range(T):
                    for c in range(C):
                        last = nc.tensor.matmul(ps[:, bank, t:t + 1], y_tile(c, t), query_w[:, c:c + 1],
                                                start=(c == 0), stop=(c == C - 1))
                last.then_inc(lin_done, 1)
                wait_all_emptied(pe, b, "query0", 1)
                for t in range(T + 1):
                    attend(b, 0, t)
                for i in range(4):
                    pe.wait_ge(av_taken, b * 2 * T + (i // 2 + 1) * (T // 2))
                    turn("y1_t", i, y)
                wait_all_emptied(pe, b, "y1_t", 4)
                for name in ("q1", "k1"):
                    for i in range(4):
                        features_by(name, i, w[name], i % 2, i // 2)
                for i in range(4):
                    nodes_by("v1", i, y_tile, w["c1"], C)
                wait_all_emptied(pe, b, "v1", 4)
                for t in range(T + 2):
                    if t < T:
                        if t >= 2:
                            pe.wait_ge(s_ready, b * 2 * T + T + t - 1)
                        for n in range(2):
                            for c in range(C):
                                last = nc.tensor.matmul(ps[:, 2 * (t % 2) + n, :], q_t[:, c, t * P:(t + 1) * P],
                                                        k_t[:, c, n * HALF:(n + 1) * HALF],
                                                        start=(c == 0), stop=(c == C - 1))
                        last.then_inc(s_done, 1)
                    if t > 0:
                        attend(b, 1, t - 1)
                for layer, (group, ready, base) in enumerate(((y, y_ready, b * T), (x_hat, normal, b * 2 * T))):
                    n = "23"[layer]
                    for i in range(4):
                        pe.wait_ge(ready, base + (i // 2 + 1) * (T // 2))
                        turn("y" + n + "_t", i, group)
                    for name in ("q" + n, "k" + n):
                        for half in range(2):
                            wait_emptied(pe, b, "y" + n + "_t", 2 * half)
                            wait_emptied(pe, b, "y" + n + "_t", 2 * half + 1)
                            features_by(name + ".0", half, w[name], half, 0)
                    for name in ("q" + n, "k" + n):
                        for half in range(2):
                            features_by(name + ".1", half, w[name], half, 1)
                    heads(b, layer, "v" + n)
                    output_products(b, layer, "o" + n)
                for i in range(4):
                    pe.wait_ge(normal, b * 2 * T + T + (i // 2 + 1) * (T // 2))
                    turn("h_t", i, x_hat)
                for i in range(2 * F):
                    if i % F == 0:
                        wait_emptied(pe, b, "h_t", 2 * (i // F))
                        wait_emptied(pe, b, "h_t", 2 * (i // F) + 1)
                    features_by("ff1", i, wf1, i // F, i % F)
                for i in range(4):
                    wait_emptied(pe, b, "ff1", (i // 2 + 1) * F - 1)
                    nodes_by("ff2", i, lambda f, t: hidden[f // 4][:, f % 4, t * P:(t + 1) * P], wf2, F)

        @block.scalar
        def _(act):
            def empty_copy(b, name, i, dst):
                wait_lin(act, b, name, i)
                nc.scalar.copy(dst, ps[:, bank_of(name, i), :]).then_inc(act_emptied, 1)

            def empty(b, name, i, dst, func=ACT.Identity, bias=0.0, scale=1.0):
                wait_lin(act, b, name, i)
                nc.scalar.activation(dst, ps[:, bank_of(name, i), :], func, bias=bias,
                                     scale=scale).then_inc(act_emptied, 1)

            def copy_probs(b, layer, t):
                base = b * 2 * T + layer * T
                act.wait_ge(t_done, base + t + 1)
                act.wait_ge(av_done, base + (t - 1 if t >= 2 else 0))
                nc.scalar.copy(probs_t[:, t % 2, 0:4, :].rearrange("p t q -> p (t q)"), ps[:, 4, :]).then_inc(t_act, 1)

            def adjacency_exp(b, t):
                if t >= 2:
                    act.wait_ge(g3_ready, b * T + t - 1)
                nc.scalar.activation(mask_exp[:, t % 2, :], mask[:, t, :], ACT.Exp, bias=minus_ones[:, 0:1],
                                     scale=2.0).then_inc(e_ready, 1)

            def head(b, layer, h, i, first=False, exps=()):
                for t in range(T):
                    for c in range(2):
                        act.wait_ge(st_done, att(b, layer, h, 2 * T, 2 * t + c + 1))
                        if c == 0:
                            act.wait_ge(pv_done, att(b, layer, h, T, t - RING + 1))
                        nc.scalar.activation(probs[:, t % RING, c * HALF:(c + 1) * HALF], ps[:, 4 + c, :], ACT.Exp,
                                             scale=DK ** -0.5).then_inc(exp_done, 1)
                    if t == LAG and not first:
                        take_sums(b, layer, ahead(h, -1), 1 - i)
                    if t in exps:
                        adjacency_exp(b, exps.index(t))

            def take_sums(b, layer, h, i):
                act.wait_ge(pv_done, att(b, layer, h, T, T))
                act.wait_ge(o_moved[i], rows_moved(b, layer, h, i))
                nc.scalar.copy(o_raw[i][:, :], ps[:, 6 + i, :]).then_inc(o_out, 1)

            act.wait_ge(const_made, CONSTS)
            with act.Fori(1, B + 1) as b:
                for half in range(2):
                    empty_copy(b, "x_t", 2 * half, y_t[:, 0, half * HALF:(half + 1) * HALF])
                for i in range(2):
                    empty(b, "key0", i, key_row[:, i * HALF:(i + 1) * HALF], bias=qk_const[:, 1:2])
                for t in range(T + 2):
                    if t < T:
                        act.wait_ge(s_ready, b * 2 * T + t + 1)
                        nc.scalar.activation(slack[:, t % 4, :], scores[:, t % 3, :], ACT.Identity,
                                             bias=slack_q[:, t:t + 1], scale=0.01).then_inc(slack_done, 1)
                    if 0 < t <= T:
                        u = t - 1
                        act.wait_ge(leaky_done, b * T + u + 1)
                        nc.scalar.activation(scores[:, u % 3, :], scores[:, u % 3, :], ACT.Exp,
                                             bias=neg_top[:, u:u + 1], accum_out=denom[:, u:u + 1]).then_inc(p_ready, 1)
                    if t > 1:
                        copy_probs(b, 0, t - 2)
                for half in range(2):
                    empty_copy(b, "y1_t", 2 * half, y_t[:, 0, half * HALF:(half + 1) * HALF])
                for name, dst, bias in (("q1", q_t, "bq1"), ("k1", k_t, "bk1")):
                    for i in range(0, 4, 2):
                        empty(b, name, i, dst[:, i // 2, 0:HALF], bias=cols[bias][:, i // 2:i // 2 + 1])
                for i in range(0, 4, 2):
                    empty_copy(b, "v1", i, values[:, 2 * i:2 * i + 2, :].rearrange("p t d -> p (t d)"))
                for t in range(T + 1):
                    if t < T:
                        act.wait_ge(s_ready, b * 2 * T + T + t + 1)
                        s = scores[:, t % 3, :]
                        nc.scalar.activation(s, s, ACT.Exp, bias=neg_top[:, t:t + 1], scale=D ** -0.5,
                                             accum_out=denom[:, t:t + 1]).then_inc(p_ready, 1)
                    if t > 0:
                        copy_probs(b, 1, t - 1)
                for layer in range(2):
                    n = "23"[layer]
                    for half in range(2):
                        dst = y_t[:, 0, half * HALF:(half + 1) * HALF]
                        if layer == 0:
                            empty_copy(b, "y2_t", 2 * half, dst)
                        else:
                            empty(b, "y3_t", 2 * half, dst, bias=cols["b1"][:, 0:1], scale=cols["g1"][:, 0:1])
                    for u in range(4 * C):
                        g, s, half = u // 4, u // 2 % 2, u % 2
                        name = "qk"[s] + n
                        wait_lin(act, b, f"{name}.{g}", half)
                        nc.scalar.activation(parts[:, 2 * s, g, half * HALF:(half + 1) * HALF],
                                             ps[:, bank_of(f"{name}.{g}", half), :], ACT.Identity,
                                             bias=cols["b" + name][:, g:g + 1]).then_inc(hi_ready, 1)
                    for h in range(2):
                        head(b, layer, (0, h), h, h == 0)
                    with act.Fori(1, H // 2 - 1) as pair:
                        for i in range(2):
                            head(b, layer, (pair, i), i)
                    for h in range(H - 2, H):
                        head(b, layer, (0, h), h % 2, exps=EARLY_EXPS if layer == 0 and h == H - 1 else ())
                    take_sums(b, layer, (0, H - 1), 1)
                    if layer == 0:
                        for t in range(len(EARLY_EXPS), T):
                            adjacency_exp(b, t)
                for half in range(2):
                    empty(b, "h_t", 2 * half, y_t[:, 0, half * HALF:(half + 1) * HALF], bias=cols["b2"][:, 0:1],
                          scale=cols["g2"][:, 0:1])
                for i in range(2 * F):
                    half, f = i // F, i % F
                    empty(b, "ff1", i, hidden[f // 4][:, f % 4, half * HALF:(half + 1) * HALF], ACT.Gelu,
                          bias=bf1[:, f:f + 1])

        @block.vector
        def _(dve):
            graph = [0]
            steps = [0]
            norms = [0]

            def then(ins):
                steps[0] += 1
                ins.then_inc(dve_step, 1)
                dve.wait_ge(dve_step, graph[0] * DVE_STEPS + steps[0])

            def row(name, n):
                return rows[name][:, :].rearrange("p (a d) -> p a d", a=1).broadcast_to([P, n, D])

            def unit(name, i):
                wait_lin(dve, graph[0], name, i)
                return ps[:, bank_of(name, i), :]

            def copy_probs(b, layer, t):
                base = b * 2 * T + layer * T
                dve.wait_ge(t_done, base + t + 1)
                dve.wait_ge(av_done, base + (t - 1 if t >= 2 else 0))
                nc.vector.tensor_copy(probs_t[:, t % 2, 4:8, :].rearrange("p t q -> p (t q)"), ps[:, 5, :])\
                  .then_inc(t_dve, 1)

            def variances(tiles):
                for t in tiles:
                    last = nc.vector.bn_stats(stats[:, t, :], y[:, t, :])
                last.then_inc(stats_ready, 1)
                norms[0] += 1
                dve.wait_ge(stats_ready, graph[0] * NORMS + norms[0])
                dve.sem_inc(passed, 1)
                for t in tiles:
                    last = nc.vector.bn_aggr(mean_var[:, t, :], stats[:, t, :])
                then(last)
                nc.vector.tensor_scalar(var_eps[:, tiles[0]:tiles[-1] + 1], mean_var[:, tiles[0]:tiles[-1] + 1, 1],
                                        EPS, None, ALU.add).then_inc(var_ready, 1)

            def normalize(tiles, dst, behind, signal=None):
                dve.wait_ge(rstd_ready, graph[0] * NORMS + norms[0] - behind + 1)
                for t in tiles:
                    last = nc.vector.tensor_scalar(dst[:, t, :], y[:, t, :], mean_var[:, t, 0:1], rstd[:, t:t + 1],
                                                   ALU.subtract, ALU.mult)
                    if signal is not None:
                        last.then_inc(signal, 1)
                if signal is None:
                    then(last)

            def heads_moved(b, layer, g):
                for i in range(2):
                    dve.wait_ge(o_moved[i], rows_moved(b, layer, (0, 4 * g + 4 + i), i))

            def invert_sums(g, cut):
                return nc.vector.reciprocal(sums_t[:, g, cut], sums_t[:, g, cut])

            def divide(g, cut):
                nc.vector.tensor_tensor(o_t[:, g, cut], o_t[:, g, cut], sums_t[:, g, cut], ALU.mult)\
                  .then_inc(o_normal, 1)

            def make_mask3(b, t):
                dve.wait_ge(e_ready, b * T + t + 1)
                if t in DVE_TILES:
                    dve.wait_ge(masked_dve, att(b, 0, (0, H - 1), len(DVE_TILES), DVE_TILES.index(t) + 1))
                else:
                    dve.wait_ge(masked_pool, att(b, 0, (0, H - 1), len(POOL_TILES), POOL_TILES.index(t) + 1))
                nc.vector.scalar_tensor_tensor(mask[:, t, :], mask[:, t, :], 1.0 / 3.0, mask_exp[:, t % 2, :],
                                               ALU.add, ALU.mult).then_inc(g3_ready, 1)

            def head(b, layer, h, i, maxima_two_ahead, spare=None):
                for t in range(T):
                    if t == 2 and (maxima_two_ahead or i == 0):
                        take_rows(b, layer, ahead(h), 1 - i, max_order(ahead(h, 2), 2 if maxima_two_ahead else 0),
                                  (i + 1) % 2)
                    if maxima_two_ahead:
                        k = t if t < 2 else t + 1
                        maximum(b, layer, i, t, max_order(ahead(h, 2), k), (i + k + 1) % 2)
                    if t in DVE_TILES:
                        dve.wait_ge(exp_done, att(b, layer, h, 2 * T, 2 * t + 2))
                        p = probs[:, t % RING, :]
                        nc.vector.tensor_tensor(p, p, mask[:, t, :], ALU.mult).then_inc(masked_dve, 1)
                    if spare is not None:
                        spare(t)
                if maxima_two_ahead:
                    cast_maxima(b, layer, i, max_order(ahead(h, 2), T))

            def maximum(b, layer, i, t, order, slot):
                dve.wait_ge(nat_done, max_count(b, layer, later(order)))
                nc.vector.tensor_reduce(row_max[i][:, t:t + 1], flat[:, slot * N:(slot + 1) * N], AX.X, ALU.max)\
                  .then_inc(max_done, 1)

            def cast_maxima(b, layer, i, last_order):
                dve.wait_ge(max_done, max_count(b, layer, later(last_order)))
                nc.vector.tensor_copy(row_max_bf[i][:, :], row_max[i][:, :]).then_inc(max_cast, 1)

            def take_rows(b, layer, h, i, order, slot):
                dve.wait_ge(nat_done, max_count(b, layer, later(order)))
                dve.wait_ge(max_row_in[i], max_rows_in(b, layer, h, i))
                nc.vector.tensor_copy(max_rows[i][:, :], ps[0:T, 2 * slot, 0:P // 2].bitcast(BF16))\
                  .then_inc(max_done, 1)

            nc.vector.memset(ones[:, :], 1.0).then_inc(setup_dve, 1)
            nc.vector.memset(minus_one[:, :], -1.0).then_inc(const_made, 1)
            for i in range(2):
                last = nc.vector.memset(v_head[i][:, :, :], 1.0)
            last.then_inc(const_made, 1)
            nc.vector.memset(minus_ones[:, :], -1.0).then_inc(const_made, 1)
            nc.vector.memset(minus_half[:, :], -0.5).then_inc(const_made, 1)
            dve.wait_ge(setup_dve, 1)
            dve.wait_ge(weights_in, 16 * len(weight_dmas))
            for c in range(C):
                nc.vector.tensor_scalar(bias_rep[:, c, :], ones[:, :], cols["fc_b"][:, c:c + 1], None, ALU.mult)\
                  .then_inc(setup_dve, 1)
            dve.wait_ge(setup_mm, 1)
            for c in range(C):
                nc.vector.tensor_scalar(key_w[:, c, :], ones[:, :], ps[:, 0, c:c + 1], None, ALU.mult)\
                  .then_inc(setup_dve, 1)
            nc.vector.tensor_copy(query_w[:, :], ps[:, 1, 0:C]).then_inc(setup_dve, 1)
            for i in range(2):
                last = nc.vector.tensor_tensor(qk_const[:, i:i + 1], ps[:, 2 + i, 0:1], qk_b[:, i:i + 1], ALU.add)
            last.then_inc(setup_dve, 1)
            dve.wait_ge(const_made, CONSTS)

            with dve.Fori(1, B + 1) as b:
                graph[0] = b
                for half in range(2):
                    nc.vector.tensor_copy(y_t[:, 1, half * HALF:(half + 1) * HALF], unit("x_t", 2 * half + 1))\
                      .then_inc(dve_emptied, 1)
                for i in range(4):
                    nc.vector.tensor_tensor(values[:, 2 * i:2 * i + 2, :],
                                            unit("proj0", i).rearrange("p (t d) -> p t d", t=2),
                                            row("fc_b", 2), ALU.add).then_inc(dve_emptied, 1)
                nc.vector.tensor_scalar(q_n[:, :], unit("query0", 0)[:, 0:T], qk_const[:, 0:1], None, ALU.add)\
                  .then_inc(dve_emptied, 1)
                wait_all_emptied(dve, b, "query0", 1)
                then(nc.vector.tensor_scalar(slack_q[:, :], q_n[:, :], 0.01, None, ALU.mult))
                for t in range(T + 3):
                    if t < T:
                        s = scores[:, t % 3, :]
                        dve.wait_ge(pen_ready, b * T + t + 1)
                        dve.sem_inc(passed, 1)
                        then(nc.vector.tensor_tensor_reduce(s, s, key_row, 1.0, LOWEST, ALU.add, ALU.max,
                                                            top[:, t:t + 1]))
                        then(nc.vector.tensor_scalar(top2[:, t:t + 1], top[:, t:t + 1], q_n[:, t:t + 1], None, ALU.add))
                        then(nc.vector.scalar_tensor_tensor(top[:, t:t + 1], top2[:, t:t + 1], 0.01, top2[:, t:t + 1],
                                                            ALU.mult, ALU.max))
                        nc.vector.tensor_scalar(neg_top[:, t:t + 1], top[:, t:t + 1], -1.0, None, ALU.mult)\
                          .then_inc(s_ready, 1)
                    if 0 < t <= T:
                        u = t - 1
                        s = scores[:, u % 3, :]
                        dve.wait_ge(slack_done, b * T + u + 1)
                        nc.vector.scalar_tensor_tensor(s, s, q_n[:, u:u + 1], slack[:, u % 4, :], ALU.add, ALU.max)\
                          .then_inc(leaky_done, 1)
                    if 1 < t <= T + 1:
                        copy_probs(b, 0, t - 2)
                    if t > 2:
                        u = t - 3
                        then(nc.vector.reciprocal(rden[:, u:u + 1], denom[:, u:u + 1]))
                        dve.wait_ge(av_done, b * 2 * T + u + 1)
                        if u == 0:
                            dve.wait_ge(stored, b * 64)
                        nc.vector.scalar_tensor_tensor(y[:, u, :], ps[:, 6 + u % 2, 0:D], rden[:, u:u + 1],
                                                       x_in[:, u, :], ALU.mult, ALU.add).then_inc(av_taken, 1)
                for half in range(2):
                    nc.vector.tensor_copy(y_t[:, 1, half * HALF:(half + 1) * HALF], unit("y1_t", 2 * half + 1))\
                      .then_inc(dve_emptied, 1)
                for name, dst, bias in (("q1", q_t, "bq1"), ("k1", k_t, "bk1")):
                    for i in (1, 3):
                        nc.vector.tensor_scalar(dst[:, i // 2, HALF:N], unit(name, i), cols[bias][:, i // 2:i // 2 + 1],
                                                None, ALU.add).then_inc(dve_emptied, 1)
                for i in (1, 3):
                    nc.vector.tensor_copy(values[:, 2 * i:2 * i + 2, :].rearrange("p t d -> p (t d)"), unit("v1", i))\
                      .then_inc(dve_emptied, 1)
                for t in range(T + 3):
                    if t < T:
                        s = scores[:, t % 3, :]
                        if t >= 3:
                            dve.wait_ge(t_done, b * 2 * T + T + t - 2)
                        nc.vector.tensor_scalar(s, mask[:, t, :], 0.0, -1e18 * D ** 0.5, ALU.is_equal, ALU.mult)\
                          .then_inc(mask_used, 1)
                        dve.wait_ge(mask_used, b * T + t + 1)
                        dve.wait_ge(s_done, b * T + t + 1)
                        dve.sem_inc(passed, 1)
                        then(nc.vector.tensor_tensor_reduce(s, flat[:, (t % 2) * N:(t % 2 + 1) * N], s, 1.0, LOWEST,
                                                            ALU.add, ALU.max, top[:, t:t + 1]))
                        nc.vector.tensor_scalar(some[:, t:t + 1], top[:, t:t + 1], -0.5e18 * D ** 0.5, None, ALU.is_gt)
                        nc.vector.tensor_scalar(neg_top[:, t:t + 1], top[:, t:t + 1], -(D ** -0.5), None, ALU.mult)\
                          .then_inc(s_ready, 1)
                    if 0 < t <= T:
                        copy_probs(b, 1, t - 1)
                    if 1 < t <= T + 1:
                        u = t - 2
                        dve.wait_ge(av_done, b * 2 * T + T + u + 1)
                        then(nc.vector.reciprocal(rden[:, u:u + 1], denom[:, u:u + 1]))
                        then(nc.vector.tensor_tensor(rden2[:, u:u + 1], rden[:, u:u + 1], some[:, u:u + 1], ALU.mult))
                        nc.vector.scalar_tensor_tensor(y[:, u, :], ps[:, 6 + u % 2, 0:D], rden2[:, u:u + 1],
                                                       y[:, u, :], ALU.mult, ALU.add).then_inc(av_taken, 1)
                        dve.wait_ge(av_taken, b * 2 * T + T + u + 1)
                        variances(range(u, u + 1))
                    if t > 2:
                        u = t - 3
                        normalize(range(u, u + 1), y, 2 if u < T - 1 else 1)
                        then(nc.vector.tensor_tensor(y[:, u, :], y[:, u, :], rows["gamma1"][:, :], ALU.mult))
                        nc.vector.tensor_tensor(y[:, u, :], y[:, u, :], rows["beta1"][:, :], ALU.add).then_inc(y_ready, 1)
                for layer in range(2):
                    n = "23"[layer]
                    for half in range(2):
                        dst = y_t[:, 1, half * HALF:(half + 1) * HALF]
                        if layer == 0:
                            nc.vector.tensor_copy(dst, unit("y2_t", 2 * half + 1)).then_inc(dve_emptied, 1)
                        else:
                            nc.vector.tensor_scalar(dst, unit("y3_t", 2 * half + 1), cols["g1"][:, 1:2],
                                                    cols["b1"][:, 1:2], ALU.mult, ALU.add).then_inc(dve_emptied, 1)
                    for u in range(4 * C):
                        g, s, half = u // 4, u // 2 % 2, u % 2
                        name = "qk"[s] + n
                        cut = slice(half * HALF, (half + 1) * HALF)
                        dve.wait_ge(hi_ready, b * 8 * C + layer * 4 * C + u + 1)
                        nc.vector.scalar_tensor_tensor(parts[:, 2 * s + 1, g, cut], unit(f"{name}.{g}", half),
                                                       cols["b" + name][:, g:g + 1], parts[:, 2 * s, g, cut],
                                                       ALU.add, ALU.subtract).then_inc(dve_emptied, 1)
                        t = u
                        if layer == 0:
                            dve.wait_ge(mask_loaded[t], b * 32 + 32)
                            nc.vector.tensor_scalar(mask[:, t, :], mask[:, t, :], 1e-8, None, ALU.max)\
                              .then_inc(g_ready, 1)
                    for t in range(T):
                        maximum(b, layer, 0, t, (FIRST, t), t % 2)
                        if t % 2:
                            i = t // 2
                            nc.vector.tensor_tensor(values[:, 2 * i:2 * i + 2, :],
                                                    unit("v" + n, i).rearrange("p (t d) -> p t d", t=2),
                                                    row("bv" + n, 2), ALU.add).then_inc(dve_emptied, 1)
                    cast_maxima(b, layer, 0, (FIRST, T - 1))
                    dve.wait_ge((g_ready, g3_ready)[layer], b * T + T)
                    for t in range(T):
                        if t == 2:
                            take_rows(b, layer, FIRST, 0, max_order(ahead(FIRST), 2), 0)
                        k = t if t < 2 else t + 1
                        maximum(b, layer, 1, t, max_order(ahead(FIRST), k), k % 2)
                    cast_maxima(b, layer, 1, max_order(ahead(FIRST), T))
                    for h in range(2):
                        head(b, layer, (0, h), h, True)
                    with dve.Fori(1, H // 2 - 1) as pair:
                        for i in range(2):
                            head(b, layer, (pair, i), i, True)

                    def invert_quarter(t):
                        if t % 2:
                            quarter = invert_sums(0, slice(t // 2 * D, (t // 2 + 1) * D))
                            if t == T - 1:
                                then(quarter)

                    def make_early_mask(t):
                        if t in EARLY_MASKS:
                            make_mask3(b, EARLY_MASKS.index(t))

                    heads_moved(b, layer, 0)
                    head(b, layer, (0, H - 2), 0, False, invert_quarter)
                    divide(0, slice(0, N))
                    head(b, layer, (0, H - 1), 1, False, make_early_mask if layer == 0 else None)
                    if layer == 0:
                        for t in (4, 5):
                            make_mask3(b, t)
                    heads_moved(b, layer, 1)
                    for half in range(2):
                        cut = slice(half * HALF, (half + 1) * HALF)
                        then(invert_sums(1, cut))
                        divide(1, cut)
                    if layer == 0:
                        for t in (6, 7):
                            make_mask3(b, t)
                    dve.wait_ge(residual, b * 3 + layer + 1)
                    halves = (range(T // 2), range(T // 2, T))
                    for half in range(2):
                        for i in (2 * half, 2 * half + 1):
                            nc.vector.tensor_tensor(y[:, 2 * i:2 * i + 2, :],
                                                    unit("o" + n, i).rearrange("p (t d) -> p t d", t=2),
                                                    y[:, 2 * i:2 * i + 2, :], ALU.add).then_inc(dve_emptied, 1)
                        wait_emptied(dve, b, "o" + n, 2 * half + 1)
                        variances(halves[half])
                    if layer == 0:
                        for tiles in halves:
                            normalize(tiles, y, 2)
                            part = y[:, tiles[0]:tiles[-1] + 1, :]
                            then(nc.vector.tensor_tensor(part, part, row("gamma2", T // 2), ALU.mult))
                            then(nc.vector.tensor_tensor(part, part, row("beta2", T // 2), ALU.add))
                            variances(tiles)
                    for half, tiles in enumerate(halves):
                        normalize(tiles, x_hat, 2 - half, normal)
                for half in range(2):
                    nc.vector.tensor_scalar(y_t[:, 1, half * HALF:(half + 1) * HALF], unit("h_t", 2 * half + 1),
                                            cols["g2"][:, 1:2], cols["b2"][:, 1:2], ALU.mult, ALU.add)\
                      .then_inc(dve_emptied, 1)
                dve.wait_ge(residual, b * 3 + 3)
                for i in range(4):
                    nc.vector.tensor_tensor(y[:, 2 * i:2 * i + 2, :], unit("ff2", i).rearrange("p (t d) -> p t d", t=2),
                                            y[:, 2 * i:2 * i + 2, :], ALU.add).then_inc(dve_emptied, 1)
            assert steps[0] == DVE_STEPS, steps[0]

        @block.gpsimd
        def _(pool):
            for s, per in per_graph:
                pool.sem_inc(s, per)
            nc.gpsimd.memset(ident[:, :], 0.0).then_inc(ident_made, 1)
            nc.gpsimd.memset(ident_bf[:, :], 0.0).then_inc(ident_made, 1)
            pool.wait_ge(ident_made, 2)
            for m in (ident, ident_bf):
                nc.gpsimd.affine_select(out=m[:, :], in_=m[:, :], compare_op=ALU.not_equal, fill=1.0, base=0,
                                        pattern=[[-1, P]], channel_multiplier=1).then_inc(const_made, 1)

            def copy_values(b, layer, h, i):
                pool.wait_ge(pv_done, att(b, layer, h, T, -T))
                pool.sem_inc(passed, 1)
                nc.gpsimd.tensor_copy(v_head[i][:, :, 0:DK], values[:, :, bass.ds(number(h) * DK, DK)]).then_inc(v_ready, 1)

            def head(b, layer, h, i, last=False):
                for t in POOL_TILES:
                    pool.wait_ge(exp_done, att(b, layer, h, 2 * T, 2 * t + 2))
                    p = probs[:, t % RING, :]
                    nc.gpsimd.tensor_tensor(p, p, mask[:, t, :], ALU.mult).then_inc(masked_pool, 1)
                    if t == POOL_TILES[1] and not last:
                        copy_values(b, layer, ahead(h), 1 - i)

            pool.wait_ge(const_made, CONSTS)
            norms = [0]

            def inverse_deviation(b, tiles):
                norms[0] += 1
                pool.wait_ge(var_ready, b * NORMS + norms[0])
                cut = slice(tiles[0], tiles[-1] + 1)
                nc.gpsimd.tensor_tensor(rstd[:, cut], var_eps[:, cut], minus_half[:, cut], ALU.pow)\
                  .then_inc(rstd_ready, 1)

            with pool.Fori(1, B + 1) as b:
                for t in range(T):
                    pool.wait_ge(mask_loaded[t], b * 32 + 16)
                    if t >= 3:
                        pool.wait_ge(t_done, b * 2 * T + t - 2)
                    elif t == 0:
                        pool.wait_ge(dve_emptied, b * N_DVE)
                    pool.sem_inc(passed, 1)
                    nc.gpsimd.tensor_scalar(scores[:, t % 3, :], mask[:, t, :], -1.0, 1e9, ALU.add, ALU.mult)\
                      .then_inc(pen_ready, 1)
                for t in range(T):
                    inverse_deviation(b, range(t, t + 1))
                for layer in range(2):
                    wait_all_emptied(pool, b, ("v2", "v3")[layer], 4)
                    copy_values(b, layer, FIRST, 0)
                    nc.gpsimd.tensor_tensor(y[:, :, :], y[:, :, :],
                                            rows[("bo2", "bo3")[layer]][:, :].rearrange("p (a d) -> p a d", a=1)
                                            .broadcast_to([P, T, D]), ALU.add).then_inc(residual, 1)
                    if layer == 0:
                        pool.wait_ge(g_ready, b * T + T)
                    for h in range(2):
                        head(b, layer, (0, h), h)
                    with pool.Fori(1, H // 2 - 1) as pair:
                        for i in range(2):
                            head(b, layer, (pair, i), i)
                    for h in range(H - 2, H):
                        head(b, layer, (0, h), h % 2, h == H - 1)
                    for _ in range(2 - layer):
                        inverse_deviation(b, range(T // 2))
                        inverse_deviation(b, range(T // 2, T))
                pool.wait_ge(normal, b * 2 * T + 2 * T)
                nc.gpsimd.tensor_tensor(y[:, :, :], y[:, :, :],
                                        rows["bf2"][:, :].rearrange("p (a d) -> p a d", a=1)
                                        .broadcast_to([P, T, D]), ALU.add).then_inc(residual, 1)


LAYOUTS = {"L0_fc_wT": "L0_gnn_fc_w", "L2_WqT": "L2_gnn_Wq", "L2_WkT": "L2_gnn_Wk", "L2_WvT": "L2_gnn_Wv",
           "L2_WoT": "L2_gnn_Wo"}

COLUMNS = ("L0_gnn_q_w", "L0_gnn_k_w", "L0_gnn_fc_b", "L1_gnn_bq", "L1_gnn_bk", "L2_gnn_bq", "L2_gnn_bk",
           "L3_gnn_bq", "L3_gnn_bk", "L3_gnn_g1", "L3_gnn_b1", "L3_gnn_g2", "L3_gnn_b2", "L3_gnn_bf1")
UNUSED = ("L2_gnn_Wq", "L2_gnn_Wk", "L2_gnn_Wv", "L2_gnn_Wo", *(n for n in COLUMNS if n != "L0_gnn_fc_b"))


def kernel(**inputs):
    import numpy as np
    import concourse.bacc as bacc
    from concourse.bass_utils import run_bass_kernel_spmd

    arrays = {name: np.ascontiguousarray(x) for name, x in inputs.items()}
    for name, source in LAYOUTS.items():
        arrays[name] = np.ascontiguousarray(np.asarray(inputs[source]).T)
    arrays["adj_t"] = np.ascontiguousarray(np.asarray(inputs["adj"]).transpose(0, 2, 1))
    for name in COLUMNS:
        arrays[name + "_columns"] = np.ascontiguousarray(np.asarray(inputs[name]).reshape(-1, P).T)
    for unused in UNUSED:
        del arrays[unused]
    nc = bacc.Bacc("TRN2", target_bir_lowering=False, num_devices=1)
    aps = {name: nc.dram_tensor(f"in_{name}", x.shape, mybir.dt.from_np(x.dtype), kind="ExternalInput").ap()
           for name, x in arrays.items()}
    shape = arrays["x"].shape
    result = nc.dram_tensor("result", shape, F32, kind="ExternalOutput").ap()
    build(nc, aps, result)
    r = run_bass_kernel_spmd(nc, [{f"in_{name}": x for name, x in arrays.items()}], core_ids=[0])
    return r.results[0]["result"]
```

```python
from contextlib import ExitStack

import concourse.bass as bass
from concourse import mybir

F32 = mybir.dt.float32
BF16 = mybir.dt.bfloat16
ACT = mybir.ActivationFunctionType
ALU = mybir.AluOpType
AX = mybir.AxisListType

P = 128
N = 1024
D = 256
T = N // P
C = D // P
HALF = 512
H = 8
DK = D // H
FF = 4 * D
F = FF // P
AUG = 3 * DK + 1
LAG = 3
RING = 4
POOL_TILES = (1, 3, 5, 7)
DVE_TILES = tuple(t for t in range(T) if t not in POOL_TILES)
EARLY_EXPS = (1, 2, 5, 6)
EARLY_MASKS = (3, 4, 6, 7)
EPS = 1e-5
AUG_DMAS = 6
AUG_COUNT = 16 * 2 * AUG_DMAS
LOWEST = -3.0e38

LINEAR = [
    ("y1_t", range(4), "AD"), ("q1", range(4), "AD"), ("k1", range(4), "AD"), ("v1", range(4), "AD"),
    ("y2_t", range(2), "AD"), ("q2.0", range(1), "D"), ("k2.0", range(1), "D"),
    ("y2_t", range(2, 4), "AD"), ("q2.0", range(1, 2), "D"), ("k2.0", range(1, 2), "D"),
    ("q2.1", range(2), "D"), ("k2.1", range(2), "D"), ("v2", range(4), "A"),
    ("x_t", range(4), "A"), ("key0", range(2), "A"), ("o2", range(4), "D"), ("proj0", range(8), "A"),
    ("y3_t", range(2), "AD"), ("q3.0", range(1), "D"), ("k3.0", range(1), "D"),
    ("y3_t", range(2, 4), "AD"), ("q3.0", range(1, 2), "D"), ("k3.0", range(1, 2), "D"),
    ("q3.1", range(2), "D"), ("k3.1", range(2), "D"), ("v3", range(4), "A"), ("o3", range(4), "D"),
    ("h_t", range(2), "AD"), ("ff1", range(8), "A"), ("h_t", range(2, 4), "AD"), ("ff1", range(8, 16), "A"),
]
PART_UNITS = [(0, 0, 0), (0, 1, 0), (0, 0, 1), (0, 1, 1), (1, 0, 0), (1, 0, 1), (1, 1, 0), (1, 1, 1)]
UPPER = ("proj0", "q2.1", "k2.1", "v2", "q3.1", "k3.1", "v3")
UNITS = [(name, i, owners[i % len(owners)]) for name, units, owners in LINEAR for i in units]
PLACE = {(name, i): at for at, (name, i, _) in enumerate(UNITS)}
N_LIN = len(UNITS)
N_ACT = sum(o == "A" for _, _, o in UNITS)
N_DVE = N_LIN - N_ACT
LIN_BANKS = 4


def bank_of(name, i):
    return PLACE[(name, i)] % LIN_BANKS + (LIN_BANKS if name in UPPER else 0)


CONSTS = 8
NORM_ORDER = [(0, 0, 0), (0, 1, 0), (0, 2, 0), (0, 0, 1), (0, 1, 1), (0, 3, 0), (0, 2, 1), (0, 3, 1),
              *((1, i, 1) for i in range(4))]
SCALED_AFTER = {(1, 0): 0, (2, 0): 1, (0, 1): 2, (2, 1): 3}
NORMS = T + len(NORM_ORDER)
DVE_STEPS = 95
DVE_STEPS_START = 10
START = 3


def emptied_before(name, i):
    at = PLACE[(name, i)]
    a = sum(o == "A" for _, _, o in UNITS[:at])
    return a, at - a


def build(nc, a, out):
    B = out.shape[0]
    with ExitStack() as ctx:
        def sb(name, shape, dt=F32):
            return ctx.enter_context(nc.sbuf_tensor(name, shape, dt))

        def sem(name):
            return ctx.enter_context(nc.semaphore(name))

        ps = ctx.enter_context(nc.psum_tensor("ps", [P, 8, HALF], F32))
        flat = ps[:, :, :].rearrange("p b n -> p (b n)")

        x_in = sb("x_in", [P, T, D])
        y = sb("y", [P, T, D])
        y_t = sb("y_t", [P, C, N])
        o_t = y_t
        values = sb("values", [P, T, D])
        x_hat = values
        mask = sb("mask", [P, T, N])
        sums_t = sb("sums_t", [P, C, N])
        region_q = sb("region_q", [P, 4096])
        region_k = sb("region_k", [P, 4096])
        region_p = sb("region_p", [P, 4096])
        q_aug = region_q[:, :].bitcast(BF16).rearrange("p (h n) -> p h n", h=H)
        k_aug = region_k[:, :].bitcast(BF16).rearrange("p (h n) -> p h n", h=H)
        probs = region_p[:, :].rearrange("p (r n) -> p r n", r=RING)
        parts = [region_p[:, 0:2 * N].bitcast(BF16).rearrange("p (s n) -> p s n", s=4),
                 sums_t[:, :, :].rearrange("p c n -> p (c n)").bitcast(BF16).rearrange("p (s n) -> p s n", s=4)]
        mask_exp = sb("mask_exp", [P, 2, N])
        values0 = sb("values0", [P, T, D])
        key_row = sb("key_row", [P, N])
        q_t = region_q[:, 0:C * N].rearrange("p (c n) -> p c n", c=C)
        k_t = region_q[:, C * N:2 * C * N].rearrange("p (c n) -> p c n", c=C)
        scores = region_p[:, 0:3 * N].rearrange("p (r n) -> p r n", r=3)
        x_t = region_q[:, 0:C * N].rearrange("p (c n) -> p c n", c=C)
        slack = sums_t
        probs_t = region_k[:, 0:2 * N].rearrange("p (r t q) -> p r t q", r=2, t=T)
        hidden = [region_q[:, :].rearrange("p (f n) -> p f n", f=4),
                  region_k[:, :].rearrange("p (f n) -> p f n", f=4)]
        fcw = region_q[:, 0:C * D].rearrange("p (c n) -> p c n", c=C)
        bias_rep = region_q[:, 1024:1024 + 3 * C * P].rearrange("p (s c n) -> p s c n", s=3, c=C)

        v_head = [sb(f"v_head{i}", [P, T, 2 * DK]) for i in range(2)]
        o_raw = [sb(f"o_raw{i}", [P, HALF]) for i in range(2)]
        row_max = [sb(f"row_max{i}", [P, T]) for i in range(2)]
        row_max_bf = [sb(f"row_max_bf{i}", [P, T], BF16) for i in range(2)]
        max_rows = [sb(f"max_rows{i}", [T, P], BF16) for i in range(2)]

        w = {n: sb(f"w_{n}", [P, C, D + (n == "fc")]) for n in
             ("fc", "q1", "k1", "c1", "q2", "k2", "v2", "o2", "q3", "k3", "v3", "o3")}
        wf1 = sb("wf1", [P, C, FF])
        wf2 = sb("wf2", [P, F, D])
        rows = {n: sb(f"r_{n}", [P, D]) for n in
                ("fc_b", "gamma1", "beta1", "bo2", "gamma2", "beta2", "bo3", "bf2")}
        cols = {n: sb(f"c_{n}", [P, C]) for n in
                ("q_w", "k_w", "fc_b", "bq1", "bk1", "bq2", "bk2", "bv2", "bq3", "bk3", "bv3", "g1", "b1", "g2", "b2")}
        bf1 = sb("bf1", [P, F])
        key_w = sb("key_w", [P, C, P])
        query_w = w["fc"][:, :, D]
        qk_b = sb("qk_b", [P, 2])
        qk_const = sb("qk_const", [P, 2])
        ident = sb("ident", [P, P])
        ident_bf = sb("ident_bf", [P, P], BF16)
        ones = sb("ones", [P, P])
        minus_one = sb("minus_one", [H, N], BF16)
        minus_ones = sb("minus_ones", [P, 1])

        q_n = sb("q_n", [P, T])
        slack_q = sb("slack_q", [P, T])
        top = sb("top", [P, T])
        top2 = sb("top2", [P, T])
        neg_top = sb("neg_top", [P, T])
        denom = sb("denom", [P, T])
        rden = sb("rden", [P, T])
        rden2 = sb("rden2", [P, T])
        some = sb("some", [P, T])
        stats = sb("stats", [P, T, 6])
        mean_var = sb("mean_var", [P, T, 2])
        var_eps = sb("var_eps", [P, T])
        minus_half = sb("minus_half", [P, T])
        rstd = sb("rstd", [P, T])
        neg_mean = sb("neg_mean", [P, T])
        shift = sb("shift", [P, T])

        setup_in = sem("setup_in")
        weights_in = sem("weights_in")
        const_made = sem("const_made")
        ident_made = sem("ident_made")
        setup_mm = sem("setup_mm")
        setup_dve = sem("setup_dve")
        x_loaded = sem("x_loaded")
        x_biased = sem("x_biased")
        mask_loaded = [sem(f"mask_loaded{t}") for t in range(T)]
        lin_done = sem("lin_done")
        act_emptied = sem("act_emptied")
        dve_emptied = sem("dve_emptied")
        dve_step = sem("dve_step")
        pen_ready = sem("pen_ready")
        mask_used = sem("mask_used")
        s_done = sem("s_done")
        s_ready = sem("s_ready")
        slack_done = sem("slack_done")
        leaky_done = sem("leaky_done")
        p_ready = sem("p_ready")
        t_done = sem("t_done")
        t_act = sem("t_act")
        t_dve = sem("t_dve")
        av_done = sem("av_done")
        av_taken = sem("av_taken")
        y_ready = sem("y_ready")
        hi_ready = sem("hi_ready")
        aug_loaded = [sem(f"aug_loaded{h}") for h in range(H)]
        ones_loaded = sem("ones_loaded")
        g_ready = sem("g_ready")
        e_ready = sem("e_ready")
        g3_ready = sem("g3_ready")
        nat_done = sem("nat_done")
        max_done = sem("max_done")
        max_cast = sem("max_cast")
        rows_done = sem("rows_done")
        rows_taken = sem("rows_taken")
        max_row_in = [sem(f"max_row_in{i}") for i in range(2)]
        st_done = sem("st_done")
        exp_done = sem("exp_done")
        masked_dve = sem("masked_dve")
        masked_pool = sem("masked_pool")
        v_ready = sem("v_ready")
        pv_done = sem("pv_done")
        o_out = sem("o_out")
        o_moved = [sem(f"o_moved{i}") for i in range(2)]
        inverted = sem("inverted")
        o_normal = sem("o_normal")
        residual = sem("residual")
        passed = sem("passed")
        stats_ready = sem("stats_ready")
        var_ready = sem("var_ready")
        rstd_ready = sem("rstd_ready")
        power_done = sem("power_done")
        normal_y = sem("normal_y")
        scaled = sem("scaled")
        shifted = sem("shifted")
        normal = sem("normal")
        ff2_done = sem("ff2_done")
        ff2_emptied = sem("ff2_emptied")
        stored = sem("stored")

        per_graph = [(x_loaded, 16), (ones_loaded, 16), (lin_done, PLACE[("x_t", 0)]),
                     (act_emptied, emptied_before("x_t", 0)[0]), (x_biased, 1), (dve_emptied, N_DVE),
                     (dve_step, DVE_STEPS - DVE_STEPS_START), (hi_ready, 8 * C), (nat_done, 2 * H * T),
                     (max_done, 2 * H * T), (st_done, 2 * H * 2 * T), (exp_done, 2 * H * 2 * T),
                     (masked_dve, 2 * H * len(DVE_TILES)), (masked_pool, 2 * H * len(POOL_TILES)),
                     (pv_done, 2 * H * T), (o_normal, 6), (inverted, 4), (residual, 3), (ff2_done, 4),
                     (ff2_emptied, 4), (stored, 64)]
        per_graph += [(s, 32) for s in mask_loaded] + [(s, AUG_COUNT) for s in aug_loaded]
        per_graph += [(s, 16 * H) for s in max_row_in] + [(s, 64 * H) for s in o_moved]
        per_graph += [(s, T) for s in (pen_ready, mask_used, s_done, slack_done, leaky_done, y_ready, g_ready,
                                       e_ready, g3_ready)]
        per_graph += [(s, 2 * T) for s in (s_ready, p_ready, t_done, t_act, t_dve, av_done, av_taken, normal)]
        per_graph += [(s, 2 * H) for s in (max_cast, rows_done, rows_taken, v_ready, o_out)]
        per_graph += [(normal_y, 4), (scaled, 4), (shifted, 4), (power_done, len(NORM_ORDER))]
        per_graph += [(s, NORMS) for s in (stats_ready, var_ready, rstd_ready)]

        def norm_count(b, layer, i, k):
            return b * NORMS + T + NORM_ORDER.index((layer, i, k)) + 1

        def att(b, layer, h, per, c):
            pair, k = h
            return (b * (2 * H) + pair * 2) * per + (layer * H + k) * per + c

        FIRST = (0, 0)

        def ahead(head, n=1):
            pair, k = head
            return pair, k + n

        def rows_moved(b, layer, h, i):
            return att(b, layer, h, 32, -32 * i)

        def max_rows_in(b, layer, h, i):
            return att(b, layer, h, 8, -8 * i)

        def number(head):
            pair, k = head
            return pair * 2 + k

        def times(b, per):
            return b[0] * per + b[1] * per if isinstance(b, tuple) else b * per

        def wait_lin(eng, b, name, i):
            eng.wait_ge(lin_done, times(b, N_LIN) + PLACE[(name, i)] + 1)

        def wait_emptied(eng, b, name, i):
            na, nd = emptied_before(name, i)
            if UNITS[PLACE[(name, i)]][2] == "A":
                eng.wait_ge(act_emptied, times(b, N_ACT) + na + 1)
            else:
                eng.wait_ge(dve_emptied, times(b, N_DVE) + nd + 1)

        def wait_all_emptied(eng, b, name, n):
            na, nd = emptied_before(name, n - 1)
            last_a = UNITS[PLACE[(name, n - 1)]][2] == "A"
            eng.wait_ge(act_emptied, times(b, N_ACT) + na + last_a)
            eng.wait_ge(dve_emptied, times(b, N_DVE) + nd + (not last_a))

        setup_dmas, weight_dmas = [], []

        block = ctx.enter_context(nc.Block())

        @block.sync
        def _(sp):
            def load(dst, src, first=False):
                sp.dma_start(dst, src).then_inc(setup_in if first else weights_in, 16)
                (setup_dmas if first else weight_dmas).append(1)

            def tiled(name):
                return a[name].rearrange("(c p) n -> p c n", p=P)

            def load_row(key, name, first=False):
                load(rows[key][:, :], a[name].rearrange("(a n) -> a n", a=1).broadcast_to([P, D]), first)

            def load_x(at):
                sp.dma_start(x_in[:, :, :], a["x"][at].rearrange("(t p) d -> p t d", p=P)).then_inc(x_loaded, 16)

            def load_adjacency(at, t):
                sp.dma_start(mask[:, t, :], a["adj"][at, t * P:(t + 1) * P, :]).then_inc(mask_loaded[t], 16)

            load(fcw, tiled("L0_gnn_fc_w"), True)
            for key, name in (("q_w", "L0_gnn_q_w"), ("k_w", "L0_gnn_k_w"), ("fc_b", "L0_gnn_fc_b"),
                              ("bv2", "L2_gnn_bv"), ("bv3", "L3_gnn_bv")):
                load(cols[key][:, :], a[name + "_columns"], True)
            for i, name in enumerate(("L0_gnn_q_b", "L0_gnn_k_b")):
                load(qk_b[:, i:i + 1], a[name].rearrange("(a n) -> a n", a=1).broadcast_to([P, 1]), True)
            for key, name in (("fc", "L0_fc_wT"), ("o2", "L2_WoT"), ("o3", "L3_gnn_Wo")):
                load(w[key][:, :, 0:D], tiled(name), True)
            for key, name in (("fc_b", "L0_gnn_fc_b"), ("bo2", "L2_gnn_bo"), ("bo3", "L3_gnn_bo")):
                load_row(key, name, True)
            load_x(0)
            for t in range(T):
                load_adjacency(0, t)
            for key, name in (("q1", "L1_gnn_Wq"), ("k1", "L1_gnn_Wk"), ("c1", "L1_gnn_Wc"),
                              ("q2", "L2_WqT"), ("k2", "L2_WkT"), ("v2", "L2_WvT"),
                              ("q3", "L3_gnn_Wq"), ("k3", "L3_gnn_Wk"), ("v3", "L3_gnn_Wv")):
                load(w[key][:, :, :], tiled(name))
            load(wf1[:, :, :], tiled("L3_gnn_Wf1"))
            load(wf2[:, :, :], tiled("L3_gnn_Wf2"))
            for key, name in (("gamma1", "L1_gnn_gamma"), ("beta1", "L1_gnn_beta"), ("gamma2", "L2_gnn_gamma"),
                              ("beta2", "L2_gnn_beta"), ("bf2", "L3_gnn_bf2")):
                load_row(key, name)
            for key, name in (("bq1", "L1_gnn_bq"), ("bk1", "L1_gnn_bk"), ("bq2", "L2_gnn_bq"), ("bk2", "L2_gnn_bk"),
                              ("bq3", "L3_gnn_bq"), ("bk3", "L3_gnn_bk"), ("g1", "L3_gnn_g1"), ("b1", "L3_gnn_b1"),
                              ("g2", "L3_gnn_g2"), ("b2", "L3_gnn_b2")):
                load(cols[key][:, :], a[name + "_columns"])
            load(bf1[:, :], a["L3_gnn_bf1_columns"])
            sp.wait_ge(const_made, CONSTS)

            def graph(b, last):
                for t in range(T):
                    sp.wait_ge(mask_used, b * T + t + 1)
                    sp.dma_start(mask[:, t, :], a["adj_t"][b - 1, t * P:(t + 1) * P, :]).then_inc(mask_loaded[t], 16)

                load_x(b - 1 if last else b)

                sp.wait_ge(y_ready, b * T + T)
                sp.dma_start(k_aug[AUG - 1:AUG, :, :], minus_one[:, :]).then_inc(ones_loaded, 16)

                for layer in range(2):
                    def max_row(h):
                        if h >= 2:
                            sp.wait_ge(max_row_in[h % 2], max_rows_in(b, layer, (0, h), h % 2))
                            sp.sem_inc(passed, 1)
                        sp.wait_ge(rows_taken, att(b, layer, (0, h), 1, 1))
                        sp.dma_start(q_aug[AUG - 1:AUG, h, :], max_rows[h % 2][:, :]).then_inc(max_row_in[h % 2], 16)

                    for g in range(C):
                        wait_emptied(sp, b, "k" + "23"[layer] + "." + str(g), 1)
                        q_high, q_low, k_high, k_low = (parts[g][:, s, :] for s in range(4))
                        for j in range(4):
                            for aug, stack in ((q_aug, (q_high, q_low, q_high)), (k_aug, (k_high, k_high, k_low))):
                                for r, part in enumerate(stack):
                                    sp.dma_start(aug[r * DK:(r + 1) * DK, 4 * g + j, :],
                                                 part[j * DK:(j + 1) * DK, :]).then_inc(aug_loaded[4 * g + j], 16)
                            if (g, j) == (1, 0):
                                max_row(0)

                    max_row(1)
                    for h in range(4, H):
                        sp.wait_ge(aug_loaded[h], b * AUG_COUNT + 16 * AUG_DMAS * (layer + 1))
                    sp.sem_inc(passed, 1)
                    for h in range(H):
                        if h + 2 < H:
                            max_row(h + 2)
                        sp.wait_ge(o_out, att(b, layer, (0, h), 1, 1))
                        r, g = DK * (h % 4), h // 4
                        for c in range(2):
                            cut = slice(c * HALF, (c + 1) * HALF)
                            for dst, at in ((o_t, 2 * DK * c), (sums_t, 2 * DK * c + DK)):
                                sp.dma_start(dst[r:r + DK, g, cut], o_raw[h % 2][at:at + DK, :])\
                                  .then_inc(o_moved[h % 2], 16)
                if not last:
                    for t in range(T):
                        load_adjacency(b, t)
                for g in range(4):
                    sp.wait_ge(ff2_emptied, b * 4 + g + 1)
                    sp.dma_start(out[b - 1].rearrange("(t p) d -> p t d", p=P)[:, 2 * g:2 * g + 2, :],
                                 y[:, 2 * g:2 * g + 2, :]).then_inc(stored, 16)

            with sp.Fori(1, B) as b:
                graph(b, False)
            graph(B, True)
            sp.wait_ge(stored, B * 64 + 64)

        @block.tensor
        def _(pe):
            pe.wait_ge(setup_in, 16 * len(setup_dmas))
            for c in range(C):
                for o in range(C):
                    nc.tensor.matmul(ps[:, 0, c:c + 1], fcw[:, o, c * P:(c + 1) * P], cols["k_w"][:, o:o + 1],
                                     start=(o == 0), stop=(o == C - 1))
                for o in range(C):
                    nc.tensor.matmul(ps[:, 1, c:c + 1], fcw[:, o, c * P:(c + 1) * P], cols["q_w"][:, o:o + 1],
                                     start=(o == 0), stop=(o == C - 1))
            pe.wait_ge(setup_dve, 1 + 3 * C)
            for i, key in enumerate(("q_w", "k_w")):
                for o in range(C):
                    nc.tensor.matmul(ps[:, 2 + i, 0:1], bias_rep[:, 0, o, :], cols[key][:, o:o + 1],
                                     start=(o == 0), stop=(o == C - 1))
            for i, key in enumerate(("o2", "o3")):
                for c in range(C):
                    last = nc.tensor.matmul(ps[:, 4 + i, 0:D], bias_rep[:, 1 + i, c, :], w[key][:, c, :],
                                            start=(c == 0), stop=(c == C - 1))
            last.then_inc(setup_mm, 1)
            pe.wait_ge(setup_dve, 1 + 3 * C + C + 2)
            pe.wait_ge(const_made, CONSTS)

            def turn(name, i, group):
                bank = free_bank(name, i)
                for j in range(4):
                    t = 4 * (i // 2) + j
                    last = nc.tensor.transpose(ps[:, bank, j * P:(j + 1) * P],
                                               group[:, t, (i % 2) * P:(i % 2 + 1) * P], ident[:, :])
                last.then_inc(lin_done, 1)

            def free_bank(name, i):
                bank = bank_of(name, i)
                for before, j, _ in reversed(UNITS[:PLACE[(name, i)]]):
                    if bank_of(before, j) == bank:
                        wait_emptied(pe, graph[0], before, j)
                        return bank
                pe.wait_ge(act_emptied, times(graph[0], N_ACT))
                pe.wait_ge(dve_emptied, times(graph[0], N_DVE))
                return bank

            def nodes_by(name, i, lhs, rhs, tiles):
                bank = 4 + i if name == "ff2" else free_bank(name, i)
                for j in range(2):
                    t = 2 * i + j
                    for c in range(tiles):
                        last = nc.tensor.matmul(ps[:, bank, j * D:(j + 1) * D], lhs(c, t), rhs[:, c, :],
                                                start=(c == 0), stop=(c == tiles - 1))
                last.then_inc(ff2_done if name == "ff2" else lin_done, 1)

            def features_by(name, i, weight, half, m):
                bank = free_bank(name, i)
                for c in range(C):
                    last = nc.tensor.matmul(ps[:, bank, :], weight[:, c, m * P:(m + 1) * P],
                                            y_t[:, c, half * HALF:(half + 1) * HALF],
                                            start=(c == 0), stop=(c == C - 1))
                last.then_inc(lin_done, 1)

            def output_products(b, layer, name):
                def product(i, j, c):
                    return nc.tensor.matmul(ps[:, bank_of(name, i), j * D:(j + 1) * D], y_tile(c, 2 * i + j),
                                            w[name][:, c, :], start=(c == 0), stop=(c == C - 1))

                pe.wait_ge(o_normal, b * 6 + layer * 3 + 1)
                for i in range(4):
                    free_bank(name, i)
                    product(i, 0, 0)
                for i in range(4):
                    if i % 2 == 0:
                        pe.wait_ge(o_normal, b * 6 + layer * 3 + 2 + i // 2)
                    product(i, 0, 1)
                    product(i, 1, 0)
                    product(i, 1, 1).then_inc(lin_done, 1)

            def y_tile(c, t):
                return y_t[:, c, t * P:(t + 1) * P]

            def attend(b, layer, t):
                base = b * 2 * T + layer * T
                if t < T:
                    pe.wait_ge(p_ready, base + t + 1)
                    pe.wait_ge(t_act, base + t)
                    pe.wait_ge(t_dve, base + t)
                    for k in range(T):
                        last = nc.tensor.transpose(flat[:, 4 * HALF + k * P:4 * HALF + (k + 1) * P],
                                                   scores[:, t % 3, k * P:(k + 1) * P], ident[:, :])
                    last.then_inc(t_done, 1)
                if t > 0:
                    pe.wait_ge(t_act, base + t)
                    pe.wait_ge(t_dve, base + t)
                    if layer or t > 2:
                        pe.wait_ge(av_taken, base + t - 2)
                    for k in range(T):
                        last = nc.tensor.matmul(ps[:, 6 + (t - 1) % 2, 0:D], probs_t[:, (t - 1) % 2, k, :],
                                                (values0, values)[layer][:, k, :], start=(k == 0), stop=(k == T - 1))
                    last.then_inc(av_done, 1)

            def head(b, layer, h, i, scores_two_ahead, first=False):
                for t in range(T):
                    rows_now = t == 2 and (scores_two_ahead or i == 0)
                    if rows_now:
                        pe.wait_ge(exp_done, att(b, layer, h, 2 * T, 2 * t))
                        rows_of_maxima(b, layer, ahead(h), 1 - i)
                    if scores_two_ahead:
                        scores_for_maximum(b, layer, ahead(h, 2), t)
                    if t == 0:
                        pe.wait_ge(max_row_in[i], max_rows_in(b, layer, ahead(h, 2), i))
                    for c in range(2):
                        if c == 1 and rows_now:
                            pe.wait_ge(rows_taken, att(b, layer, ahead(h), 1, 1))
                        if c == 1 and first and t == 0:
                            pe.wait_ge(rows_taken, att(b, layer, h, 1, 1))
                        pe.wait_ge(exp_done, att(b, layer, h, 2 * T, 2 * t + c - 1))
                        nc.tensor.matmul(ps[:, 4 + c, :], k_aug[0:AUG, number(h), t * P:(t + 1) * P],
                                         q_aug[0:AUG, number(h), c * HALF:(c + 1) * HALF],
                                         start=True, stop=True).then_inc(st_done, 1)
                    if t >= LAG:
                        with_values(b, layer, h, i, t - LAG)
                    elif not first:
                        with_values(b, layer, ahead(h, -1), 1 - i, T - LAG + t)

            def scores_for_maximum(b, layer, h, t, wait=True):
                if wait:
                    pe.wait_ge(max_done, att(b, layer, h, T, t - 1))
                for c in range(2):
                    last = nc.tensor.matmul(ps[:, 2 * (t % 2) + c, :], q_aug[0:AUG - 1, number(h), t * P:(t + 1) * P],
                                            k_aug[0:AUG - 1, number(h), c * HALF:(c + 1) * HALF],
                                            start=True, stop=True)
                last.then_inc(nat_done, 1)

            def rows_of_maxima(b, layer, h, i):
                pe.wait_ge(max_cast, att(b, layer, h, 1, 1))
                nc.tensor.transpose(ps[0:T, 5, 0:P // 2].bitcast(BF16), row_max_bf[i][:, :],
                                    ident_bf[:, :]).then_inc(rows_done, 1)

            def with_values(b, layer, h, i, t):
                if t in DVE_TILES:
                    pe.wait_ge(masked_dve, att(b, layer, h, len(DVE_TILES), DVE_TILES.index(t) + 1))
                else:
                    pe.wait_ge(masked_pool, att(b, layer, h, len(POOL_TILES), POOL_TILES.index(t) + 1))
                if t == 0:
                    pe.wait_ge(v_ready, att(b, layer, h, 1, 1))
                    pe.wait_ge(o_out, att(b, layer, h, 1, -1))
                for c in range(2):
                    last = nc.tensor.matmul(ps[64 * c:64 * c + 64, 6 + i, :], v_head[i][:, t, :],
                                            probs[:, t % RING, c * HALF:(c + 1) * HALF],
                                            start=(t == 0), stop=(t == T - 1))
                last.then_inc(pv_done, 1)

            def head_loaded(b, layer, h):
                pe.wait_ge(aug_loaded[h], b * AUG_COUNT + 16 * AUG_DMAS * (layer + 1))

            def heads(b, layer, v):
                head_loaded(b, layer, 0)
                for t in range(T):
                    scores_for_maximum(b, layer, FIRST, t, t >= 2)
                    if t % 2:
                        nodes_by(v, t // 2, y_tile, w[v], C)
                head_loaded(b, layer, 1)
                for t in range(T):
                    if t == 2:
                        wait_all_emptied(pe, b, v, 4)
                        rows_of_maxima(b, layer, FIRST, 0)
                    scores_for_maximum(b, layer, ahead(FIRST), t)
                pe.wait_ge(ones_loaded, b * 16 + 16)
                for h in range(2, 4):
                    head_loaded(b, layer, h)
                for h in range(2):
                    head(b, layer, (0, h), h, True, h == 0)
                for h in range(4, H):
                    head_loaded(b, layer, h)
                pe.sem_inc(passed, 1)
                with pe.Fori(1, H // 2 - 1) as pair:
                    for i in range(2):
                        head(b, layer, (pair, i), i, True)
                for h in range(H - 2, H):
                    head(b, layer, (0, h), h % 2, False)
                for t in range(T - LAG, T):
                    with_values(b, layer, (0, H - 1), 1, t)

            graph = [0]

            def next_keys(b):
                graph[0] = b
                pe.wait_ge(x_loaded, b * 16 + 32)
                for i in range(4):
                    turn("x_t", i, x_in)
                wait_all_emptied(pe, b, "x_t", 4)
                for i in range(2):
                    bank = free_bank("key0", i)
                    for c in range(C):
                        last = nc.tensor.matmul(ps[:, bank, :], key_w[:, c, :], x_t[:, c, i * HALF:(i + 1) * HALF],
                                                start=(c == 0), stop=(c == C - 1))
                    last.then_inc(lin_done, 1)

            def next_values(b):
                for t in range(T):
                    bank = free_bank("proj0", t)
                    for c in range(C):
                        last = nc.tensor.matmul(ps[:, bank, 0:D + 1], x_t[:, c, t * P:(t + 1) * P], w["fc"][:, c, :],
                                                start=(c == 0), stop=(c == C - 1))
                    last.then_inc(lin_done, 1)

            def whole(b, final):
                graph[0] = b
                pe.wait_ge(ff2_emptied, b * 4)
                wait_all_emptied(pe, (b, -1), "proj0", T)
                for t in range(T + 1):
                    attend(b, 0, t)
                for i in range(4):
                    pe.wait_ge(av_taken, b * 2 * T + (i // 2 + 1) * (T // 2))
                    turn("y1_t", i, y)
                wait_all_emptied(pe, b, "y1_t", 4)
                for name in ("q1", "k1"):
                    for i in range(4):
                        features_by(name, i, w[name], i % 2, i // 2)
                for i in range(4):
                    nodes_by("v1", i, y_tile, w["c1"], C)
                wait_all_emptied(pe, b, "v1", 4)
                for t in range(T + 2):
                    if t < T:
                        if t >= 2:
                            pe.wait_ge(s_ready, b * 2 * T + T + t - 1)
                        for n in range(2):
                            for c in range(C):
                                last = nc.tensor.matmul(ps[:, 2 * (t % 2) + n, :], q_t[:, c, t * P:(t + 1) * P],
                                                        k_t[:, c, n * HALF:(n + 1) * HALF],
                                                        start=(c == 0), stop=(c == C - 1))
                        last.then_inc(s_done, 1)
                    if t == T + 1:
                        pe.wait_ge(s_ready, b * 2 * T + 2 * T)
                        pe.wait_ge(y_ready, b * T + T // 2)
                        for i in range(2):
                            turn("y2_t", i, y)
                    if t > 0:
                        attend(b, 1, t - 1)
                for layer, (group, ready, base) in enumerate(((y, y_ready, b * T), (x_hat, normal, b * 2 * T))):
                    n = "23"[layer]
                    for half in range(2):
                        if layer or half:
                            pe.wait_ge(ready, base + (half + 1) * (T // 2))
                            for i in (2 * half, 2 * half + 1):
                                turn("y" + n + "_t", i, group)
                        for i in (2 * half, 2 * half + 1):
                            wait_emptied(pe, b, "y" + n + "_t", i)
                        for name in ("q" + n, "k" + n):
                            features_by(name + ".0", half, w[name], half, 0)
                    for name in ("q" + n, "k" + n):
                        for half in range(2):
                            features_by(name + ".1", half, w[name], half, 1)
                    heads(b, layer, "v" + n)
                    if layer == 0:
                        pe.wait_ge(max_done, att(b, 0, (0, H), T, 0))
                        next_keys(b)
                    output_products(b, layer, "o" + n)
                    if layer == 0:
                        next_values(b)
                for half in range(2):
                    pe.wait_ge(normal, b * 2 * T + T + (half + 1) * (T // 2))
                    for i in (2 * half, 2 * half + 1):
                        turn("h_t", i, x_hat)
                    for i in (2 * half, 2 * half + 1):
                        wait_emptied(pe, b, "h_t", i)
                    for f in range(F):
                        features_by("ff1", half * F + f, wf1, half, f)
                for i in range(4):
                    wait_emptied(pe, b, "ff1", (i // 2 + 1) * F - 1)
                    nodes_by("ff2", i, lambda f, t: hidden[f // 4][:, f % 4, t * P:(t + 1) * P], wf2, F)

            next_keys(0)
            wait_all_emptied(pe, 0, "key0", 2)
            pe.sem_inc(lin_done, PLACE[("proj0", 0)] - PLACE[("key0", 1)] - 1)
            next_values(0)
            wait_lin(pe, 0, "proj0", T - 1)
            pe.sem_inc(lin_done, N_LIN - PLACE[("proj0", T - 1)] - 1)
            pe.wait_ge(weights_in, 16 * len(weight_dmas))
            with pe.Fori(1, B) as b:
                whole(b, False)
            whole(B, True)

        @block.scalar
        def _(act):
            def empty_copy(b, name, i, dst):
                wait_lin(act, b, name, i)
                nc.scalar.copy(dst, ps[:, bank_of(name, i), :]).then_inc(act_emptied, 1)

            def empty(b, name, i, dst, func=ACT.Identity, bias=0.0, scale=1.0):
                wait_lin(act, b, name, i)
                nc.scalar.activation(dst, ps[:, bank_of(name, i), :], func, bias=bias,
                                     scale=scale).then_inc(act_emptied, 1)

            def empty_turn(b, name, half):
                dst = y_t[:, 0, half * HALF:(half + 1) * HALF]
                if name == "y2_t":
                    empty_copy(b, name, 2 * half, dst)
                else:
                    k = {"y3_t": "1", "h_t": "2"}[name]
                    empty(b, name, 2 * half, dst, bias=cols["b" + k][:, 0:1], scale=cols["g" + k][:, 0:1])

            def copy_probs(b, layer, t):
                base = b * 2 * T + layer * T
                act.wait_ge(t_done, base + t + 1)
                act.wait_ge(av_done, base + (t - 1 if t >= 2 else 0))
                nc.scalar.copy(probs_t[:, t % 2, 0:4, :].rearrange("p t q -> p (t q)"), ps[:, 4, :]).then_inc(t_act, 1)

            def adjacency_exp(b, t):
                if t >= 2:
                    act.wait_ge(g3_ready, b * T + t - 1)
                nc.scalar.activation(mask_exp[:, t % 2, :], mask[:, t, :], ACT.Exp, bias=minus_ones[:, 0:1],
                                     scale=2.0).then_inc(e_ready, 1)

            def head(b, layer, h, i, first=False, final=False, exps=()):
                for t in range(T):
                    if t == 2 and not final:
                        take_rows(b, layer, ahead(h), 1 - i)
                    for c in range(2):
                        act.wait_ge(st_done, att(b, layer, h, 2 * T, 2 * t + c + 1))
                        if c == 0:
                            act.wait_ge(pv_done, att(b, layer, h, T, t - RING + 1))
                        nc.scalar.activation(probs[:, t % RING, c * HALF:(c + 1) * HALF], ps[:, 4 + c, :], ACT.Exp,
                                             scale=DK ** -0.5).then_inc(exp_done, 1)
                    if t == LAG and not first:
                        take_sums(b, layer, ahead(h, -1), 1 - i)
                    if t in exps:
                        adjacency_exp(b, exps.index(t))

            def take_rows(b, layer, h, i):
                act.wait_ge(rows_done, att(b, layer, h, 1, 1))
                act.wait_ge(max_row_in[i], max_rows_in(b, layer, h, i))
                nc.scalar.copy(max_rows[i][:, :], ps[0:T, 5, 0:P // 2].bitcast(BF16)).then_inc(rows_taken, 1)

            def take_sums(b, layer, h, i):
                act.wait_ge(pv_done, att(b, layer, h, T, T))
                act.wait_ge(o_moved[i], rows_moved(b, layer, h, i))
                nc.scalar.copy(o_raw[i][:, :], ps[:, 6 + i, :]).then_inc(o_out, 1)

            act.wait_ge(const_made, CONSTS)
            def layer0(b, steps):
                for t in steps:
                    if t < T:
                        act.wait_ge(s_ready, times(b, 2 * T) + t + 1)
                        nc.scalar.activation(slack[:, t % 2, :], scores[:, t % 3, :], ACT.Identity,
                                             bias=slack_q[:, t:t + 1], scale=0.01).then_inc(slack_done, 1)
                    if 0 < t <= T:
                        u = t - 1
                        act.wait_ge(leaky_done, times(b, T) + u + 1)
                        nc.scalar.activation(scores[:, u % 3, :], scores[:, u % 3, :], ACT.Exp,
                                             bias=neg_top[:, u:u + 1], accum_out=denom[:, u:u + 1]).then_inc(p_ready, 1)
                    if t > START - 1:
                        copy_probs(b, 0, t - 2)

            def next_keys(b):
                for i in range(4):
                    empty_copy(b, "x_t", i, x_t[:, i % 2, i // 2 * HALF:(i // 2 + 1) * HALF])
                for i in range(2):
                    empty(b, "key0", i, key_row[:, i * HALF:(i + 1) * HALF], bias=qk_const[:, 1:2])

            def next_values(b, tiles):
                for t in tiles:
                    wait_lin(act, b, "proj0", t)
                    bank = bank_of("proj0", t)
                    nc.scalar.copy(values0[:, t, :], ps[:, bank, 0:D])
                    nc.scalar.activation(q_n[:, t:t + 1], ps[:, bank, D:D + 1], ACT.Identity,
                                         bias=qk_const[:, 0:1]).then_inc(act_emptied, 1)

            def whole(b, final):
                copy_probs(b, 0, 0)
                layer0(b, range(START, T + 2))
                for half in range(2):
                    empty_copy(b, "y1_t", 2 * half, y_t[:, 0, half * HALF:(half + 1) * HALF])
                for name, dst, bias in (("q1", q_t, "bq1"), ("k1", k_t, "bk1")):
                    for i in range(0, 4, 2):
                        empty(b, name, i, dst[:, i // 2, 0:HALF], bias=cols[bias][:, i // 2:i // 2 + 1])
                for i in range(0, 4, 2):
                    empty_copy(b, "v1", i, values[:, 2 * i:2 * i + 2, :].rearrange("p t d -> p (t d)"))
                for t in range(T + 1):
                    if t < T:
                        act.wait_ge(s_ready, b * 2 * T + T + t + 1)
                        s = scores[:, t % 3, :]
                        nc.scalar.activation(s, s, ACT.Exp, bias=neg_top[:, t:t + 1], scale=D ** -0.5,
                                             accum_out=denom[:, t:t + 1]).then_inc(p_ready, 1)
                    if t > 0:
                        copy_probs(b, 1, t - 1)
                for layer in range(2):
                    n = "23"[layer]
                    if layer == 0:
                        empty_turn(b, "y2_t", 0)
                    for u, (g, q_or_k, half) in enumerate(PART_UNITS):
                        if u == 2:
                            empty_turn(b, "y" + n + "_t", 1)
                        name = "qk"[q_or_k] + n
                        wait_lin(act, b, f"{name}.{g}", half)
                        nc.scalar.activation(parts[g][:, 2 * q_or_k, half * HALF:(half + 1) * HALF],
                                             ps[:, bank_of(f"{name}.{g}", half), :], ACT.Identity,
                                             bias=cols["b" + name][:, g:g + 1]).then_inc(hi_ready, 1)
                    for i in range(4):
                        empty_copy(b, "v" + n, i, values[:, 2 * i:2 * i + 2, :].rearrange("p t d -> p (t d)"))
                    take_rows(b, layer, FIRST, 0)
                    for h in range(2):
                        head(b, layer, (0, h), h, h == 0)
                    with act.Fori(1, H // 2 - 1) as pair:
                        for i in range(2):
                            head(b, layer, (pair, i), i)
                    for h in range(H - 2, H):
                        head(b, layer, (0, h), h % 2, final=h == H - 1,
                             exps=EARLY_EXPS if layer == 0 and h == H - 1 else ())
                    take_sums(b, layer, (0, H - 1), 1)
                    if layer == 0:
                        for t in range(len(EARLY_EXPS), T):
                            adjacency_exp(b, t)
                            if t == len(EARLY_EXPS) + 1:
                                next_keys(b)
                    for place, (at, i, k) in enumerate(NORM_ORDER):
                        if at == layer:
                            act.wait_ge(rstd_ready, norm_count(b, layer, i, k))
                            for t in (2 * i, 2 * i + 1):
                                last = nc.scalar.activation((y, x_hat)[k][:, t, :], y[:, t, :], ACT.Identity,
                                                            bias=shift[:, t:t + 1], scale=rstd[:, t:t + 1])
                                if k == 1:
                                    last.then_inc(normal, 1)
                            if k == 0:
                                last.then_inc(normal_y, 1)
                            if place < T // 2:
                                next_values(b, range(2 * place, 2 * place + 2))
                            if (i, k) == (2, 1):
                                empty_turn(b, ("y3_t", "h_t")[layer], 0)
                for i in range(2 * F):
                    half, f = i // F, i % F
                    if i == F:
                        empty_turn(b, "h_t", 1)
                    empty(b, "ff1", i, hidden[f // 4][:, f % 4, half * HALF:(half + 1) * HALF], ACT.Gelu,
                          bias=bf1[:, f:f + 1])
                if not final:
                    layer0((b, 1), range(START))

            next_keys(0)
            next_values(0, range(T))
            wait_emptied(act, 0, "proj0", T - 1)
            act.sem_inc(act_emptied, N_ACT - emptied_before("proj0", T - 1)[0] - 1)
            layer0(1, range(START))
            act.wait_ge(weights_in, 16 * len(weight_dmas))
            with act.Fori(1, B) as b:
                whole(b, False)
            whole(B, True)

        @block.vector
        def _(dve):
            graph = [0]
            body = [0]
            steps = [DVE_STEPS - DVE_STEPS_START]
            norms = [0]

            def then(ins):
                steps[0] += 1
                ins.then_inc(dve_step, 1)
                dve.wait_ge(dve_step, body[0] * DVE_STEPS + steps[0])

            def row(name, n):
                return rows[name][:, :].rearrange("p (a d) -> p a d", a=1).broadcast_to([P, n, D])

            def unit(name, i):
                wait_lin(dve, graph[0], name, i)
                return ps[:, bank_of(name, i), :]

            def empty_turn(name, half):
                dst = y_t[:, 1, half * HALF:(half + 1) * HALF]
                if name == "y2_t":
                    nc.vector.tensor_copy(dst, unit(name, 2 * half + 1)).then_inc(dve_emptied, 1)
                else:
                    k = {"y3_t": "1", "h_t": "2"}[name]
                    nc.vector.tensor_scalar(dst, unit(name, 2 * half + 1), cols["g" + k][:, 1:2],
                                            cols["b" + k][:, 1:2], ALU.mult, ALU.add).then_inc(dve_emptied, 1)

            def copy_probs(b, layer, t):
                base = b * 2 * T + layer * T
                dve.wait_ge(t_done, base + t + 1)
                dve.wait_ge(av_done, base + (t - 1 if t >= 2 else 0))
                nc.vector.tensor_copy(probs_t[:, t % 2, 4:8, :].rearrange("p t q -> p (t q)"), ps[:, 5, :])\
                  .then_inc(t_dve, 1)

            def variances(tiles, negate=False):
                for t in tiles:
                    last = nc.vector.bn_stats(stats[:, t, :], y[:, t, :])
                last.then_inc(stats_ready, 1)
                norms[0] += 1
                dve.wait_ge(stats_ready, graph[0] * NORMS + norms[0])
                dve.sem_inc(passed, 1)
                for t in tiles:
                    last = nc.vector.bn_aggr(mean_var[:, t, :], stats[:, t, :])
                then(last)
                if negate:
                    nc.vector.tensor_scalar(neg_mean[:, tiles[0]:tiles[-1] + 1], mean_var[:, tiles[0]:tiles[-1] + 1, 0],
                                            -1.0, None, ALU.mult)
                nc.vector.tensor_scalar(var_eps[:, tiles[0]:tiles[-1] + 1], mean_var[:, tiles[0]:tiles[-1] + 1, 1],
                                        EPS, None, ALU.add).then_inc(var_ready, 1)

            def normalize(tiles, dst, behind):
                dve.wait_ge(rstd_ready, graph[0] * NORMS + norms[0] - behind + 1)
                for t in tiles:
                    last = nc.vector.tensor_scalar(dst[:, t, :], y[:, t, :], mean_var[:, t, 0:1], rstd[:, t:t + 1],
                                                   ALU.subtract, ALU.mult)
                then(last)

            def heads_moved(b, layer, g):
                for i in range(2):
                    dve.wait_ge(o_moved[i], rows_moved(b, layer, (0, 4 * g + 4 + i), i))

            def invert_sums(g, cut):
                return nc.vector.reciprocal(sums_t[:, g, cut], sums_t[:, g, cut])

            def make_mask3(b, t):
                dve.wait_ge(e_ready, b * T + t + 1)
                if t in DVE_TILES:
                    dve.wait_ge(masked_dve, att(b, 0, (0, H - 1), len(DVE_TILES), DVE_TILES.index(t) + 1))
                else:
                    dve.wait_ge(masked_pool, att(b, 0, (0, H - 1), len(POOL_TILES), POOL_TILES.index(t) + 1))
                nc.vector.scalar_tensor_tensor(mask[:, t, :], mask[:, t, :], 1.0 / 3.0, mask_exp[:, t % 2, :],
                                               ALU.add, ALU.mult).then_inc(g3_ready, 1)

            def head(b, layer, h, i, maxima_two_ahead, spare=None):
                for t in range(T):
                    if maxima_two_ahead:
                        maximum(b, layer, ahead(h, 2), i, t)
                    if t in DVE_TILES:
                        dve.wait_ge(exp_done, att(b, layer, h, 2 * T, 2 * t + 2))
                        p = probs[:, t % RING, :]
                        nc.vector.tensor_tensor(p, p, mask[:, t, :], ALU.mult).then_inc(masked_dve, 1)
                    if spare is not None:
                        spare(t)
                if maxima_two_ahead:
                    cast_maxima(b, layer, ahead(h, 2), i)

            def maximum(b, layer, h, i, t):
                dve.wait_ge(nat_done, att(b, layer, h, T, t + 1))
                nc.vector.tensor_reduce(row_max[i][:, t:t + 1], flat[:, (t % 2) * N:(t % 2 + 1) * N], AX.X, ALU.max)\
                  .then_inc(max_done, 1)

            def cast_maxima(b, layer, h, i):
                dve.wait_ge(max_done, att(b, layer, h, T, T))
                nc.vector.tensor_copy(row_max_bf[i][:, :], row_max[i][:, :]).then_inc(max_cast, 1)

            nc.vector.memset(ones[:, :], 1.0).then_inc(setup_dve, 1)
            nc.vector.memset(minus_one[:, :], -1.0).then_inc(const_made, 1)
            for i in range(2):
                last = nc.vector.memset(v_head[i][:, :, :], 1.0)
            last.then_inc(const_made, 1)
            nc.vector.memset(minus_ones[:, :], -1.0).then_inc(const_made, 1)
            nc.vector.memset(minus_half[:, :], -0.5).then_inc(const_made, 1)
            dve.wait_ge(setup_dve, 1)
            dve.wait_ge(setup_in, 16 * len(setup_dmas))
            for i, key in enumerate(("fc_b", "bv2", "bv3")):
                for c in range(C):
                    nc.vector.tensor_scalar(bias_rep[:, i, c, :], ones[:, :], cols[key][:, c:c + 1], None, ALU.mult)\
                      .then_inc(setup_dve, 1)
            dve.wait_ge(setup_mm, 1)
            for c in range(C):
                nc.vector.tensor_scalar(key_w[:, c, :], ones[:, :], ps[:, 0, c:c + 1], None, ALU.mult)\
                  .then_inc(setup_dve, 1)
            nc.vector.tensor_copy(query_w, ps[:, 1, 0:C]).then_inc(setup_dve, 1)
            for i in range(2):
                last = nc.vector.tensor_tensor(qk_const[:, i:i + 1], ps[:, 2 + i, 0:1], qk_b[:, i:i + 1], ALU.add)
            last.then_inc(setup_dve, 1)
            for i, key in enumerate(("bo2", "bo3")):
                nc.vector.tensor_tensor(rows[key][:, :], rows[key][:, :], ps[:, 4 + i, 0:D], ALU.add)\
                  .then_inc(const_made, 1)
            dve.wait_ge(const_made, CONSTS)

            def layer0(b, steps):
                for t in steps:
                    if t < T:
                        s = scores[:, t % 3, :]
                        dve.wait_ge(pen_ready, times(b, T) + t + 1)
                        dve.sem_inc(passed, 1)
                        then(nc.vector.tensor_tensor_reduce(s, s, key_row[:, :], 1.0, LOWEST, ALU.add, ALU.max,
                                                            top[:, t:t + 1]))
                        then(nc.vector.tensor_scalar(top2[:, t:t + 1], top[:, t:t + 1], q_n[:, t:t + 1], None, ALU.add))
                        then(nc.vector.scalar_tensor_tensor(top[:, t:t + 1], top2[:, t:t + 1], 0.01, top2[:, t:t + 1],
                                                            ALU.mult, ALU.max))
                        nc.vector.tensor_scalar(neg_top[:, t:t + 1], top[:, t:t + 1], -1.0, None, ALU.mult)\
                          .then_inc(s_ready, 1)
                    if 0 < t <= T:
                        u = t - 1
                        s = scores[:, u % 3, :]
                        dve.wait_ge(slack_done, times(b, T) + u + 1)
                        nc.vector.scalar_tensor_tensor(s, s, q_n[:, u:u + 1], slack[:, u % 2, :], ALU.add, ALU.max)\
                          .then_inc(leaky_done, 1)
                    if START - 1 < t <= T + 1:
                        copy_probs(b, 0, t - 2)
                    if t > 2:
                        u = t - 3
                        then(nc.vector.reciprocal(rden[:, u:u + 1], denom[:, u:u + 1]))
                        dve.wait_ge(av_done, b * 2 * T + u + 1)
                        if u == 0:
                            dve.wait_ge(stored, b * 64)
                            dve.wait_ge(x_biased, b + 1)
                        nc.vector.scalar_tensor_tensor(y[:, u, :], ps[:, 6 + u % 2, 0:D], rden[:, u:u + 1],
                                                       x_in[:, u, :], ALU.mult, ALU.add).then_inc(av_taken, 1)

            def start(b, before):
                wait_all_emptied(dve, before, "proj0", T)
                then(nc.vector.tensor_scalar(slack_q[:, :], q_n[:, :], 0.01, None, ALU.mult))
                layer0(b, range(START))

            def whole(b, final):
                graph[0] = body[0] = b
                steps[0] = norms[0] = 0
                copy_probs(b, 0, 0)
                layer0(b, range(START, T + 3))
                for half in range(2):
                    nc.vector.tensor_copy(y_t[:, 1, half * HALF:(half + 1) * HALF], unit("y1_t", 2 * half + 1))\
                      .then_inc(dve_emptied, 1)
                for name, dst, bias in (("q1", q_t, "bq1"), ("k1", k_t, "bk1")):
                    for i in (1, 3):
                        nc.vector.tensor_scalar(dst[:, i // 2, HALF:N], unit(name, i), cols[bias][:, i // 2:i // 2 + 1],
                                                None, ALU.add).then_inc(dve_emptied, 1)
                for i in (1, 3):
                    nc.vector.tensor_copy(values[:, 2 * i:2 * i + 2, :].rearrange("p t d -> p (t d)"), unit("v1", i))\
                      .then_inc(dve_emptied, 1)
                for t in range(T + 3):
                    if t < T:
                        s = scores[:, t % 3, :]
                        if t >= 3:
                            dve.wait_ge(t_done, b * 2 * T + T + t - 2)
                        nc.vector.tensor_scalar(s, mask[:, t, :], 0.0, -1e18 * D ** 0.5, ALU.is_equal, ALU.mult)\
                          .then_inc(mask_used, 1)
                        dve.wait_ge(mask_used, b * T + t + 1)
                        dve.wait_ge(s_done, b * T + t + 1)
                        dve.sem_inc(passed, 1)
                        then(nc.vector.tensor_tensor_reduce(s, flat[:, (t % 2) * N:(t % 2 + 1) * N], s, 1.0, LOWEST,
                                                            ALU.add, ALU.max, top[:, t:t + 1]))
                        nc.vector.tensor_scalar(some[:, t:t + 1], top[:, t:t + 1], -0.5e18 * D ** 0.5, None, ALU.is_gt)
                        nc.vector.tensor_scalar(neg_top[:, t:t + 1], top[:, t:t + 1], -(D ** -0.5), None, ALU.mult)\
                          .then_inc(s_ready, 1)
                    if 0 < t <= T:
                        copy_probs(b, 1, t - 1)
                    if 1 < t <= T + 1:
                        u = t - 2
                        if u == T - 1:
                            empty_turn("y2_t", 0)
                        dve.wait_ge(av_done, b * 2 * T + T + u + 1)
                        then(nc.vector.reciprocal(rden[:, u:u + 1], denom[:, u:u + 1]))
                        then(nc.vector.tensor_tensor(rden2[:, u:u + 1], rden[:, u:u + 1], some[:, u:u + 1], ALU.mult))
                        nc.vector.scalar_tensor_tensor(y[:, u, :], ps[:, 6 + u % 2, 0:D], rden2[:, u:u + 1],
                                                       y[:, u, :], ALU.mult, ALU.add).then_inc(av_taken, 1)
                        dve.wait_ge(av_taken, b * 2 * T + T + u + 1)
                        variances(range(u, u + 1))
                    if t > 2:
                        u = t - 3
                        normalize(range(u, u + 1), y, 2 if u < T - 1 else 1)
                        then(nc.vector.tensor_tensor(y[:, u, :], y[:, u, :], rows["gamma1"][:, :], ALU.mult))
                        nc.vector.tensor_tensor(y[:, u, :], y[:, u, :], rows["beta1"][:, :], ALU.add)\
                          .then_inc(y_ready, 1)
                for layer in range(2):
                    n = "23"[layer]
                    for u, (g, q_or_k, half) in enumerate(PART_UNITS):
                        if u == 2:
                            empty_turn("y" + n + "_t", 1)
                        name = "qk"[q_or_k] + n
                        cut = slice(half * HALF, (half + 1) * HALF)
                        dve.wait_ge(hi_ready, b * 8 * C + layer * 4 * C + u + 1)
                        nc.vector.scalar_tensor_tensor(parts[g][:, 2 * q_or_k + 1, cut], unit(f"{name}.{g}", half),
                                                       cols["b" + name][:, g:g + 1], parts[g][:, 2 * q_or_k, cut],
                                                       ALU.add, ALU.subtract).then_inc(dve_emptied, 1)
                        t = u
                        if layer == 0:
                            dve.wait_ge(mask_loaded[t], b * 32 + 32)
                            nc.vector.tensor_scalar(mask[:, t, :], mask[:, t, :], 1e-8, None, ALU.max)\
                              .then_inc(g_ready, 1)
                        elif t < 2:
                            make_mask3(b, T - 2 + t)
                    for t in range(T):
                        maximum(b, layer, FIRST, 0, t)
                    cast_maxima(b, layer, FIRST, 0)
                    dve.wait_ge((g_ready, g3_ready)[layer], b * T + T)
                    for t in range(T):
                        maximum(b, layer, ahead(FIRST), 1, t)
                    cast_maxima(b, layer, ahead(FIRST), 1)
                    for h in range(2):
                        head(b, layer, (0, h), h, True)
                    with dve.Fori(1, H // 2 - 1) as pair:
                        for i in range(2):
                            head(b, layer, (pair, i), i, True)

                    def invert_quarter(t):
                        if t % 2:
                            quarter = invert_sums(0, slice(t // 2 * D, (t // 2 + 1) * D))
                            if t == T - 1:
                                then(quarter)

                    def make_early_mask(t):
                        if t in EARLY_MASKS:
                            make_mask3(b, EARLY_MASKS.index(t))

                    heads_moved(b, layer, 0)
                    head(b, layer, (0, H - 2), 0, False, invert_quarter)
                    nc.vector.tensor_tensor(o_t[:, 0, :], o_t[:, 0, :], sums_t[:, 0, :], ALU.mult)\
                      .then_inc(o_normal, 1)
                    head(b, layer, (0, H - 1), 1, False, make_early_mask if layer == 0 else None)
                    if layer == 0:
                        for t in (4, 5):
                            make_mask3(b, t)
                    heads_moved(b, layer, 1)
                    for half in range(2):
                        invert_sums(1, slice(half * HALF, (half + 1) * HALF)).then_inc(inverted, 1)
                    dve.wait_ge(residual, b * 3 + layer + 1)
                    for at, i, k in NORM_ORDER:
                        if at != layer:
                            continue
                        part = y[:, 2 * i:2 * i + 2, :]
                        if (at, i, k) == (0, 3, 1):
                            empty_turn("y3_t", 0)
                        if (layer, k) != (0, 1):
                            nc.vector.tensor_tensor(part, unit("o" + n, i).rearrange("p (t d) -> p t d", t=2),
                                                    part, ALU.add).then_inc(dve_emptied, 1)
                            wait_emptied(dve, b, "o" + n, i)
                        else:
                            dve.wait_ge(shifted, b * 4 + i + 1)
                        variances(range(2 * i, 2 * i + 2), True)
                        if layer == 0 and (i, k) in SCALED_AFTER:
                            u = SCALED_AFTER[(i, k)]
                            part = y[:, 2 * u:2 * u + 2, :]
                            dve.wait_ge(normal_y, b * 4 + u + 1)
                            nc.vector.tensor_tensor(part, part, row("gamma2", 2), ALU.mult).then_inc(scaled, 1)
                for half in range(2):
                    empty_turn("h_t", half)
                if not final:
                    start((b, 1), b)
                dve.wait_ge(residual, b * 3 + 3)
                for i in range(4):
                    dve.wait_ge(ff2_done, b * 4 + i + 1)
                    nc.vector.tensor_tensor(y[:, 2 * i:2 * i + 2, :],
                                            ps[:, 4 + i, :].rearrange("p (t d) -> p t d", t=2),
                                            y[:, 2 * i:2 * i + 2, :], ALU.add).then_inc(ff2_emptied, 1)
                assert final or steps[0] == DVE_STEPS, steps[0]

            start(1, 0)
            assert steps[0] == DVE_STEPS, steps[0]
            dve.wait_ge(weights_in, 16 * len(weight_dmas))
            with dve.Fori(1, B) as b:
                whole(b, False)
            whole(B, True)

        @block.gpsimd
        def _(pool):
            for s, per in per_graph:
                pool.sem_inc(s, per)
            nc.gpsimd.memset(ident[:, :], 0.0).then_inc(ident_made, 1)
            nc.gpsimd.memset(ident_bf[:, :], 0.0).then_inc(ident_made, 1)
            pool.wait_ge(ident_made, 2)
            for m in (ident, ident_bf):
                nc.gpsimd.affine_select(out=m[:, :], in_=m[:, :], compare_op=ALU.not_equal, fill=1.0, base=0,
                                        pattern=[[-1, P]], channel_multiplier=1).then_inc(const_made, 1)

            def copy_values(b, layer, h, i):
                pool.wait_ge(pv_done, att(b, layer, h, T, -T))
                pool.sem_inc(passed, 1)
                nc.gpsimd.tensor_copy(v_head[i][:, :, 0:DK], values[:, :, bass.ds(number(h) * DK, DK)])\
                  .then_inc(v_ready, 1)

            def head(b, layer, h, i, last=False):
                for t in POOL_TILES:
                    pool.wait_ge(exp_done, att(b, layer, h, 2 * T, 2 * t + 2))
                    p = probs[:, t % RING, :]
                    nc.gpsimd.tensor_tensor(p, p, mask[:, t, :], ALU.mult).then_inc(masked_pool, 1)
                    if t == POOL_TILES[1] and not last:
                        copy_values(b, layer, ahead(h), 1 - i)

            pool.wait_ge(const_made, CONSTS)
            norms = [0]

            def inverse_deviation(b, tiles):
                norms[0] += 1
                pool.wait_ge(var_ready, b * NORMS + norms[0])
                cut = slice(tiles[0], tiles[-1] + 1)
                power = nc.gpsimd.tensor_tensor(rstd[:, cut], var_eps[:, cut], minus_half[:, cut], ALU.pow)
                if norms[0] <= T:
                    power.then_inc(rstd_ready, 1)
                else:
                    power.then_inc(power_done, 1)
                    pool.wait_ge(power_done, b * len(NORM_ORDER) + norms[0] - T)
                    nc.gpsimd.tensor_tensor(shift[:, cut], neg_mean[:, cut], rstd[:, cut], ALU.mult)\
                      .then_inc(rstd_ready, 1)

            def penalties(b, tiles):
                for t in tiles:
                    pool.wait_ge(mask_loaded[t], times(b, 32) + 16)
                    if t >= 3:
                        pool.wait_ge(t_done, times(b, 2 * T) + t - 2)
                    elif t == 0:
                        pool.wait_ge(pv_done, times(b, 2 * H * T))
                    pool.sem_inc(passed, 1)
                    nc.gpsimd.tensor_scalar(scores[:, t % 3, :], mask[:, t, :], -1.0, 1e9, ALU.add, ALU.mult)\
                      .then_inc(pen_ready, 1)

            def add_bias(b, before):
                wait_lin(pool, before, "x_t", 3)
                nc.gpsimd.tensor_tensor(x_in[:, :, :], x_in[:, :, :],
                                        rows["fc_b"][:, :].rearrange("p (a d) -> p a d", a=1)
                                        .broadcast_to([P, T, D]), ALU.add).then_inc(x_biased, 1)

            def whole(b, final):
                norms[0] = 0
                penalties(b, range(3, T))
                for t in range(T):
                    inverse_deviation(b, range(t, t + 1))
                for layer in range(2):
                    wait_all_emptied(pool, b, ("v2", "v3")[layer], 4)
                    copy_values(b, layer, FIRST, 0)
                    nc.gpsimd.tensor_tensor(y[:, :, :], y[:, :, :],
                                            rows[("bo2", "bo3")[layer]][:, :].rearrange("p (a d) -> p a d", a=1)
                                            .broadcast_to([P, T, D]), ALU.add).then_inc(residual, 1)
                    if layer == 0:
                        pool.wait_ge(g_ready, b * T + T)
                    for h in range(2):
                        head(b, layer, (0, h), h)
                    with pool.Fori(1, H // 2 - 1) as pair:
                        for i in range(2):
                            head(b, layer, (pair, i), i)
                    for h in range(H - 2, H):
                        head(b, layer, (0, h), h % 2, h == H - 1)
                    for half in range(2):
                        pool.wait_ge(inverted, b * 4 + layer * 2 + half + 1)
                        cut = slice(half * HALF, (half + 1) * HALF)
                        nc.gpsimd.tensor_tensor(o_t[:, 1, cut], o_t[:, 1, cut], sums_t[:, 1, cut], ALU.mult)\
                          .then_inc(o_normal, 1)
                    for at, i, k in NORM_ORDER:
                        if at == layer:
                            inverse_deviation(b, range(2 * i, 2 * i + 2))
                            if layer == 0 and (i, k) in SCALED_AFTER:
                                u = SCALED_AFTER[(i, k)]
                                part = y[:, 2 * u:2 * u + 2, :]
                                pool.wait_ge(scaled, b * 4 + u + 1)
                                nc.gpsimd.tensor_tensor(part, part,
                                                        rows["beta2"][:, :].rearrange("p (a d) -> p a d", a=1)
                                                        .broadcast_to([P, 2, D]), ALU.add).then_inc(shifted, 1)
                pool.wait_ge(normal, b * 2 * T + 2 * T)
                nc.gpsimd.tensor_tensor(y[:, :, :], y[:, :, :],
                                        rows["bf2"][:, :].rearrange("p (a d) -> p a d", a=1)
                                        .broadcast_to([P, T, D]), ALU.add).then_inc(residual, 1)
                if not final:
                    penalties((b, 1), range(3))
                    add_bias((b, 1), b)

            penalties(1, range(3))
            add_bias(1, 0)
            pool.wait_ge(weights_in, 16 * len(weight_dmas))
            with pool.Fori(1, B) as b:
                whole(b, False)
            whole(B, True)


LAYOUTS = {"L0_fc_wT": "L0_gnn_fc_w", "L2_WqT": "L2_gnn_Wq", "L2_WkT": "L2_gnn_Wk", "L2_WvT": "L2_gnn_Wv",
           "L2_WoT": "L2_gnn_Wo"}

COLUMNS = ("L0_gnn_q_w", "L0_gnn_k_w", "L0_gnn_fc_b", "L1_gnn_bq", "L1_gnn_bk", "L2_gnn_bq", "L2_gnn_bk", "L2_gnn_bv",
           "L3_gnn_bq", "L3_gnn_bk", "L3_gnn_bv", "L3_gnn_g1", "L3_gnn_b1", "L3_gnn_g2", "L3_gnn_b2", "L3_gnn_bf1")
UNUSED = ("L2_gnn_Wq", "L2_gnn_Wk", "L2_gnn_Wv", "L2_gnn_Wo", *(n for n in COLUMNS if n != "L0_gnn_fc_b"))


def kernel(**inputs):
    import numpy as np
    import concourse.bacc as bacc
    from concourse.bass_utils import run_bass_kernel_spmd

    arrays = {name: np.ascontiguousarray(x) for name, x in inputs.items()}
    for name, source in LAYOUTS.items():
        arrays[name] = np.ascontiguousarray(np.asarray(inputs[source]).T)
    arrays["adj_t"] = np.ascontiguousarray(np.asarray(inputs["adj"]).transpose(0, 2, 1))
    for name in COLUMNS:
        arrays[name + "_columns"] = np.ascontiguousarray(np.asarray(inputs[name]).reshape(-1, P).T)
    for unused in UNUSED:
        del arrays[unused]
    nc = bacc.Bacc("TRN2", target_bir_lowering=False, num_devices=1)
    aps = {name: nc.dram_tensor(f"in_{name}", x.shape, mybir.dt.from_np(x.dtype), kind="ExternalInput").ap()
           for name, x in arrays.items()}
    shape = arrays["x"].shape
    result = nc.dram_tensor("result", shape, F32, kind="ExternalOutput").ap()
    build(nc, aps, result)
    r = run_bass_kernel_spmd(nc, [{f"in_{name}": x for name, x in arrays.items()}], core_ids=[0])
    return r.results[0]["result"]
```
